# Optimizing a Trainium2 kernel written in Bass

```python
import numpy as np
import jax
import jax.numpy as jnp

def _softmax(x, axis=-1):
    return jax.nn.softmax(x, axis=axis)

def _gelu(x):
    return jax.nn.gelu(x, approximate=True)

def _silu(x):
    return jax.nn.silu(x)

def _sigmoid(x):
    return jax.nn.sigmoid(x)

def _layernorm(x, axis=-1, eps=1e-05):
    m = jnp.mean(x, axis=axis, keepdims=True)
    v = jnp.var(x, axis=axis, keepdims=True)
    return (x - m) / jnp.sqrt(v + eps)

def _scatter_add(tgt, idx, src, axis=0):
    return tgt.at[idx].add(src)

def _segment_sum(src, seg, n):
    return jax.ops.segment_sum(src, seg, n)
kernel_name = 'mk_xattn_ffn_d2_seqx_r8_d77269'

def setup_inputs(seed: int=0):
    np.random.seed(seed)
    _w = jnp.asarray

    def _rec_inputs():
        import jax
        import jax.numpy as jnp
        _rk = jax.random.key(seed)
        x = -0.000125 + 0.9999 * jax.random.normal(jax.random.fold_in(_rk, 1), (2, 256, 512), jnp.float32)
        _lenS = 256 - jax.random.randint(jax.random.fold_in(_rk, 7), (2,), 0, max(1, 256 // 4) + 1, jnp.int32)
        _lenS2 = 512 - jax.random.randint(jax.random.fold_in(_rk, 8), (2,), 0, max(1, 512 // 4) + 1, jnp.int32)
        _ctx_4096P = jax.random.normal(jax.random.fold_in(_rk, 11), (2, 16, 512), jnp.float32)
        _ctx_4096c = jax.random.dirichlet(jax.random.fold_in(_rk, 511), 0.3 * jnp.ones((16,), jnp.float32), (2, 512))
        _ctx_4096t = jnp.einsum('bsk,bkd->bsd', _ctx_4096c, _ctx_4096P)
        _ctx_4096t = _ctx_4096t * jax.lax.rsqrt(jnp.mean(jnp.square(_ctx_4096t)) + 1e-12) * 0.953939
        ctx_4096 = -5.72187e-05 + 0.999849 * (_ctx_4096t + 0.3 * jax.random.normal(jax.random.fold_in(_rk, 611), (2, 512, 512), jnp.float32))
        _validS = jnp.arange(256)[None, :] < _lenS[:, None]
        _validS2 = jnp.arange(512)[None, :] < _lenS2[:, None]
        _causal = jnp.tril(jnp.ones((256, 256), dtype=bool))
        mask_1x1xSxS2_ff0 = jnp.where(jnp.ones((1, 1, 256, 512), dtype=bool), 0.0, -1000000000.0).astype(jnp.float32)
        return (x, ctx_4096, mask_1x1xSxS2_ff0)
    x, ctx_4096, mask_1x1xSxS2_ff0 = _rec_inputs()

    def _L0_xattn_setup():
        import jax, jax.numpy as jnp
        import numpy as np
        QMIN = 0.0
        QMAX = 255.0

        def fake_quant(x, scale, zp):
            s = scale.reshape(())
            z = zp.reshape(())
            q = jnp.clip(jnp.round(x / s + z), QMIN, QMAX)
            return (q - z) * s
        key = jax.random.key(seed)
        k1, k2 = jax.random.split(key)
        B, M, K, N = (4, 256, 512, 512)
        x1 = jax.random.normal(k1, (B, M, K), dtype=jnp.float32)
        x2 = jax.random.normal(k2, (B, K, N), dtype=jnp.float32)
        x1_scale = jnp.full((1,), 8.0 / 255.0, dtype=jnp.float32)
        x1_zp = jnp.full((1,), 128.0, dtype=jnp.float32)
        x2_scale = jnp.full((1,), 8.0 / 255.0, dtype=jnp.float32)
        x2_zp = jnp.full((1,), 128.0, dtype=jnp.float32)
        return {'x1': x1, 'x2': x2, 'x1_scale': x1_scale, 'x1_zp': x1_zp, 'x2_scale': x2_scale, 'x2_zp': x2_zp}
    _L0_xattn_all = _L0_xattn_setup()
    _L0_xattn_in = {k: v for k, v in _L0_xattn_all.items() if k in ('x1_scale', 'x1_zp', 'x2_scale', 'x2_zp')}
    del _L0_xattn_all

    def _L0_ffn_setup():
        import jax, jax.numpy as jnp
        import numpy as np
        GROUP = 64

        def dequant_q40(w, s, out_features, in_features):
            msb = w >> 4
            lsb = (w & 15 ^ 8) - 8
            g = jnp.concatenate([msb, lsb], axis=1).reshape(-1, GROUP)
            deq = g.astype(s.dtype) * s[:, None]
            return deq.reshape(out_features, in_features)
        key = jax.random.key(seed)
        ks = jax.random.split(key, 7)
        dim, hidden = (512, 1376)
        B, S = (2, 256)

        def packed(k, din, dout):
            return jax.random.randint(k, (din * dout // GROUP // 2, GROUP), -128, 128, dtype=jnp.int32)

        def scales(k, din, dout):
            return (jax.random.uniform(k, (din * dout // GROUP,), dtype=jnp.float32) + 0.5) * 0.01
        x = jax.random.normal(ks[0], (B, S, dim), dtype=jnp.float32)
        w1 = packed(ks[1], dim, hidden)
        s1 = scales(ks[2], dim, hidden)
        w2 = packed(ks[3], hidden, dim)
        s2 = scales(ks[4], hidden, dim)
        w3 = packed(ks[5], dim, hidden)
        s3 = scales(ks[6], dim, hidden)
        return {'x': x, 'w1': w1, 's1': s1, 'w2': w2, 's2': s2, 'w3': w3, 's3': s3}
    _L0_ffn_all = _L0_ffn_setup()
    _L0_ffn_in = {k: v for k, v in _L0_ffn_all.items() if k in ('w1', 's1', 'w2', 's2', 'w3', 's3')}
    del _L0_ffn_all

    def _L1_xattn_setup():
        import jax, jax.numpy as jnp
        import numpy as np
        NUM_HEADS = 32
        NUM_KV_HEADS = 8
        HEAD_DIM = 128
        HIDDEN = 512
        EPS = 1e-05

        def rmsnorm(x, w, eps=EPS):
            xf = x.astype(jnp.float32)
            var = jnp.mean(xf * xf, axis=-1, keepdims=True)
            return w * (xf * jax.lax.rsqrt(var + eps)).astype(x.dtype)
        key = jax.random.key(seed)
        ks = jax.random.split(key, 10)
        B, Q, KV = (1, 128, 6404)
        s = 1.0 / np.sqrt(HIDDEN)
        return {'hidden_states': jax.random.normal(ks[0], (B, Q, HIDDEN), jnp.float32), 'cross_attention_states': jax.random.normal(ks[1], (B, KV, HIDDEN), jnp.float32), 'attention_mask': jnp.zeros((B, 1, Q, KV), jnp.float32), 'q_proj_w': jax.random.normal(ks[2], (NUM_HEADS * HEAD_DIM, HIDDEN), jnp.float32) * s, 'k_proj_w': jax.random.normal(ks[3], (NUM_KV_HEADS * HEAD_DIM, HIDDEN), jnp.float32) * s, 'v_proj_w': jax.random.normal(ks[4], (NUM_KV_HEADS * HEAD_DIM, HIDDEN), jnp.float32) * s, 'o_proj_w': jax.random.normal(ks[5], (HIDDEN, NUM_HEADS * HEAD_DIM), jnp.float32) * s, 'q_norm_w': jnp.ones((HEAD_DIM,), jnp.float32), 'k_norm_w': jnp.ones((HEAD_DIM,), jnp.float32)}
    _L1_xattn_all = _L1_xattn_setup()
    _L1_xattn_in = {k: v for k, v in _L1_xattn_all.items() if k in ('q_proj_w', 'k_proj_w', 'v_proj_w', 'o_proj_w', 'q_norm_w', 'k_norm_w')}
    del _L1_xattn_all

    def _L1_ffn_setup():
        import jax, jax.numpy as jnp
        import numpy as np
        NUM_EXPERTS = 8
        D_IN = 512
        D_OUT = 512
        key = jax.random.key(seed)
        k_x, k_gw, k_gb, k_ew, k_eb = jax.random.split(key, 5)
        x = jax.random.normal(k_x, (4, 256, D_IN), dtype=jnp.float32)
        gate_w = jax.random.normal(k_gw, (NUM_EXPERTS, D_IN), dtype=jnp.float32) * 0.02
        gate_b = jax.random.normal(k_gb, (NUM_EXPERTS,), dtype=jnp.float32) * 0.02
        expert_w = jax.random.normal(k_ew, (NUM_EXPERTS, D_OUT, D_IN), dtype=jnp.float32) * 0.02
        expert_b = jax.random.normal(k_eb, (NUM_EXPERTS, D_OUT), dtype=jnp.float32) * 0.02
        return {'x': x, 'gate_w': gate_w, 'gate_b': gate_b, 'expert_w': expert_w, 'expert_b': expert_b}
    _L1_ffn_all = _L1_ffn_setup()
    _L1_ffn_in = {k: v for k, v in _L1_ffn_all.items() if k in ('gate_w', 'gate_b', 'expert_w', 'expert_b')}
    del _L1_ffn_all
    return {'x': x, 'ctx_4096': ctx_4096, 'mask_1x1xSxS2_ff0': mask_1x1xSxS2_ff0, 'L0_xattn_x1_scale': _L0_xattn_in['x1_scale'], 'L0_xattn_x1_zp': _L0_xattn_in['x1_zp'], 'L0_xattn_x2_scale': _L0_xattn_in['x2_scale'], 'L0_xattn_x2_zp': _L0_xattn_in['x2_zp'], 'L0_ffn_w1': _L0_ffn_in['w1'], 'L0_ffn_s1': _L0_ffn_in['s1'], 'L0_ffn_w2': _L0_ffn_in['w2'], 'L0_ffn_s2': _L0_ffn_in['s2'], 'L0_ffn_w3': _L0_ffn_in['w3'], 'L0_ffn_s3': _L0_ffn_in['s3'], 'L1_xattn_q_proj_w': _L1_xattn_in['q_proj_w'], 'L1_xattn_k_proj_w': _L1_xattn_in['k_proj_w'], 'L1_xattn_v_proj_w': _L1_xattn_in['v_proj_w'], 'L1_xattn_o_proj_w': _L1_xattn_in['o_proj_w'], 'L1_xattn_q_norm_w': _L1_xattn_in['q_norm_w'], 'L1_xattn_k_norm_w': _L1_xattn_in['k_norm_w'], 'L1_ffn_gate_w': _L1_ffn_in['gate_w'], 'L1_ffn_gate_b': _L1_ffn_in['gate_b'], 'L1_ffn_expert_w': _L1_ffn_in['expert_w'], 'L1_ffn_expert_b': _L1_ffn_in['expert_b']}

def reference(x, ctx_4096, mask_1x1xSxS2_ff0, L0_xattn_x1_scale, L0_xattn_x1_zp, L0_xattn_x2_scale, L0_xattn_x2_zp, L0_ffn_w1, L0_ffn_s1, L0_ffn_w2, L0_ffn_s2, L0_ffn_w3, L0_ffn_s3, L1_xattn_q_proj_w, L1_xattn_k_proj_w, L1_xattn_v_proj_w, L1_xattn_o_proj_w, L1_xattn_q_norm_w, L1_xattn_k_norm_w, L1_ffn_gate_w, L1_ffn_gate_b, L1_ffn_expert_w, L1_ffn_expert_b):
    import jax
    import jax.numpy as jnp

    def _L0_xattn_ref(x1, x2, x1_scale, x1_zp, x2_scale, x2_zp):
        import jax, jax.numpy as jnp
        import numpy as np
        QMIN = 0.0
        QMAX = 255.0

        def fake_quant(x, scale, zp):
            s = scale.reshape(())
            z = zp.reshape(())
            q = jnp.clip(jnp.round(x / s + z), QMIN, QMAX)
            return (q - z) * s
        q1 = fake_quant(x1, x1_scale, x1_zp)
        q2 = fake_quant(x2, x2_scale, x2_zp)
        return jnp.matmul(q1, q2)

    def _L0_ffn_ref(x, w1, s1, w2, s2, w3, s3):
        import jax, jax.numpy as jnp
        import numpy as np
        GROUP = 64

        def dequant_q40(w, s, out_features, in_features):
            msb = w >> 4
            lsb = (w & 15 ^ 8) - 8
            g = jnp.concatenate([msb, lsb], axis=1).reshape(-1, GROUP)
            deq = g.astype(s.dtype) * s[:, None]
            return deq.reshape(out_features, in_features)
        dim = x.shape[-1]
        hidden = w1.shape[0] * w1.shape[1] * 2 // dim
        W1 = dequant_q40(w1, s1, hidden, dim)
        W3 = dequant_q40(w3, s3, hidden, dim)
        W2 = dequant_q40(w2, s2, dim, hidden)
        a = jnp.einsum('bsd,hd->bsh', x, W1)
        b = jnp.einsum('bsd,hd->bsh', x, W3)
        h = jax.nn.silu(a) * b
        return jnp.einsum('bsh,dh->bsd', h, W2)

    def _L1_xattn_ref(hidden_states, cross_attention_states, attention_mask, q_proj_w, k_proj_w, v_proj_w, o_proj_w, q_norm_w, k_norm_w):
        import jax, jax.numpy as jnp
        import numpy as np
        NUM_HEADS = 32
        NUM_KV_HEADS = 8
        HEAD_DIM = 128
        HIDDEN = 512
        EPS = 1e-05

        def rmsnorm(x, w, eps=EPS):
            xf = x.astype(jnp.float32)
            var = jnp.mean(xf * xf, axis=-1, keepdims=True)
            return w * (xf * jax.lax.rsqrt(var + eps)).astype(x.dtype)
        B, Q, _ = hidden_states.shape
        KV = cross_attention_states.shape[1]
        n_rep = NUM_HEADS // NUM_KV_HEADS
        q = (hidden_states @ q_proj_w.T).reshape(B, Q, NUM_HEADS, HEAD_DIM).transpose(0, 2, 1, 3)
        k = (cross_attention_states @ k_proj_w.T).reshape(B, KV, NUM_KV_HEADS, HEAD_DIM).transpose(0, 2, 1, 3)
        v = (cross_attention_states @ v_proj_w.T).reshape(B, KV, NUM_KV_HEADS, HEAD_DIM).transpose(0, 2, 1, 3)
        q = rmsnorm(q, q_norm_w)
        k = jnp.repeat(k, n_rep, axis=1)
        v = jnp.repeat(v, n_rep, axis=1)
        k = rmsnorm(k, k_norm_w)
        scale = 1.0 / np.sqrt(HEAD_DIM)
        scores = jnp.einsum('bhqd,bhkd->bhqk', q, k) * scale + attention_mask
        attn = jax.nn.softmax(scores.astype(jnp.float32), axis=-1).astype(q.dtype)
        out = jnp.einsum('bhqk,bhkd->bhqd', attn, v)
        out = out.transpose(0, 2, 1, 3).reshape(B, Q, NUM_HEADS * HEAD_DIM)
        return out @ o_proj_w.T

    def _L1_ffn_ref(x, gate_w, gate_b, expert_w, expert_b):
        import jax, jax.numpy as jnp
        import numpy as np
        NUM_EXPERTS = 8
        D_IN = 512
        D_OUT = 512
        orig_shape = x.shape
        xf = x.reshape(-1, x.shape[-1])
        gate_logits = xf @ gate_w.T + gate_b
        gates = jax.nn.softmax(gate_logits, axis=-1)
        selected = jnp.argmax(gates, axis=-1)
        out = jnp.zeros((xf.shape[0], expert_w.shape[1]), dtype=xf.dtype)
        for j in range(expert_w.shape[0]):
            yj = xf @ expert_w[j].T + expert_b[j]
            out = out + jnp.where((selected == j)[:, None], yj, 0.0)
        return out.reshape(*orig_shape[:-1], expert_w.shape[1])
    x = x + _L0_xattn_ref(_layernorm(x, axis=-1), ctx_4096, L0_xattn_x1_scale, L0_xattn_x1_zp, L0_xattn_x2_scale, L0_xattn_x2_zp)
    x = x + _L0_ffn_ref(_layernorm(x, axis=-1), L0_ffn_w1, L0_ffn_s1, L0_ffn_w2, L0_ffn_s2, L0_ffn_w3, L0_ffn_s3)
    x = x + _L1_xattn_ref(_layernorm(x, axis=-1), ctx_4096, mask_1x1xSxS2_ff0, L1_xattn_q_proj_w, L1_xattn_k_proj_w, L1_xattn_v_proj_w, L1_xattn_o_proj_w, L1_xattn_q_norm_w, L1_xattn_k_norm_w)
    x = x + _L1_ffn_ref(_layernorm(x, axis=-1), L1_ffn_gate_w, L1_ffn_gate_b, L1_ffn_expert_w, L1_ffn_expert_b)
    return x

_drawn_inputs = setup_inputs


def setup_inputs(seed=0):
    import zlib

    import numpy as np

    out = dict(_drawn_inputs(seed))
    spreads = {'L1_xattn_q_norm_w': (1.0, 0.6), 'L1_xattn_k_norm_w': (1.0, 0.6)}
    factors = {'L0_ffn_s1': 2.94,
     'L0_ffn_s2': 3.051,
     'L0_ffn_s3': 3.096,
     'L1_ffn_gate_b': 64.0,
     'L1_ffn_expert_b': 64.0,
     'L1_ffn_gate_w': 5.921,
     'L1_ffn_expert_w': 5.704}
    for name, (base, spread) in spreads.items():
        noise = np.random.default_rng([zlib.crc32(name.encode()), seed]).standard_normal(out[name].shape)
        drawn = base * np.exp(spread * noise) if base else spread * noise
        out[name] = jnp.asarray(drawn.astype(out[name].dtype))
    for name, factor in factors.items():
        out[name] = (out[name] * factor).astype(out[name].dtype)
    return out
```

```python
from contextlib import ExitStack

import concourse.bass as bass
from concourse import mybir

ALU = mybir.AluOpType
ACT = mybir.ActivationFunctionType
AX = mybir.AxisListType
F32 = mybir.dt.float32
F16 = mybir.dt.float16
BF16 = mybir.dt.bfloat16
I32 = mybir.dt.int32

P = 128
B, S, S2, D = 2, 256, 512, 512
T = B * S // P
C = D // P
KT = S2 // P
HEADS, KV, HD = 32, 8, 128
REP = HEADS // KV
G = KV * B
QT = S // P
GROUP = 64
HIDDEN = 1376
HT = -(-HIDDEN // P)
EXPERTS = 8
EPS = 1e-5

W_SCALE = 64.0
P_SCALE = 1024.0
O_SCALE = 16.0
ROUND = 12582912.0
MID = 128.0
BIG = 3.0e38

CTX_T, WK, NAT, WV, WQ, WO, WE = [0, 2], [1, 3], [4, 5], [6, 7], 8, 16, 24
ITEMS = 32
ITEM = 2048
CUT_V, CUT_Q, CUT_O, CUT_E = 4, 6, 14, 22
FFN_INT, FFN_SC = 1024, 1536


def kernel_program(nc, x_in, stream, ffn_int, ffn_scale, mask_in, small_in, shift_in, ident_in, bias_in, out):
    with ExitStack() as ctx:
        def sem(name):
            return ctx.enter_context(nc.semaphore(name))

        arena = ctx.enter_context(nc.sbuf_tensor("arena", [P, 204 * 256], F32))

        def at(kib, n, dtype):
            words = n if dtype in (F32, I32) else n // 2
            a = arena[:, kib * 256:kib * 256 + words]
            return a if dtype == F32 else a.bitcast(dtype)

        x_res = at(0, T * D, F32).rearrange("p (t d) -> p t d", t=T)
        xn = at(8, T * D, F32).rearrange("p (t d) -> p t d", t=T)
        xT_hi = at(16, C * 512, F16).rearrange("p (c n) -> p c n", c=C)
        xT_lo = at(20, C * 512, F16).rearrange("p (c n) -> p c n", c=C)
        kT_hi = at(24, KV * B * S2, F16).rearrange("p (h n) -> p h n", h=KV)
        kT_lo = at(40, KV * B * S2, F16).rearrange("p (h n) -> p h n", h=KV)
        kT_flat = [at(24, KV * B * S2, F16), at(40, KV * B * S2, F16)]
        v_hi = at(56, KV * B * S2, F16).rearrange("p (h n) -> p h n", h=KV)
        v_lo = at(72, KV * B * S2, F16).rearrange("p (h n) -> p h n", h=KV)
        v_flat = [at(56, KV * B * S2, F16), at(72, KV * B * S2, F16)]
        ring = at(88, 2 * ITEM, F32).rearrange("p (s n) -> p s n", s=2)
        raw_int = [at(104 + 10 * s, FFN_INT, I32) for s in range(2)]
        raw_sc = [at(108 + 10 * s, FFN_SC, F32) for s in range(2)]
        wo_hi = [at(104 + 8 * s, ITEM, F16) for s in range(2)]
        wo_lo = [at(108 + 8 * s, ITEM, F16) for s in range(2)]
        mask = at(120, QT * S2, F32).rearrange("p (q n) -> p q n", q=QT)
        cT_hi = at(124, C * B * S2, F16).rearrange("p (c n) -> p c n", c=C)
        cT_lo = at(132, C * B * S2, F16).rearrange("p (c n) -> p c n", c=C)
        wv_hi = at(140, 2 * ITEM, F16).rearrange("p (h n) -> p h n", h=2)
        wv_lo = at(148, 2 * ITEM, F16).rearrange("p (h n) -> p h n", h=2)
        wk_hi = at(156, 2 * ITEM, F16).rearrange("p (h n) -> p h n", h=2)
        wk_lo = at(164, 2 * ITEM, F16).rearrange("p (h n) -> p h n", h=2)
        q2 = at(172, B * KT * D, BF16).rearrange("p (b k n) -> p b k n", b=B, k=KT)
        q1T = at(180, KT * 512, BF16).rearrange("p (k n) -> p k n", k=KT)
        k_unit = at(184, 2 * 512, F32).rearrange("p (s n) -> p s n", s=2)
        k_square = at(188, 2 * 512, F32).rearrange("p (s n) -> p s n", s=2)
        q1 = at(192, T * D, BF16).rearrange("p (t n) -> p t n", t=T)
        col_term = at(196, B * D, F32).rearrange("p (b n) -> p b n", b=B)
        cross = at(200, 2 * D, F32).rearrange("p (s n) -> p s n", s=2)
        nib = at(156, FFN_SC, I32)
        w13_f = at(162, 1024, F32)
        w2_f = [at(166 + 2 * s, 512, F32) for s in range(2)]
        w13_hi = [at(170 + 4 * s, 1024, F16) for s in range(2)]
        w13_lo = [at(172 + 4 * s, 1024, F16) for s in range(2)]
        w2_hi = [at(178 + 2 * s, 512, F16) for s in range(2)]
        w2_lo = [at(179 + 2 * s, 512, F16) for s in range(2)]
        h_hi = [at(182 + 2 * s, 512, F16) for s in range(2)]
        h_lo = [at(183 + 2 * s, 512, F16) for s in range(2)]
        q_hi = at(124, G * REP * S, F16)
        q_lo = at(156, G * REP * S, F16)
        wq_hi = [at(188 + 8 * s, ITEM, F16) for s in range(2)]
        wq_lo = [at(192 + 8 * s, ITEM, F16) for s in range(2)]
        pT_hi = [at(188 + 8 * s, KT * 512, F16).rearrange("p (k n) -> p k n", k=KT) for s in range(2)]
        pT_lo = [at(192 + 8 * s, KT * 512, F16).rearrange("p (k n) -> p k n", k=KT) for s in range(2)]

        bias_f = at(24, D, F32)[0:EXPERTS, :]
        oneT = at(26, T * P, F16)[0:EXPERTS, :].rearrange("e (t n) -> e t n", t=T)

        def sb(name, shape, dtype):
            return ctx.enter_context(nc.sbuf_tensor(name, shape, dtype))

        ident = sb("ident", [P, P], F32)
        ident_b = sb("ident_b", [P, P], BF16)
        ones_b = sb("ones_b", [P, P], BF16)
        small = sb("small", [P, 56], F32)
        shift = sb("shift", [P, 6], I32)
        eps = sb("eps", [P, 1], F32)
        cst = sb("cst", [P, 12], F32)
        gate_hi = sb("gate_hi", [P, C * EXPERTS], F16)
        gate_lo = sb("gate_lo", [P, C * EXPERTS], F16)
        ln_st = sb("ln_st", [P, T, 6], F32)
        ln_mv = sb("ln_mv", [P, T, 2], F32)
        ln_sd = sb("ln_sd", [P, T], F32)
        ln_r = sb("ln_r", [P, T], F32)
        row_sum = sb("row_sum", [P, T], F32)
        row_term = sb("row_term", [P, T], F32)
        sumsq = sb("sumsq", [P, 2, REP], F32)
        rms = sb("rms", [P, 2, REP], F32)
        inv_rms = sb("inv_rms", [P, 2, REP], F32)
        nmax = sb("nmax", [P, 4], F32)
        psum_p = sb("psum_p", [P, 4], F32)
        inv_p = sb("inv_p", [P, 4], F32)
        lg = sb("lg", [P, T, EXPERTS], F32)
        top = sb("top", [P, T], F32)
        cand = sb("cand", [P, T, EXPERTS], F32)
        first = sb("first", [P, T], F32)
        onehot = sb("onehot", [P, T, EXPERTS], F32)
        onehot_s = sb("onehot_s", [P, T, EXPERTS], F32)

        bank = [ctx.enter_context(nc.psum_tensor(f"bank{i}", [P, 512], F32)) for i in range(8)]

        const_in = sem("const_in")
        x_loaded = sem("x_loaded")
        mask_loaded = sem("mask_loaded")
        bias_loaded = sem("bias_loaded")
        ring_in = [sem("ring_in0"), sem("ring_in1")]
        ffn_in = [sem("ffn_in0"), sem("ffn_in1")]
        out_stored = sem("out_stored")
        cst_ready = sem("cst_ready")
        dve_step = sem("dve_step")
        pool_step = sem("pool_step")
        cut_hi = sem("cut_hi")
        cut_lo = sem("cut_lo")
        ln_stats = sem("ln_stats")
        ln_std = sem("ln_std")
        ln_rstd = sem("ln_rstd")
        xn_ready = sem("xn_ready")
        xT_turned = sem("xT_turned")
        xT_cut_hi = sem("xT_cut_hi")
        xT_cut_lo = sem("xT_cut_lo")
        x_scaled = sem("x_scaled")
        nat_scaled = sem("nat_scaled")
        q1_ready = sem("q1_ready")
        q2_ready = sem("q2_ready")
        q1_turned = sem("q1_turned")
        q1T_ready = sem("q1T_ready")
        col_sum = sem("col_sum")
        cross_done = sem("cross_done")
        cross_used = sem("cross_used")
        n_proj = sem("n_proj")
        n_square = sem("n_square")
        n_sumsq = sem("n_sumsq")
        n_rms = sem("n_rms")
        n_inv = sem("n_inv")
        n_unit = sem("n_unit")
        n_turned = sem("n_turned")
        n_hi = sem("n_hi")
        n_lo = sem("n_lo")
        v_proj = sem("v_proj")
        v_cut_hi = sem("v_cut_hi")
        v_cut_lo = sem("v_cut_lo")
        nibbles = sem("nibbles")
        floated = sem("floated")
        w_scaled = sem("w_scaled")
        w13_cut_hi = sem("w13_cut_hi")
        w13_cut_lo = sem("w13_cut_lo")
        w2_cut_hi = sem("w2_cut_hi")
        w2_cut_lo = sem("w2_cut_lo")
        ab_done = sem("ab_done")
        exp_a = sem("exp_a")
        silu_step = sem("silu_step")
        h_ready = sem("h_ready")
        h_cut_hi = sem("h_cut_hi")
        h_cut_lo = sem("h_cut_lo")
        ffn_tile = sem("ffn_tile")
        ffn_out = sem("ffn_out")
        scored = sem("scored")
        masked = sem("masked")
        exped = sem("exped")
        inverted = sem("inverted")
        p_ready = sem("p_ready")
        p_turned = sem("p_turned")
        p_hi = sem("p_hi")
        p_lo = sem("p_lo")
        pv_done = sem("pv_done")
        o_hi = sem("o_hi")
        o_lo = sem("o_lo")
        o_group = sem("o_group")
        o_out = sem("o_out")
        logits = sem("logits")
        chosen = sem("chosen")
        choice_turned = sem("choice_turned")
        choice_T = sem("choice_T")
        bias_out = sem("bias_out")
        bias_added = sem("bias_added")
        e_unit = sem("e_unit")
        e_added = sem("e_added")

        def wait(eng, s, count):
            if not (isinstance(count, int) and count <= 0):
                eng.wait_ge(s, count)

        def item_of(cut):
            return cut if cut < CUT_V else cut + 2

        def chunks(a):
            return a.rearrange("p (c n) -> p c n", c=C)

        def cut_target(cut, par):
            if cut in (0, 2):
                b = cut // 2
                return cT_hi[:, :, b * S2:(b + 1) * S2], cT_lo[:, :, b * S2:(b + 1) * S2]
            if cut in (1, 3):
                return chunks(wk_hi[:, cut // 2, :]), chunks(wk_lo[:, cut // 2, :])
            return chunks(wv_hi[:, cut - CUT_V, :]), chunks(wv_lo[:, cut - CUT_V, :])

        def k_units(eng, step, after_first=None, after_third=None):
            for half in range(2):
                step(half, 0, 0)
                done = 0
                if half == 0:
                    if after_first:
                        after_first()
                    step(0, 1, 1)
                    step(0, 2, 0)
                    done = 1
                    if after_third:
                        after_third()
                with eng.Fori(done, 3) as m:
                    step(half, 2 * m + 1, 1)
                    step(half, 2 * m + 2, 0)
                step(half, 7, 1)

        block = ctx.enter_context(nc.Block())

        @block.sync
        def _(sp):
            sp.dma_start(x_res, x_in.rearrange("(t p) d -> p t d", p=P)).then_inc(x_loaded, 16)

            def load_item(r, slot, count):
                if isinstance(r, int) and r < 2:
                    pass
                elif isinstance(r, int) and r < 6:
                    sp.wait_ge(cut_lo, r - 1)
                elif isinstance(r, int) and r < 8:
                    sp.wait_ge(q2_ready, r - 5)
                else:
                    sp.wait_ge(cut_lo, count)
                sp.dma_start(ring[:, slot, :], stream[r]).then_inc(ring_in[slot], 16)

            def load_ffn(j, par):
                wait(sp, w_scaled, j - 1)
                sp.dma_start(raw_int[par], ffn_int[j]).then_inc(ffn_in[par], 16)
                sp.dma_start(raw_sc[par], ffn_scale[j]).then_inc(ffn_in[par], 16)

            load_item(0, 0, 0)
            load_item(1, 1, 0)
            sp.dma_start(small[:], small_in).then_inc(const_in, 16)
            sp.dma_start(shift[:], shift_in).then_inc(const_in, 16)
            sp.dma_start(ident[:], ident_in).then_inc(const_in, 16)
            load_item(2, 0, 0)
            load_item(3, 1, 0)
            load_ffn(0, 0)
            load_item(4, 0, 0)
            load_item(5, 1, 0)
            load_ffn(1, 1)
            load_item(6, 0, 0)
            load_item(7, 1, 0)
            load_item(8, 0, 5)
            load_item(9, 1, 6)
            with sp.Fori(1, HT // 2) as m:
                load_ffn(2 * m, 0)
                load_ffn(2 * m + 1, 1)
            load_ffn(HT - 1, 0)
            sp.wait_ge(w_scaled, HT - 1)
            sp.dma_start(mask, mask_in.rearrange("(q p) n -> p q n", p=P)).then_inc(mask_loaded, 16)
            with sp.Fori(5, WE // 2) as m:
                load_item(2 * m, 0, 2 * m - 3)
                load_item(2 * m + 1, 1, 2 * m - 2)
            sp.wait_ge(scored, 8 * G)
            sp.dma_start(bias_f, bias_in).then_inc(bias_loaded, 16)
            with sp.Fori(WE // 2, ITEMS // 2) as m:
                load_item(2 * m, 0, 2 * m - 3)
                load_item(2 * m + 1, 1, 2 * m - 2)
            for t in range(T):
                sp.wait_ge(e_added, T * (EXPERTS - 1) + t + 1)
                sp.dma_start(out[t * P:(t + 1) * P, :], x_res[:, t, :]).then_inc(out_stored, 16)
            sp.wait_ge(out_stored, 16 * T)

        @block.gpsimd
        def _(pool):
            steps = [0]

            def then(ins):
                steps[0] += 1
                ins.then_inc(pool_step, 1)
                pool.wait_ge(pool_step, steps[0])

            pool.wait_ge(cst_ready, 1)
            pool.wait_ge(ln_rstd, 1)
            for t in range(T):
                then(nc.gpsimd.tensor_scalar(xn[:, t, :], x_res[:, t, :], ln_mv[:, t, 0:1], ln_r[:, t:t + 1],
                                             ALU.subtract, ALU.mult))
                then(nc.gpsimd.tensor_scalar(xn[:, t, :], xn[:, t, :], cst[:, 0:1], small[:, 1:2],
                                             ALU.mult, ALU.add))
                nc.gpsimd.tensor_scalar(xn[:, t, :], xn[:, t, :], 255.0, 0.0, ALU.min, ALU.max).then_inc(x_scaled, 1)
            for b in range(B):
                pool.wait_ge(ring_in[NAT[b] % 2], 16 * (NAT[b] // 2 + 1))
                raw = ring[:, NAT[b] % 2, :]
                then(nc.gpsimd.tensor_scalar(raw, raw, cst[:, 1:2], small[:, 3:4], ALU.mult, ALU.add))
                nc.gpsimd.tensor_scalar(raw, raw, 255.0, 0.0, ALU.min, ALU.max).then_inc(nat_scaled, 1)

            def scale_weights(j, par):
                pool.wait_ge(floated, j + 1)
                pool.wait_ge(ffn_in[par], 16 * (j + 2 - par))
                nc.gpsimd.tensor_tensor(w13_f, w13_f, raw_sc[par][:, 0:1024], ALU.mult)
                nc.gpsimd.tensor_tensor(w2_f[par], w2_f[par], raw_sc[par][:, 1024:1536],
                                        ALU.mult).then_inc(w_scaled, 1)

            scale_weights(0, 0)
            scale_weights(1, 1)
            with pool.Fori(1, HT // 2) as m:
                scale_weights(2 * m, 0)
                scale_weights(2 * m + 1, 1)
            scale_weights(HT - 1, 0)

            def normalise(k, u):
                pool.wait_ge(inverted, k + 1)
                nc.gpsimd.tensor_tensor(xn[:, u % 4, :], xn[:, u % 4, :],
                                        inv_p[:, u % 4:u % 4 + 1].broadcast_to([P, S2]),
                                        ALU.mult).then_inc(p_ready, 1)

            with pool.Fori(0, G) as g:
                for u in range(8):
                    normalise(8 * g + u, u)

        @block.scalar
        def _(act):
            def cut(c, par, target, scale):
                r = item_of(c) if isinstance(c, int) else c + 2
                act.wait_ge(ring_in[par], (r // 2 + 1) * 16 if isinstance(r, int) else 8 * (r - par) + 16)
                nc.scalar.activation(target, chunks(ring[:, par, :]), ACT.Copy, scale=scale).then_inc(cut_hi, 1)

            def layer_norm_std(stage, t0, t1):
                act.wait_ge(ln_stats, T * stage + t1)
                nc.scalar.activation(ln_sd[:, t0:t1], ln_mv[:, t0:t1, 1], ACT.Sqrt, bias=eps[:]).then_inc(ln_std, 1)

            def turned_x(stage):
                for t in range(T):
                    act.wait_ge(xT_turned, T * (stage - 1) + t + 1)
                    nc.scalar.activation(xT_hi[:, :, t * P:(t + 1) * P],
                                         bank[4 + t][:].rearrange("p (c n) -> p c n", c=C),
                                         ACT.Copy).then_inc(xT_cut_hi, 1)

            def norm_square(n, par, square):
                act.wait_ge(n_proj, n + 1)
                wait(act, n_sumsq, n - 1)
                nc.scalar.activation(square[:, par, :], bank[par][:], ACT.Square,
                                     scale=1.0 / W_SCALE).then_inc(n_square, 1)
                act.wait_ge(n_sumsq, n + 1)
                nc.scalar.activation(rms[:, par, :], sumsq[:, par, :], ACT.Sqrt, bias=eps[:],
                                     scale=1.0 / HD).then_inc(n_rms, 1)

            def norm_hi(n, par, target, weight):
                act.wait_ge(n_turned, n + 1)
                nc.scalar.activation(target, bank[2 + par][:].rearrange("p (h n) -> p h n", h=REP), ACT.Copy,
                                     scale=weight).then_inc(n_hi, 1)

            act.wait_ge(cst_ready, 1)
            layer_norm_std(0, 0, T)
            cut(0, 0, cut_target(0, 0)[0], 1.0)
            cut(1, 1, cut_target(1, 1)[0], W_SCALE)

            def k_tail(half, i, par):
                norm_hi(8 * half + i, par, kT_hi[:, REP * half:REP * half + REP, bass.ds(i * P, P)], cst[:, 11:12])

            def k_step(half, i, par):
                norm_square(8 * half + i, par, k_square)
                if isinstance(i, int) and i == 0:
                    if half:
                        k_tail(half - 1, 7, 1)
                else:
                    k_tail(half, i - 1, 1 - par)

            k_units(act, k_step,
                    lambda: cut(2, 0, cut_target(2, 0)[0], 1.0),
                    lambda: cut(3, 1, cut_target(3, 1)[0], W_SCALE))
            k_tail(1, 7, 1)
            cut(4, 0, cut_target(4, 0)[0], W_SCALE)
            cut(5, 1, cut_target(5, 1)[0], W_SCALE)
            act.wait_ge(const_in, 48)
            nc.scalar.activation(gate_hi[:], small[:, 24:56], ACT.Copy, scale=W_SCALE).then_inc(cst_ready, 1)
            for t in range(T):
                layer_norm_std(1, t, t + 1)

            def v_step(half, i, par):
                act.wait_ge(v_proj, 8 * half + i + 1)
                nc.scalar.activation(v_hi[:, REP * half:REP * half + REP, bass.ds(i * P, P)],
                                     bank[par][:].rearrange("p (h n) -> p h n", h=REP), ACT.Copy,
                                     scale=1.0 / W_SCALE).then_inc(v_cut_hi, 1)

            def to_float(j, par):
                act.wait_ge(nibbles, j + 1)
                wait(act, w13_cut_lo, j)
                nc.scalar.activation(w13_f, nib[:, 0:1024], ACT.Copy)
                wait(act, w2_cut_lo, j - 1)
                nc.scalar.activation(w2_f[par], nib[:, 1024:1536], ACT.Copy).then_inc(floated, 1)

            def w13_hi_part(j, par):
                act.wait_ge(w_scaled, j + 1)
                wait(act, ab_done, j - 1)
                nc.scalar.activation(w13_hi[par], w13_f, ACT.Copy, scale=W_SCALE).then_inc(w13_cut_hi, 1)

            def w2_hi_part(j, par):
                act.wait_ge(w_scaled, j + 1)
                wait(act, ffn_tile, j - 1)
                nc.scalar.activation(w2_hi[par], w2_f[par], ACT.Copy, scale=W_SCALE).then_inc(w2_cut_hi, 1)

            with act.Fori(0, 4) as m:
                v_step(0, 2 * m, 0)
                v_step(0, 2 * m + 1, 1)
            turned_x(1)
            to_float(0, 0)
            with act.Fori(0, 3) as m:
                v_step(1, 2 * m, 0)
                v_step(1, 2 * m + 1, 1)
            w13_hi_part(0, 0)
            w2_hi_part(0, 0)
            v_step(1, 6, 0)
            to_float(1, 1)
            v_step(1, 7, 1)
            w13_hi_part(1, 1)

            def ffn_step(j, par):
                if not (isinstance(j, int) and j + 2 >= HT):
                    to_float(j + 2, par)
                act.wait_ge(ab_done, j + 1)
                wait(act, h_ready, j)
                nc.scalar.activation(xn[:, 0, :], bank[2 * par][:], ACT.Exp, scale=-1.0 / W_SCALE).then_inc(exp_a, 1)
                act.wait_ge(h_ready, j + 1)
                wait(act, ffn_tile, j - 1)
                nc.scalar.activation(h_hi[par], xn[:, 3, :], ACT.Copy).then_inc(h_cut_hi, 1)
                if not (isinstance(j, int) and j + 2 >= HT):
                    w13_hi_part(j + 2, par)
                if not (isinstance(j, int) and j + 1 >= HT):
                    w2_hi_part(j + 1, 1 - par)

            ffn_step(0, 0)
            ffn_step(1, 1)
            with act.Fori(1, 4) as m:
                ffn_step(2 * m, 0)
                ffn_step(2 * m + 1, 1)
            for j in range(8, HT):
                ffn_step(j, j % 2)

            def q_cut(kv, par):
                wait(act, n_proj, 16 + 4 * kv - 4)
                cut(CUT_Q + kv, par, chunks(wq_hi[par]), W_SCALE)

            def q_target(flat, kv, t):
                base = kv * (B * REP * S) + (t // QT) * (REP * S)
                return flat[:, bass.ds(base, REP * S)].rearrange("p (h n) -> p h n", h=REP)[
                    :, :, (t % QT) * P:(t % QT + 1) * P]

            def q_tail(kv, t):
                norm_hi(16 + 4 * kv + t, t % 2, q_target(q_hi, kv, t), cst[:, 10:11])

            def q_group(kv, par):
                for t in range(T):
                    norm_square(16 + 4 * kv + t, t % 2, xn[:, 2:4, :])
                    if t:
                        q_tail(kv, t - 1)
                    elif not (isinstance(kv, int) and kv == 0):
                        q_tail(kv - 1, T - 1)
                    if t == 1 and not (isinstance(kv, int) and kv + 1 >= KV):
                        q_cut(kv + 1, 1 - par)

            for t in range(T):
                layer_norm_std(2, t, t + 1)
            q_cut(0, 0)
            turned_x(2)
            q_group(0, 0)
            q_group(1, 1)
            with act.Fori(1, 3) as m:
                q_group(2 * m, 0)
                q_group(2 * m + 1, 1)
            q_group(6, 0)
            q_group(7, 1)
            q_tail(7, T - 1)

            def o_hi_part(m, pair):
                act.wait_ge(pv_done, m + 1)
                nc.scalar.activation(q_hi[:, bass.ds(m * 512, 512)], bank[6 + pair][:], ACT.Copy,
                                     scale=O_SCALE / P_SCALE).then_inc(o_hi, 1)

            def attend(g, u):
                k = 8 * g + u
                first, last = isinstance(g, int) and g == 0, isinstance(g, int) and g == G
                if u == 0 and not (isinstance(g, int) and g < 2):
                    o_hi_part(2 * g - 3, 1)
                if u == 4 and not first:
                    o_hi_part(2 * g - 2, 0)
                if not last:
                    act.wait_ge(masked, k + 1)
                    nc.scalar.activation(xn[:, u % 4, :], xn[:, u % 4, :], ACT.Exp, bias=nmax[:, u % 4:u % 4 + 1],
                                         scale=-1.0, accum_out=psum_p[:, u % 4:u % 4 + 1]).then_inc(exped, 1)
                if not (first and u < 3) and not (last and u >= 3):
                    w = (u + 5) % 8
                    act.wait_ge(p_turned, k - 2)
                    if u >= 3:
                        wait(act, pv_done, 2 * g + w // 4 - 1)
                    else:
                        wait(act, pv_done, 2 * g - 2)
                    pair, h, qt = w // 4, w // 2 % 2, w % 2
                    nc.scalar.activation(pT_hi[pair][:, :, h * S + qt * P:h * S + (qt + 1) * P],
                                         bank[4 + w % 2][:].rearrange("p (k n) -> p k n", k=KT),
                                         ACT.Copy, scale=P_SCALE).then_inc(p_hi, 1)

            for u in range(8):
                attend(0, u)
            for u in range(8):
                attend(1, u)
            with act.Fori(2, G) as g:
                for u in range(8):
                    attend(g, u)
            for u in range(8):
                attend(G, u)
            o_hi_part(2 * G - 1, 1)

            def o_cut(kv, par):
                wait(act, o_group, kv - 1)
                cut(CUT_O + kv, par, chunks(wo_hi[par]), W_SCALE)

            def e_cut(j, par):
                wait(act, e_unit, T * (j - 1))
                cut(CUT_E + j, par, chunks(wq_hi[par]), W_SCALE)

            o_cut(0, 0)
            o_cut(1, 1)
            with act.Fori(1, KV // 2) as m:
                o_cut(2 * m, 0)
                o_cut(2 * m + 1, 1)
            e_cut(0, 0)
            e_cut(1, 1)
            for t in range(T):
                layer_norm_std(3, t, t + 1)
            turned_x(3)
            with act.Fori(1, EXPERTS // 2) as m:
                e_cut(2 * m, 0)
                e_cut(2 * m + 1, 1)

        @block.vector
        def _(dve):
            steps = [0]

            def then(ins):
                steps[0] += 1
                ins.then_inc(dve_step, 1)
                dve.wait_ge(dve_step, steps[0])

            def cut(c, par, hi, lo, scale):
                dve.wait_ge(cut_hi, c + 1)
                nc.vector.scalar_tensor_tensor(lo, chunks(ring[:, par, :]), scale, hi, ALU.mult,
                                               ALU.subtract).then_inc(cut_lo, 1)

            def cut_k(c):
                hi, lo = cut_target(c, 0)
                cut(c, item_of(c) % 2, hi, lo, 1.0 if c in (0, 2) else W_SCALE)

            def layer_norm_stats(t):
                then(nc.vector.bn_stats(ln_st[:, t, :], x_res[:, t, :]))
                nc.vector.bn_aggr(ln_mv[:, t, :], ln_st[:, t, :]).then_inc(ln_stats, 1)

            def layer_norm_out(stage, t):
                dve.wait_ge(ln_std, 1 + T * (stage - 1) + t + 1)
                then(nc.vector.reciprocal(ln_r[:, t:t + 1], ln_sd[:, t:t + 1]))
                nc.vector.tensor_scalar(xn[:, t, :], x_res[:, t, :], ln_mv[:, t, 0:1], ln_r[:, t:t + 1],
                                        ALU.subtract, ALU.mult).then_inc(xn_ready, 1)

            def turned_x(stage):
                for t in range(T):
                    dve.wait_ge(xT_cut_hi, T * (stage - 1) + t + 1)
                    nc.vector.tensor_tensor(xT_lo[:, :, t * P:(t + 1) * P],
                                            bank[4 + t][:].rearrange("p (c n) -> p c n", c=C),
                                            xT_hi[:, :, t * P:(t + 1) * P], ALU.subtract).then_inc(xT_cut_lo, 1)

            def norm_scale(n, par, square, unit):
                dve.wait_ge(n_square, n + 1)
                nc.vector.tensor_reduce(sumsq[:, par, :], square[:, par, :].rearrange("p (h n) -> p h n", h=REP),
                                        AX.X, ALU.add).then_inc(n_sumsq, 1)
                dve.wait_ge(n_rms, n + 1)
                nc.vector.reciprocal(inv_rms[:, par, :], rms[:, par, :]).then_inc(n_inv, 1)
                dve.wait_ge(n_inv, n + 1)
                wait(dve, n_turned, n - 1)
                nc.vector.scalar_tensor_tensor(
                    unit[:, par, :].rearrange("p (h n) -> p h n", h=REP),
                    bank[par][:].rearrange("p (h n) -> p h n", h=REP), 1.0 / W_SCALE,
                    inv_rms[:, par, :].unsqueeze(2).broadcast_to([P, REP, HD]), ALU.mult,
                    ALU.mult).then_inc(n_unit, 1)

            def norm_lo(n, par, hi, lo, weight):
                dve.wait_ge(n_hi, n + 1)
                nc.vector.scalar_tensor_tensor(lo, bank[2 + par][:].rearrange("p (h n) -> p h n", h=REP), weight,
                                               hi, ALU.mult, ALU.subtract).then_inc(n_lo, 1)

            nc.vector.memset(ones_b[:], 1.0)
            nc.vector.memset(eps[:], EPS)
            dve.wait_ge(const_in, 48)
            nc.vector.tensor_copy(ident_b[:], ident[:])
            then(nc.vector.reciprocal(cst[:, 0:1], small[:, 0:1]))
            nc.vector.reciprocal(cst[:, 1:2], small[:, 2:3])
            nc.vector.tensor_tensor(cst[:, 2:3], small[:, 0:1], small[:, 2:3], ALU.mult)
            nc.vector.tensor_scalar(cst[:, 3:4], small[:, 1:2], -1.0, MID, ALU.mult, ALU.add)
            then(nc.vector.tensor_scalar(cst[:, 4:5], small[:, 3:4], -1.0, MID, ALU.mult, ALU.add))
            then(nc.vector.tensor_tensor(cst[:, 5:6], cst[:, 3:4], cst[:, 4:5], ALU.mult))
            then(nc.vector.tensor_scalar(cst[:, 5:6], cst[:, 5:6], float(S2), None, ALU.mult))
            nc.vector.tensor_scalar(cst[:, 10:12], small[:, 4:6], float(HD) ** -0.25, None,
                                    ALU.mult).then_inc(cst_ready, 1)
            dve.wait_ge(x_loaded, 16)
            for t in range(T):
                layer_norm_stats(t)
            dve.wait_ge(ln_std, 1)
            nc.vector.reciprocal(ln_r[:], ln_sd[:]).then_inc(ln_rstd, 1)
            cut_k(0)
            cut_k(1)

            def k_tail(half, i, par):
                hs = slice(REP * half, REP * half + REP)
                norm_lo(8 * half + i, par, kT_hi[:, hs, bass.ds(i * P, P)], kT_lo[:, hs, bass.ds(i * P, P)],
                        cst[:, 11:12])

            def k_step(half, i, par):
                norm_scale(8 * half + i, par, k_square, k_unit)
                if isinstance(i, int) and i == 0:
                    if half:
                        quantise()
                        k_tail(half - 1, 7, 1)
                else:
                    k_tail(half, i - 1, 1 - par)

            def quantise():
                for t in range(T):
                    dve.wait_ge(x_scaled, t + 1)
                    then(nc.vector.tensor_scalar(q1[:, t, :], xn[:, t, :], ROUND, ROUND + MID, ALU.add,
                                                 ALU.subtract))
                    nc.vector.tensor_reduce(row_sum[:, t:t + 1], q1[:, t, :], AX.X, ALU.add).then_inc(q1_ready, 1)
                for b in range(B):
                    dve.wait_ge(nat_scaled, b + 1)
                    nc.vector.tensor_scalar(q2[:, b, :, :], chunks(ring[:, NAT[b] % 2, :]), ROUND, ROUND + MID,
                                            ALU.add, ALU.subtract).then_inc(q2_ready, 1)

            k_units(dve, k_step, lambda: cut_k(2), lambda: cut_k(3))
            k_tail(1, 7, 1)

            for t in range(T):
                dve.wait_ge(q1_turned, t + 1)
                nc.vector.tensor_copy(q1T[:, :, t * P:(t + 1) * P],
                                      bank[4 + t % 2][:].bitcast(BF16)[:, 0:KT * P].rearrange(
                                          "p (k n) -> p k n", k=KT)).then_inc(q1T_ready, 1)
            cut_k(4)
            then(nc.vector.tensor_scalar(row_term[:], row_sum[:], cst[:, 4:5], cst[:, 5:6], ALU.mult, ALU.add))
            for b in range(B):
                dve.wait_ge(col_sum, b + 1)
                then(nc.vector.tensor_scalar(col_term[:, b, :], bank[4 + b][:], cst[:, 3:4], None, ALU.mult))
            for t in range(T + 1):
                if t < T:
                    dve.wait_ge(cross_done, t + 1)
                    ins = nc.vector.scalar_tensor_tensor(cross[:, t % 2, :], bank[6 + t % 2][:],
                                                         row_term[:, t:t + 1], col_term[:, t // QT, :],
                                                         ALU.add, ALU.add)
                    ins.then_inc(cross_used, 1)
                    dve.wait_ge(cross_used, t + 1)
                    then(nc.vector.scalar_tensor_tensor(x_res[:, t, :], cross[:, t % 2, :], cst[:, 2:3],
                                                        x_res[:, t, :], ALU.mult, ALU.add))
                    layer_norm_stats(t)
                if t:
                    layer_norm_out(1, t - 1)
            cut_k(5)

            def v_step(half, i, par):
                hs = slice(REP * half, REP * half + REP)
                dve.wait_ge(v_cut_hi, 8 * half + i + 1)
                nc.vector.scalar_tensor_tensor(v_lo[:, hs, bass.ds(i * P, P)],
                                               bank[par][:].rearrange("p (h n) -> p h n", h=REP), 1.0 / W_SCALE,
                                               v_hi[:, hs, bass.ds(i * P, P)], ALU.mult,
                                               ALU.subtract).then_inc(v_cut_lo, 1)

            def unpack(j, par):
                dve.wait_ge(ffn_in[par], 16 * (j + 2 - par))
                wait(dve, floated, j)
                words = raw_int[par][:, 0:512].rearrange("p (m h) -> p m h", m=4)
                out13 = nib[:, 0:1024].rearrange("p (m b h) -> p m b h", m=4, b=2)
                for b in range(2):
                    nc.vector.tensor_scalar(out13[:, :, b, :], words, shift[:, 4 + b:5 + b], 28,
                                            ALU.logical_shift_left, ALU.arith_shift_right)
                out2 = nib[:, 1024:1536].rearrange("p (q r) -> p q r", r=4)
                for r in range(4):
                    ins = nc.vector.tensor_scalar(out2[:, :, r], raw_int[par][:, 512 + 128 * r:640 + 128 * r],
                                                  shift[:, r:r + 1], 28, ALU.logical_shift_left,
                                                  ALU.arith_shift_right)
                ins.then_inc(nibbles, 1)

            def w13_lo_part(j, par):
                dve.wait_ge(w13_cut_hi, j + 1)
                nc.vector.scalar_tensor_tensor(w13_lo[par], w13_f, W_SCALE, w13_hi[par], ALU.mult,
                                               ALU.subtract).then_inc(w13_cut_lo, 1)

            def w2_lo_part(j, par):
                dve.wait_ge(w2_cut_hi, j + 1)
                nc.vector.scalar_tensor_tensor(w2_lo[par], w2_f[par], W_SCALE, w2_hi[par], ALU.mult,
                                               ALU.subtract).then_inc(w2_cut_lo, 1)

            with dve.Fori(0, 4) as m:
                v_step(0, 2 * m, 0)
                v_step(0, 2 * m + 1, 1)
            turned_x(1)
            unpack(0, 0)
            with dve.Fori(0, 3) as m:
                v_step(1, 2 * m, 0)
                v_step(1, 2 * m + 1, 1)
            w13_lo_part(0, 0)
            w2_lo_part(0, 0)
            unpack(1, 1)
            v_step(1, 6, 0)
            v_step(1, 7, 1)
            w13_lo_part(1, 1)

            def ffn_step(j, par):
                if not (isinstance(j, int) and j + 2 >= HT):
                    unpack(j + 2, par)
                dve.wait_ge(exp_a, j + 1)
                wait(dve, silu_step, 3 * j)
                nc.vector.tensor_scalar(xn[:, 0, :], xn[:, 0, :], 1.0, None, ALU.add).then_inc(silu_step, 1)
                dve.wait_ge(silu_step, 3 * j + 1)
                nc.vector.reciprocal(xn[:, 1, :], xn[:, 0, :]).then_inc(silu_step, 1)
                dve.wait_ge(silu_step, 3 * j + 2)
                nc.vector.tensor_tensor(xn[:, 2, :], bank[2 * par][:], xn[:, 1, :], ALU.mult).then_inc(silu_step, 1)
                dve.wait_ge(silu_step, 3 * j + 3)
                wait(dve, h_cut_lo, j)
                nc.vector.scalar_tensor_tensor(xn[:, 3, :], xn[:, 2, :], W_SCALE ** -2, bank[2 * par + 1][:],
                                               ALU.mult, ALU.mult).then_inc(h_ready, 1)
                dve.wait_ge(h_cut_hi, j + 1)
                nc.vector.tensor_tensor(h_lo[par], xn[:, 3, :], h_hi[par], ALU.subtract).then_inc(h_cut_lo, 1)
                if not (isinstance(j, int) and j + 2 >= HT):
                    w13_lo_part(j + 2, par)
                if not (isinstance(j, int) and j + 1 >= HT):
                    w2_lo_part(j + 1, 1 - par)

            ffn_step(0, 0)
            ffn_step(1, 1)
            with dve.Fori(1, 4) as m:
                ffn_step(2 * m, 0)
                ffn_step(2 * m + 1, 1)
            for j in range(8, HT):
                ffn_step(j, j % 2)

            def residual(stage, done, per, banks, scale):
                for t in range(T + 1):
                    if t < T:
                        dve.wait_ge(done, per + t)
                        then(nc.vector.scalar_tensor_tensor(x_res[:, t, :], banks[t][:], scale, x_res[:, t, :],
                                                            ALU.mult, ALU.add))
                        layer_norm_stats(t)
                    if t:
                        layer_norm_out(stage, t - 1)

            residual(2, ffn_out, 1, bank[4:8], 1.0 / W_SCALE)

            def q_cut(kv, par):
                cut(CUT_Q + kv, par, chunks(wq_hi[par]), chunks(wq_lo[par]), W_SCALE)

            def q_target(flat, kv, t):
                base = kv * (B * REP * S) + (t // QT) * (REP * S)
                return flat[:, bass.ds(base, REP * S)].rearrange("p (h n) -> p h n", h=REP)[
                    :, :, (t % QT) * P:(t % QT + 1) * P]

            def q_tail(kv, t):
                norm_lo(16 + 4 * kv + t, t % 2, q_target(q_hi, kv, t), q_target(q_lo, kv, t), cst[:, 10:11])

            def q_group(kv, par):
                for t in range(T):
                    norm_scale(16 + 4 * kv + t, t % 2, xn[:, 2:4, :], xn[:, 0:2, :])
                    if t:
                        q_tail(kv, t - 1)
                    elif not (isinstance(kv, int) and kv == 0):
                        q_tail(kv - 1, T - 1)
                    if t == 1 and not (isinstance(kv, int) and kv + 1 >= KV):
                        q_cut(kv + 1, 1 - par)

            q_cut(0, 0)
            turned_x(2)
            q_group(0, 0)
            q_group(1, 1)
            with dve.Fori(1, 3) as m:
                q_group(2 * m, 0)
                q_group(2 * m + 1, 1)
            q_group(6, 0)
            q_group(7, 1)
            q_tail(7, T - 1)

            def o_lo_part(m, pair):
                dve.wait_ge(o_hi, m + 1)
                nc.vector.scalar_tensor_tensor(q_lo[:, bass.ds(m * 512, 512)], bank[6 + pair][:],
                                               O_SCALE / P_SCALE, q_hi[:, bass.ds(m * 512, 512)], ALU.mult,
                                               ALU.subtract).then_inc(o_lo, 1)

            def attend(g, u):
                k = 8 * g + u
                first, last = isinstance(g, int) and g == 0, isinstance(g, int) and g == G
                if u == 0 and not (isinstance(g, int) and g < 2):
                    o_lo_part(2 * g - 3, 1)
                if u == 4 and not first:
                    o_lo_part(2 * g - 2, 0)
                if not (first and u < 2) and not (last and u > 1):
                    wait(dve, exped, k - 1)
                if not last:
                    dve.wait_ge(scored, k + 1)
                    wait(dve, p_turned, k - 3)
                    if first and u == 0:
                        dve.wait_ge(mask_loaded, 16)
                if not (first and u < 2) and not (last and u > 1):
                    v = (u + 2) % 4
                    nc.vector.reciprocal(inv_p[:, v:v + 1], psum_p[:, v:v + 1]).then_inc(inverted, 1)
                if not last:
                    nc.vector.tensor_tensor_reduce(xn[:, u % 4, :], bank[u % 4][:], mask[:, u % 2, :], -1.0, BIG,
                                                   ALU.add, ALU.min, nmax[:, u % 4:u % 4 + 1]).then_inc(masked, 1)
                if not (first and u < 3) and not (last and u >= 3):
                    w = (u + 5) % 8
                    pair, h, qt = w // 4, w // 2 % 2, w % 2
                    dve.wait_ge(p_hi, k - 2)
                    cols = slice(h * S + qt * P, h * S + (qt + 1) * P)
                    nc.vector.scalar_tensor_tensor(pT_lo[pair][:, :, cols],
                                                   bank[4 + w % 2][:].rearrange("p (k n) -> p k n", k=KT), P_SCALE,
                                                   pT_hi[pair][:, :, cols], ALU.mult,
                                                   ALU.subtract).then_inc(p_lo, 1)

            for u in range(8):
                attend(0, u)
            for u in range(8):
                attend(1, u)
            with dve.Fori(2, G) as g:
                for u in range(8):
                    attend(g, u)
            for u in range(8):
                attend(G, u)
            o_lo_part(2 * G - 1, 1)

            def o_cut(kv, par):
                cut(CUT_O + kv, par, chunks(wo_hi[par]), chunks(wo_lo[par]), W_SCALE)

            def e_cut(j, par):
                cut(CUT_E + j, par, chunks(wq_hi[par]), chunks(wq_lo[par]), W_SCALE)

            with dve.Fori(0, KV // 2) as m:
                o_cut(2 * m, 0)
                o_cut(2 * m + 1, 1)
            e_cut(0, 0)
            e_cut(1, 1)
            dve.wait_ge(cst_ready, 2)
            then(nc.vector.scalar_tensor_tensor(gate_lo[:], small[:, 24:56], W_SCALE, gate_hi[:], ALU.mult,
                                                ALU.subtract))
            residual(3, o_out, 1, bank[0:4], 1.0 / (W_SCALE * O_SCALE))
            turned_x(3)

            gate_bias, index = small[:, 8:16], small[:, 16:24]
            for t in range(T):
                dve.wait_ge(logits, T)
                then(nc.vector.scalar_tensor_tensor(lg[:, t, :], bank[0][:, t * EXPERTS:(t + 1) * EXPERTS],
                                                    1.0 / W_SCALE, gate_bias, ALU.mult, ALU.add))
            then(nc.vector.tensor_reduce(top[:], lg[:], AX.X, ALU.max))
            for t in range(T):
                then(nc.vector.tensor_scalar(cand[:, t, :], lg[:, t, :], top[:, t:t + 1], float(EXPERTS),
                                             ALU.is_lt, ALU.mult))
                then(nc.vector.tensor_tensor(cand[:, t, :], cand[:, t, :], index, ALU.add))
            then(nc.vector.tensor_reduce(first[:], cand[:], AX.X, ALU.min))
            for t in range(T):
                then(nc.vector.tensor_scalar(onehot[:, t, :], index, first[:, t:t + 1], None, ALU.is_equal))
                nc.vector.tensor_scalar(onehot_s[:, t, :], onehot[:, t, :], 1.0 / W_SCALE, None,
                                        ALU.mult).then_inc(chosen, 1)
            bias_hl = [wo_hi[0][0:EXPERTS, 0:D], wo_lo[0][0:EXPERTS, 0:D]]
            dve.wait_ge(bias_loaded, 16)
            then(nc.vector.tensor_scalar(bias_hl[0], bias_f[:], W_SCALE, None, ALU.mult))
            then(nc.vector.scalar_tensor_tensor(bias_hl[1], bias_f[:], W_SCALE, bias_hl[0], ALU.mult, ALU.subtract))
            dve.wait_ge(choice_turned, 1)
            nc.vector.tensor_copy(oneT, bank[1][0:EXPERTS, :].rearrange("e (t n) -> e t n", t=T)).then_inc(
                choice_T, 1)
            for t in range(T):
                dve.wait_ge(bias_out, t + 1)
                nc.vector.scalar_tensor_tensor(x_res[:, t, :], bank[2 + t % 2][:], 1.0 / W_SCALE,
                                               x_res[:, t, :], ALU.mult, ALU.add).then_inc(bias_added, 1)
            dve.wait_ge(bias_added, T)

            def expert(j):
                for t in range(T):
                    dve.wait_ge(e_unit, T * j + t + 1)
                    wait(dve, e_added, T * (j - 1) + t + 1)
                    nc.vector.scalar_tensor_tensor(x_res[:, t, :], bank[4 + t][:], onehot_s[:, t, bass.ds(j, 1)],
                                                   x_res[:, t, :], ALU.mult, ALU.add).then_inc(e_added, 1)

            expert(0)
            expert(1)
            with dve.Fori(1, EXPERTS // 2) as m:
                e_cut(2 * m, 0)
                expert(2 * m)
                e_cut(2 * m + 1, 1)
                expert(2 * m + 1)

        @block.tensor
        def _(pe):
            def three(out_ap, pairs, start=True, stop=True):
                n = 0
                for (w_hi, w_lo), (m_hi, m_lo) in pairs:
                    for w, m in ((w_hi, m_hi), (w_hi, m_lo), (w_lo, m_hi)):
                        mm = nc.tensor.matmul(out_ap, w, m, start=start and n == 0,
                                              stop=stop and n == 3 * len(pairs) - 1, skip_group_check=True)
                        n += 1
                return mm

            def turn_x(stage):
                for t in range(T):
                    pe.wait_ge(xn_ready, T * (stage - 1) + t + 1)
                    for c in range(C):
                        mm = nc.tensor.transpose(bank[4 + t][:, c * P:(c + 1) * P], xn[:, t, c * P:(c + 1) * P],
                                                 ident[:])
                    mm.then_inc(xT_turned, 1)

            def norm_turn(n, par, unit):
                pe.wait_ge(n_unit, n + 1)
                wait(pe, n_lo, n - 1)
                for h in range(REP):
                    mm = nc.tensor.transpose(bank[2 + par][:, h * HD:(h + 1) * HD],
                                             unit[:, par, h * HD:(h + 1) * HD], ident[:])
                mm.then_inc(n_turned, 1)

            def kv_project(i, par, half, w_hi, w_lo):
                tile = bass.ds(i * P, P)
                return three(bank[par][:], [((cT_hi[:, c, tile], cT_lo[:, c, tile]),
                                             (w_hi[:, half, c * 512:(c + 1) * 512],
                                              w_lo[:, half, c * 512:(c + 1) * 512])) for c in range(C)])

            def k_step(half, i, par):
                n = 8 * half + i
                if isinstance(i, int) and i == 0:
                    pe.wait_ge(cut_lo, 2 if half == 0 else 4)
                wait(pe, n_unit, n - 1)
                kv_project(i, par, half, wk_hi, wk_lo).then_inc(n_proj, 1)
                if not (isinstance(n, int) and n == 0):
                    norm_turn(n - 1, 1 - par, k_unit)

            pe.wait_ge(const_in, 48)
            k_units(pe, k_step, None, lambda: pe.wait_ge(cut_lo, 3))
            norm_turn(15, 1, k_unit)

            for t in range(T):
                pe.wait_ge(q1_ready, t + 1)
                wait(pe, q1T_ready, t - 1)
                for c in range(KT):
                    mm = nc.tensor.transpose(bank[4 + t % 2][:].bitcast(BF16)[:, c * P:(c + 1) * P],
                                             q1[:, t, c * P:(c + 1) * P], ident_b[:])
                mm.then_inc(q1_turned, 1)
            pe.wait_ge(q1T_ready, T)
            pe.wait_ge(q2_ready, B)
            for b in range(B):
                for c in range(KT):
                    mm = nc.tensor.matmul(bank[4 + b][:], ones_b[:], q2[:, b, c, :], start=(c == 0),
                                          stop=(c == KT - 1))
                mm.then_inc(col_sum, 1)
            for t in range(T):
                wait(pe, cross_used, t - 1)
                for c in range(KT):
                    mm = nc.tensor.matmul(bank[6 + t % 2][:], q1T[:, c, t * P:(t + 1) * P], q2[:, t // QT, c, :],
                                          start=(c == 0), stop=(c == KT - 1))
                mm.then_inc(cross_done, 1)

            def v_step(half, i, par):
                n = 8 * half + i
                wait(pe, v_cut_lo, n - 1)
                kv_project(i, par, half, wv_hi, wv_lo).then_inc(v_proj, 1)

            pe.wait_ge(n_unit, 16)
            pe.wait_ge(cut_lo, CUT_V + 1)
            v_step(0, 0, 0)
            v_step(0, 1, 1)
            with pe.Fori(1, 4) as m:
                v_step(0, 2 * m, 0)
                v_step(0, 2 * m + 1, 1)
            turn_x(1)
            pe.wait_ge(cut_lo, CUT_V + 2)
            with pe.Fori(0, 4) as m:
                v_step(1, 2 * m, 0)
                v_step(1, 2 * m + 1, 1)

            def ffn_ab(j, par):
                pe.wait_ge(w13_cut_lo, j + 1)
                wait(pe, h_ready, j - 1)
                for mat in range(2):
                    mm = three(bank[2 * par + mat][:],
                               [((w13_hi[par][:, (4 * mat + c) * P:(4 * mat + c + 1) * P],
                                  w13_lo[par][:, (4 * mat + c) * P:(4 * mat + c + 1) * P]),
                                 (xT_hi[:, c, :], xT_lo[:, c, :])) for c in range(C)])
                mm.then_inc(ab_done, 1)

            def ffn_down(j, par, start=False, stop=False):
                pe.wait_ge(h_cut_lo, j + 1)
                pe.wait_ge(w2_cut_lo, j + 1)
                for t in range(T):
                    tok = slice(t * P, (t + 1) * P)
                    mm = three(bank[4 + t][:], [((h_hi[par][:, tok], h_lo[par][:, tok]), (w2_hi[par], w2_lo[par]))],
                               start=start, stop=stop)
                    if stop:
                        mm.then_inc(ffn_out, 1)
                if not stop:
                    mm.then_inc(ffn_tile, 1)

            pe.wait_ge(xT_cut_lo, T)
            pe.wait_ge(v_cut_lo, 16)
            ffn_ab(0, 0)
            ffn_ab(1, 1)
            ffn_down(0, 0, start=True)
            with pe.Fori(1, HT // 2) as m:
                ffn_ab(2 * m, 0)
                ffn_down(2 * m - 1, 1)
                ffn_ab(2 * m + 1, 1)
                ffn_down(2 * m, 0)
            ffn_ab(HT - 1, 0)
            ffn_down(HT - 2, 1)
            ffn_down(HT - 1, 0, stop=True)

            turn_x(2)
            pe.wait_ge(xT_cut_lo, 2 * T)

            def q_group(kv, par):
                pe.wait_ge(cut_lo, CUT_Q + kv + 1)
                for t in range(T):
                    n = 16 + 4 * kv + t
                    wait(pe, n_unit, n - 1)
                    tok = slice(t * P, (t + 1) * P)
                    three(bank[t % 2][:], [((xT_hi[:, c, tok], xT_lo[:, c, tok]),
                                            (wq_hi[par][:, c * 512:(c + 1) * 512],
                                             wq_lo[par][:, c * 512:(c + 1) * 512])) for c in range(C)]
                          ).then_inc(n_proj, 1)
                    if not (isinstance(n, int) and n == 16):
                        norm_turn(n - 1, 1 - t % 2, xn[:, 0:2, :])

            q_group(0, 0)
            q_group(1, 1)
            with pe.Fori(1, KV // 2) as m:
                q_group(2 * m, 0)
                q_group(2 * m + 1, 1)
            norm_turn(16 + 4 * KV - 1, 1, xn[:, 0:2, :])
            pe.wait_ge(n_lo, 16 + 4 * KV)

            def attend(g, u):
                k = 8 * g + u
                first, last = isinstance(g, int) and g == 0, isinstance(g, int) and g == G
                if not last:
                    wait(pe, masked, k - 3)
                    h, qt = u // 2, u % 2
                    off = g * (REP * S) + h * S + qt * P
                    three(bank[u % 4][:], [((q_hi[:, bass.ds(off, P)], q_lo[:, bass.ds(off, P)]),
                                            (kT_flat[0][:, bass.ds(g * S2, S2)],
                                             kT_flat[1][:, bass.ds(g * S2, S2)]))]).then_inc(scored, 1)
                if not (first and u < 3) and not (last and u >= 3):
                    w = (u + 5) % 8
                    pe.wait_ge(p_ready, k - 2)
                    wait(pe, p_lo, k - 4)
                    for c in range(KT):
                        mm = nc.tensor.transpose(bank[4 + w % 2][:, c * P:(c + 1) * P],
                                                 xn[:, w % 4, c * P:(c + 1) * P], ident[:])
                    mm.then_inc(p_turned, 1)
                if not first:
                    pair, c = u // 4, u % 4
                    if c == 0:
                        pe.wait_ge(p_lo, 8 * g - 4 if pair == 0 else 8 * g)
                        wait(pe, o_lo, 2 * g - 3 + pair)
                    off = (g - 1) * S2 + c * P
                    mm = three(bank[6 + pair][:], [((v_flat[0][:, bass.ds(off, P)], v_flat[1][:, bass.ds(off, P)]),
                                                    (pT_hi[pair][:, c, :], pT_lo[pair][:, c, :]))],
                               start=(c == 0), stop=(c == KT - 1))
                    if c == KT - 1:
                        mm.then_inc(pv_done, 1)

            for u in range(8):
                attend(0, u)
            for u in range(8):
                attend(1, u)
            with pe.Fori(2, G) as g:
                for u in range(8):
                    attend(g, u)
            for u in range(8):
                attend(G, u)

            def o_step(kv, par, start=False, stop=False):
                pe.wait_ge(cut_lo, CUT_O + kv + 1)
                for t in range(T):
                    pairs = []
                    for h in range(REP):
                        off = kv * (B * REP * S) + (t // QT) * (REP * S) + h * S + (t % QT) * P
                        pairs.append(((q_hi[:, bass.ds(off, P)], q_lo[:, bass.ds(off, P)]),
                                      (wo_hi[par][:, h * D:(h + 1) * D], wo_lo[par][:, h * D:(h + 1) * D])))
                    mm = three(bank[t][:], pairs, start=start, stop=stop)
                    if stop:
                        mm.then_inc(o_out, 1)
                if not stop:
                    mm.then_inc(o_group, 1)

            pe.wait_ge(masked, 8 * G)
            pe.wait_ge(o_lo, 2 * G)
            o_step(0, 0, start=True)
            o_step(1, 1)
            with pe.Fori(1, KV // 2 - 1) as m:
                o_step(2 * m, 0)
                o_step(2 * m + 1, 1)
            o_step(KV - 2, 0)
            o_step(KV - 1, 1, stop=True)

            turn_x(3)
            for t in range(T):
                pe.wait_ge(xT_cut_lo, 3 * T + t + 1 - T)
                tok = slice(t * P, (t + 1) * P)
                three(bank[0][:, t * EXPERTS:(t + 1) * EXPERTS],
                      [((xT_hi[:, c, tok], xT_lo[:, c, tok]),
                        (gate_hi[:, c * EXPERTS:(c + 1) * EXPERTS], gate_lo[:, c * EXPERTS:(c + 1) * EXPERTS]))
                       for c in range(C)]).then_inc(logits, 1)

            def expert(j, par):
                pe.wait_ge(cut_lo, CUT_E + j + 1)
                for t in range(T):
                    wait(pe, e_added, T * (j - 1) + t + 1)
                    tok = slice(t * P, (t + 1) * P)
                    three(bank[4 + t][:], [((xT_hi[:, c, tok], xT_lo[:, c, tok]),
                                            (wq_hi[par][:, c * 512:(c + 1) * 512],
                                             wq_lo[par][:, c * 512:(c + 1) * 512])) for c in range(C)]
                          ).then_inc(e_unit, 1)

            expert(0, 0)
            pe.wait_ge(chosen, T)
            for t in range(T):
                mm = nc.tensor.transpose(bank[1][0:EXPERTS, t * P:(t + 1) * P], onehot[:, t, :], ident[:])
            mm.then_inc(choice_turned, 1)
            pe.wait_ge(choice_T, 1)
            for t in range(T):
                wait(pe, bias_added, t - 1)
                for hl in range(2):
                    part = (wo_hi if hl == 0 else wo_lo)[0][0:EXPERTS, 0:D]
                    mm = nc.tensor.matmul(bank[2 + t % 2][:], oneT[:, t, :], part, start=(hl == 0), stop=(hl == 1))
                mm.then_inc(bias_out, 1)
            expert(1, 1)
            with pe.Fori(1, EXPERTS // 2) as m:
                expert(2 * m, 0)
                expert(2 * m + 1, 1)


def hidden_tiles(a):
    import numpy as np

    pad = np.zeros((HT * P - a.shape[0],) + a.shape[1:], a.dtype)
    return np.concatenate([a, pad]).reshape((HT, P) + a.shape[1:])


def kernel(**inputs):
    import numpy as np
    import concourse.bacc as bacc
    from concourse import mybir as mb
    from concourse.bass_utils import run_bass_kernel_spmd as run

    a = {k: np.asarray(v) for k, v in inputs.items()}
    x, context = a["x"], a["ctx_4096"]

    order = np.arange(D).reshape(2, 2, 2, GROUP).transpose(0, 2, 1, 3).reshape(-1)

    def item(rows):
        return rows.reshape(C, P, 512).transpose(1, 0, 2).reshape(P, ITEM)

    wk, wv = a["L1_xattn_k_proj_w"].T, a["L1_xattn_v_proj_w"].T
    wq, wo = a["L1_xattn_q_proj_w"].T[order], a["L1_xattn_o_proj_w"].T[:, order]
    stream = [item(context[0].T), item(wk[:, 0:512]), item(context[1].T), item(wk[:, 512:1024]),
              item(context[0][order][:, order]), item(context[1][order][:, order]), item(wv[:, 0:512]), item(wv[:, 512:1024])]
    stream += [item(wq[:, 512 * g:512 * g + 512]) for g in range(KV)]
    stream += [item(wo[512 * g:512 * g + 512]) for g in range(KV)]
    stream += [item(a["L1_ffn_expert_w"][j].T[order][:, order]) for j in range(EXPERTS)]

    def words(w):
        w = w.reshape(HIDDEN, 2, 2, GROUP)
        return hidden_tiles(w).transpose(0, 3, 4, 2, 1).reshape(HT, P, 2 * P)

    def scales(s):
        s = s.reshape(HIDDEN, 2, 2, 2)
        s = np.repeat(hidden_tiles(s).transpose(0, 3, 2, 4, 1), GROUP, axis=1)
        return s.reshape(HT, P, 4 * P)

    w2 = a["L0_ffn_w2"]
    w2 = hidden_tiles(np.concatenate([w2, w2], axis=1).reshape(D, HIDDEN).T[:, order])
    w2 = w2.reshape(HT, P, P, 4).transpose(0, 1, 3, 2).reshape(HT, P, D)
    s2 = hidden_tiles(np.repeat(a["L0_ffn_s2"], GROUP).reshape(D, HIDDEN).T[:, order])
    ffn_int = np.concatenate([words(a["L0_ffn_w1"]), words(a["L0_ffn_w3"]), w2], axis=2)
    ffn_scale = np.concatenate([scales(a["L0_ffn_s1"]), scales(a["L0_ffn_s3"]), s2], axis=2)
    part = np.arange(P)
    shift = np.stack([np.where((96 * r + part) % P < GROUP, 24, 28) for r in range(4)]
                     + [np.full(P, 24), np.full(P, 28)], axis=1).astype(np.int32)

    small = np.zeros((P, 56), np.float32)
    for i, name in enumerate(["x1_scale", "x1_zp", "x2_scale", "x2_zp"]):
        small[:, i] = a["L0_xattn_" + name][0]
    small[:, 4] = a["L1_xattn_q_norm_w"]
    small[:, 5] = a["L1_xattn_k_norm_w"]
    small[:, 8:16] = a["L1_ffn_gate_b"]
    small[:, 16:24] = np.arange(EXPERTS)
    small[:, 24:56] = a["L1_ffn_gate_w"].T[order].reshape(C, P, EXPERTS).transpose(1, 0, 2).reshape(P, -1)

    arrays = {"x": x.reshape(B * S, D)[:, order], "stream": np.stack(stream), "ffn_int": ffn_int, "ffn_scale": ffn_scale,
              "mask": a["mask_1x1xSxS2_ff0"].reshape(S, S2), "small": small, "shift": shift,
              "ident": np.eye(P, dtype=np.float32), "bias": a["L1_ffn_expert_b"][:, order]}
    arrays = {k: np.ascontiguousarray(v) for k, v in arrays.items()}
    nc = bacc.Bacc("TRN2", target_bir_lowering=False, num_devices=1)
    args = [nc.dram_tensor(f"in_{k}", v.shape, mb.dt.from_np(v.dtype), kind="ExternalInput").ap()
            for k, v in arrays.items()]
    out = nc.dram_tensor("out", (B * S, D), mb.dt.float32, kind="ExternalOutput").ap()
    kernel_program(nc, *args, out)
    r = run(nc, [{f"in_{k}": v for k, v in arrays.items()}], core_ids=[0])
    return np.ascontiguousarray(r.results[0]["out"][:, np.argsort(order)]).reshape(B, S, D)
```

```python
from contextlib import ExitStack

import concourse.bass as bass
from concourse import mybir

ALU = mybir.AluOpType
ACT = mybir.ActivationFunctionType
AX = mybir.AxisListType
F32 = mybir.dt.float32
F16 = mybir.dt.float16
BF16 = mybir.dt.bfloat16
I32 = mybir.dt.int32

P = 128
B, S, S2, D = 2, 256, 512, 512
T = B * S // P
C = D // P
KT = S2 // P
HEADS, KV, HD = 32, 8, 128
REP = HEADS // KV
G = KV * B
QT = S // P
GROUP = 64
HIDDEN = 1376
HT = -(-HIDDEN // P)
EXPERTS = 8
EPS = 1e-5

Q_BANKS = [0, 1, 4, 5]
Q_PIECES = [[0, 1], [2], [3], []]
W_SCALE = 64.0
P_SCALE = 1024.0
O_SCALE = 16.0
ROUND = 12582912.0
MID = 128.0
BIG = 3.0e38

CTX_T, WK, NAT, WV, WQ, WO, WE = [0, 2], [1, 3], [4, 5], [6, 7], 8, 16, 24
ITEMS = 32
ITEM = 2048
CUT_V, CUT_Q, CUT_O, CUT_E = 4, 6, 14, 22
FFN_INT, FFN_SC = 1024, 1536


def kernel_program(nc, x_in, stream, ffn_int, ffn_scale, mask_in, small_in, shift_in, ident_in, bias_in, out):
    with ExitStack() as ctx:
        def sem(name):
            return ctx.enter_context(nc.semaphore(name))

        arena = ctx.enter_context(nc.sbuf_tensor("arena", [P, 204 * 256], F32))

        def at(kib, n, dtype):
            words = n if dtype in (F32, I32) else n // 2
            a = arena[:, kib * 256:kib * 256 + words]
            return a if dtype == F32 else a.bitcast(dtype)

        x_res = at(0, T * D, F32).rearrange("p (t d) -> p t d", t=T)
        xn = at(8, T * D, F32).rearrange("p (t d) -> p t d", t=T)
        xT_hi = at(16, C * 512, F16).rearrange("p (c n) -> p c n", c=C)
        xT_lo = at(20, C * 512, F16).rearrange("p (c n) -> p c n", c=C)
        kT_hi = at(24, KV * B * S2, F16).rearrange("p (h n) -> p h n", h=KV)
        kT_lo = at(40, KV * B * S2, F16).rearrange("p (h n) -> p h n", h=KV)
        kT_flat = [at(24, KV * B * S2, F16), at(40, KV * B * S2, F16)]
        v_hi = at(56, KV * B * S2, F16).rearrange("p (h n) -> p h n", h=KV)
        v_lo = at(72, KV * B * S2, F16).rearrange("p (h n) -> p h n", h=KV)
        v_flat = [at(56, KV * B * S2, F16), at(72, KV * B * S2, F16)]
        ring = at(88, 2 * ITEM, F32).rearrange("p (s n) -> p s n", s=2)
        raw_int = [at(104 + 10 * s, FFN_INT, I32) for s in range(2)]
        raw_sc = [at(108 + 10 * s, FFN_SC, F32) for s in range(2)]
        wo_hi = [at(104 + 8 * s, ITEM, F16) for s in range(2)]
        wo_lo = [at(108 + 8 * s, ITEM, F16) for s in range(2)]
        mask = at(120, QT * S2, F32).rearrange("p (q n) -> p q n", q=QT)
        cT_hi = at(124, C * B * S2, F16).rearrange("p (c n) -> p c n", c=C)
        cT_lo = at(132, C * B * S2, F16).rearrange("p (c n) -> p c n", c=C)
        wv_hi = at(140, 2 * ITEM, F16).rearrange("p (h n) -> p h n", h=2)
        wv_lo = at(148, 2 * ITEM, F16).rearrange("p (h n) -> p h n", h=2)
        wk_hi = at(156, 2 * ITEM, F16).rearrange("p (h n) -> p h n", h=2)
        wk_lo = at(164, 2 * ITEM, F16).rearrange("p (h n) -> p h n", h=2)
        q2 = at(172, B * KT * D, BF16).rearrange("p (b k n) -> p b k n", b=B, k=KT)
        q1T = at(180, KT * 512, BF16).rearrange("p (k n) -> p k n", k=KT)
        k_unit = at(184, 2 * 512, F32).rearrange("p (s n) -> p s n", s=2)
        k_square = at(188, 2 * 512, F32).rearrange("p (s n) -> p s n", s=2)
        q1 = at(192, T * D, BF16).rearrange("p (t n) -> p t n", t=T)
        col_term = at(196, B * D, F32).rearrange("p (b n) -> p b n", b=B)
        cross = at(200, 2 * D, F32).rearrange("p (s n) -> p s n", s=2)
        nib = at(156, FFN_SC, I32)
        w13_f = [at(162, 1024, F32), at(200, 1024, F32)]
        w2_f = [at(166 + 2 * s, 512, F32) for s in range(2)]
        w13_hi = [at(170 + 4 * s, 1024, F16) for s in range(2)]
        w13_lo = [at(172 + 4 * s, 1024, F16) for s in range(2)]
        w2_hi = [at(178 + 2 * s, 512, F16) for s in range(2)]
        w2_lo = [at(179 + 2 * s, 512, F16) for s in range(2)]
        h_hi = [at(182 + 2 * s, 512, F16) for s in range(2)]
        h_lo = [at(183 + 2 * s, 512, F16) for s in range(2)]
        q_hi = at(124, G * REP * S, F16)
        q_lo = at(156, G * REP * S, F16)
        wq_hi = [at(188 + 8 * s, ITEM, F16) for s in range(2)]
        wq_lo = [at(192 + 8 * s, ITEM, F16) for s in range(2)]
        pT_hi = [at(188 + 8 * s, KT * 512, F16).rearrange("p (k n) -> p k n", k=KT) for s in range(2)]
        pT_lo = [at(192 + 8 * s, KT * 512, F16).rearrange("p (k n) -> p k n", k=KT) for s in range(2)]

        bias_f = at(24, D, F32)[0:EXPERTS, :]
        oneT = at(26, T * P, F16)[0:EXPERTS, :].rearrange("e (t n) -> e t n", t=T)

        def sb(name, shape, dtype):
            return ctx.enter_context(nc.sbuf_tensor(name, shape, dtype))

        ident = sb("ident", [P, P], F32)
        ident_b = sb("ident_b", [P, P], BF16)
        ones_b = sb("ones_b", [P, P], BF16)
        small = sb("small", [P, 56], F32)
        shift = sb("shift", [P, 6], I32)
        eps = sb("eps", [P, 1], F32)
        cst = sb("cst", [P, 12], F32)
        gate_hi = sb("gate_hi", [P, C * EXPERTS], F16)
        gate_lo = sb("gate_lo", [P, C * EXPERTS], F16)
        ln_st = sb("ln_st", [P, T, 6], F32)
        ln_mv = sb("ln_mv", [P, T, 2], F32)
        ln_sd = sb("ln_sd", [P, T], F32)
        ln_r = sb("ln_r", [P, T], F32)
        row_sum = sb("row_sum", [P, T], F32)
        row_term = sb("row_term", [P, T], F32)
        sumsq = sb("sumsq", [P, 2, REP], F32)
        rms = sb("rms", [P, 2, REP], F32)
        inv_rms = sb("inv_rms", [P, 2, REP], F32)
        nmax = sb("nmax", [P, 4], F32)
        psum_p = sb("psum_p", [P, 4], F32)
        inv_p = sb("inv_p", [P, 4], F32)
        lg = sb("lg", [P, T, EXPERTS], F32)
        top = sb("top", [P, T], F32)
        cand = sb("cand", [P, T, EXPERTS], F32)
        first = sb("first", [P, T], F32)
        onehot = sb("onehot", [P, T, EXPERTS], F32)
        onehot_s = sb("onehot_s", [P, T, EXPERTS], F32)

        bank = [ctx.enter_context(nc.psum_tensor(f"bank{i}", [P, 512], F32)) for i in range(8)]

        const_in = sem("const_in")
        x_loaded = sem("x_loaded")
        mask_loaded = sem("mask_loaded")
        bias_loaded = sem("bias_loaded")
        ring_in = [sem("ring_in0"), sem("ring_in1")]
        ffn_in = [sem("ffn_in0"), sem("ffn_in1")]
        out_stored = sem("out_stored")
        cst_ready = sem("cst_ready")
        dve_step = sem("dve_step")
        pool_step = sem("pool_step")
        cut_hi = sem("cut_hi")
        cut_lo = sem("cut_lo")
        ln_stats = sem("ln_stats")
        ln_std = sem("ln_std")
        ln_rstd = sem("ln_rstd")
        xn_ready = sem("xn_ready")
        xT_turned = sem("xT_turned")
        xT_cut_hi = sem("xT_cut_hi")
        xT_cut_lo = sem("xT_cut_lo")
        x_scaled = sem("x_scaled")
        nat_scaled = sem("nat_scaled")
        q1_ready = sem("q1_ready")
        q2_ready = sem("q2_ready")
        q1_turned = sem("q1_turned")
        q1T_ready = sem("q1T_ready")
        col_sum = sem("col_sum")
        cross_done = sem("cross_done")
        cross_used = sem("cross_used")
        n_proj = sem("n_proj")
        n_square = sem("n_square")
        n_sumsq = sem("n_sumsq")
        n_rms = sem("n_rms")
        n_inv = sem("n_inv")
        n_unit = sem("n_unit")
        n_turned = sem("n_turned")
        n_hi = sem("n_hi")
        n_lo = sem("n_lo")
        v_proj = sem("v_proj")
        v_cut_hi = sem("v_cut_hi")
        v_cut_lo = sem("v_cut_lo")
        w13_nibbles = sem("w13_nibbles")
        w2_nibbles = sem("w2_nibbles")
        w13_float = sem("w13_float")
        w2_float = sem("w2_float")
        w13_scaled = sem("w13_scaled")
        w2_scaled = sem("w2_scaled")
        w13_cut_hi = sem("w13_cut_hi")
        w13_cut_lo = sem("w13_cut_lo")
        w2_cut_hi = sem("w2_cut_hi")
        w2_cut_lo = sem("w2_cut_lo")
        ab_done = sem("ab_done")
        silu_a = sem("silu_a")
        h_ready = sem("h_ready")
        h_cut_hi = sem("h_cut_hi")
        h_cut_lo = sem("h_cut_lo")
        ffn_tile = sem("ffn_tile")
        ffn_out = sem("ffn_out")
        scored = sem("scored")
        masked = sem("masked")
        exped = sem("exped")
        inverted = sem("inverted")
        p_ready = sem("p_ready")
        p_turned = sem("p_turned")
        p_hi = sem("p_hi")
        p_lo = sem("p_lo")
        pv_done = sem("pv_done")
        o_hi = sem("o_hi")
        o_lo = sem("o_lo")
        o_group = sem("o_group")
        o_out = sem("o_out")
        logits = sem("logits")
        chosen = sem("chosen")
        choice_turned = sem("choice_turned")
        choice_T = sem("choice_T")
        bias_out = sem("bias_out")
        bias_added = sem("bias_added")
        e_unit = sem("e_unit")
        e_added = sem("e_added")

        def wait(eng, s, count):
            if not (isinstance(count, int) and count <= 0):
                eng.wait_ge(s, count)

        def item_of(cut):
            return cut if cut < CUT_V else cut + 2

        def chunks(a):
            return a.rearrange("p (c n) -> p c n", c=C)

        def cut_target(cut, par):
            if cut in (0, 2):
                b = cut // 2
                return cT_hi[:, :, b * S2:(b + 1) * S2], cT_lo[:, :, b * S2:(b + 1) * S2]
            if cut in (1, 3):
                return chunks(wk_hi[:, cut // 2, :]), chunks(wk_lo[:, cut // 2, :])
            return chunks(wv_hi[:, cut - CUT_V, :]), chunks(wv_lo[:, cut - CUT_V, :])

        def k_units(eng, step, after_first=None, after_third=None):
            for half in range(2):
                step(half, 0, 0)
                done = 0
                if half == 0:
                    if after_first:
                        after_first()
                    step(0, 1, 1)
                    step(0, 2, 0)
                    done = 1
                    if after_third:
                        after_third()
                with eng.Fori(done, 3) as m:
                    step(half, 2 * m + 1, 1)
                    step(half, 2 * m + 2, 0)
                step(half, 7, 1)

        block = ctx.enter_context(nc.Block())

        @block.sync
        def _(sp):

            def load_item(r, slot, count):
                if isinstance(r, int) and r < 2:
                    pass
                elif isinstance(r, int) and r < 6:
                    sp.wait_ge(cut_lo, C * (r - 1))
                elif isinstance(r, int) and r < 8:
                    sp.wait_ge(q2_ready, r - 5)
                else:
                    sp.wait_ge(cut_lo, C * (count))
                sp.dma_start(ring[:, slot, :], stream[r]).then_inc(ring_in[slot], 16)

            def load_ffn(j, par):
                wait(sp, w2_scaled, j - 1)
                sp.dma_start(raw_int[par], ffn_int[j]).then_inc(ffn_in[par], 16)
                sp.dma_start(raw_sc[par], ffn_scale[j]).then_inc(ffn_in[par], 16)

            load_item(0, 0, 0)
            load_item(1, 1, 0)
            sp.dma_start(x_res, x_in.rearrange("(t p) d -> p t d", p=P)).then_inc(x_loaded, 16)
            sp.dma_start(small[:], small_in).then_inc(const_in, 16)
            sp.dma_start(shift[:], shift_in).then_inc(const_in, 16)
            sp.dma_start(ident[:], ident_in).then_inc(const_in, 16)
            load_item(2, 0, 0)
            load_item(3, 1, 0)
            load_ffn(0, 0)
            load_item(4, 0, 0)
            load_item(5, 1, 0)
            load_ffn(1, 1)
            load_item(6, 0, 0)
            load_item(7, 1, 0)
            load_item(8, 0, 5)
            load_item(9, 1, 6)
            with sp.Fori(1, HT // 2) as m:
                load_ffn(2 * m, 0)
                load_ffn(2 * m + 1, 1)
            load_ffn(HT - 1, 0)
            sp.wait_ge(w2_scaled, HT - 1)
            sp.dma_start(mask, mask_in.rearrange("(q p) n -> p q n", p=P)).then_inc(mask_loaded, 16)
            with sp.Fori(5, WE // 2) as m:
                load_item(2 * m, 0, 2 * m - 3)
                load_item(2 * m + 1, 1, 2 * m - 2)
            sp.wait_ge(scored, 8 * G)
            sp.dma_start(bias_f, bias_in).then_inc(bias_loaded, 16)
            with sp.Fori(WE // 2, ITEMS // 2) as m:
                load_item(2 * m, 0, 2 * m - 3)
                load_item(2 * m + 1, 1, 2 * m - 2)
            for t in range(T):
                sp.wait_ge(e_added, T * (EXPERTS - 1) + t + 1)
                sp.dma_start(out[t * P:(t + 1) * P, :], x_res[:, t, :]).then_inc(out_stored, 16)
            sp.wait_ge(out_stored, 16 * T)

        @block.gpsimd
        def _(pool):
            steps = [0]

            def then(ins):
                steps[0] += 1
                ins.then_inc(pool_step, 1)
                pool.wait_ge(pool_step, steps[0])

            pool.wait_ge(cst_ready, 1)
            pool.wait_ge(ln_rstd, 1)
            for t in range(T):
                then(nc.gpsimd.tensor_scalar(xn[:, t, :], x_res[:, t, :], ln_mv[:, t, 0:1], ln_r[:, t:t + 1],
                                             ALU.subtract, ALU.mult))
                then(nc.gpsimd.tensor_scalar(xn[:, t, :], xn[:, t, :], cst[:, 0:1], small[:, 1:2],
                                             ALU.mult, ALU.add))
                nc.gpsimd.tensor_scalar(xn[:, t, :], xn[:, t, :], 255.0, 0.0, ALU.min, ALU.max).then_inc(x_scaled, 1)
            for b in range(B):
                pool.wait_ge(ring_in[NAT[b] % 2], 16 * (NAT[b] // 2 + 1))
                raw = ring[:, NAT[b] % 2, :]
                then(nc.gpsimd.tensor_scalar(raw, raw, cst[:, 1:2], small[:, 3:4], ALU.mult, ALU.add))
                nc.gpsimd.tensor_scalar(raw, raw, 255.0, 0.0, ALU.min, ALU.max).then_inc(nat_scaled, 1)

            def scale_w2(j, par):
                pool.wait_ge(w2_float, j + 1)
                nc.gpsimd.tensor_tensor(w2_f[par], w2_f[par], raw_sc[par][:, 1024:1536], ALU.mult).then_inc(w2_scaled, 1)

            def scale_w13(j, par):
                pool.wait_ge(ffn_in[par], 16 * (j + 2 - par))
                pool.wait_ge(w13_float, j + 1)
                nc.gpsimd.tensor_tensor(w13_f[par], w13_f[par], raw_sc[par][:, 0:1024], ALU.mult).then_inc(
                    w13_scaled, 1)

            scale_w13(0, 0)
            scale_w2(0, 0)
            scale_w13(1, 1)
            with pool.Fori(1, HT // 2) as m:
                scale_w2(2 * m - 1, 1)
                scale_w13(2 * m, 0)
                scale_w2(2 * m, 0)
                scale_w13(2 * m + 1, 1)
            scale_w2(HT - 2, 1)
            scale_w13(HT - 1, 0)
            scale_w2(HT - 1, 0)

            def normalise(k, u):
                pool.wait_ge(inverted, k + 1)
                nc.gpsimd.tensor_tensor(xn[:, u % 4, :], xn[:, u % 4, :],
                                        inv_p[:, u % 4:u % 4 + 1].broadcast_to([P, S2]),
                                        ALU.mult).then_inc(p_ready, 1)

            with pool.Fori(0, G) as g:
                for u in range(8):
                    normalise(8 * g + u, u)

        @block.scalar
        def _(act):
            def cut(c, par, target, scale, pieces=range(C)):
                r = item_of(c) if isinstance(c, int) else c + 2
                for p in pieces:
                    if p == 0:
                        act.wait_ge(ring_in[par], (r // 2 + 1) * 16 if isinstance(r, int) else 8 * (r - par) + 16)
                    nc.scalar.activation(target[:, p, :], chunks(ring[:, par, :])[:, p, :], ACT.Copy,
                                         scale=scale).then_inc(cut_hi, 1)

            def layer_norm_std(stage, t0, t1):
                act.wait_ge(ln_stats, T * stage + t1)
                nc.scalar.activation(ln_sd[:, t0:t1], ln_mv[:, t0:t1, 1], ACT.Sqrt, bias=eps[:]).then_inc(ln_std, 1)

            def turned_x(stage):
                for t in range(T):
                    act.wait_ge(xT_turned, T * (stage - 1) + t + 1)
                    nc.scalar.activation(xT_hi[:, :, t * P:(t + 1) * P],
                                         bank[4 + t][:].rearrange("p (c n) -> p c n", c=C),
                                         ACT.Copy).then_inc(xT_cut_hi, 1)

            def norm_square(n, par, square, source):
                act.wait_ge(n_proj, n + 1)
                wait(act, n_sumsq, n - 1)
                nc.scalar.activation(square[:, par, :], source[:], ACT.Square,
                                     scale=1.0 / W_SCALE).then_inc(n_square, 1)
                act.wait_ge(n_sumsq, n + 1)
                nc.scalar.activation(rms[:, par, :], sumsq[:, par, :], ACT.Sqrt, bias=eps[:],
                                     scale=1.0 / HD).then_inc(n_rms, 1)

            def norm_hi(n, par, target, weight):
                act.wait_ge(n_turned, n + 1)
                nc.scalar.activation(target, bank[2 + par][:].rearrange("p (h n) -> p h n", h=REP), ACT.Copy,
                                     scale=weight).then_inc(n_hi, 1)

            cut(0, 0, cut_target(0, 0)[0], 1.0)
            cut(1, 1, cut_target(1, 1)[0], W_SCALE)
            act.wait_ge(cst_ready, 1)
            layer_norm_std(0, 0, T)

            def k_tail(half, i, par):
                norm_hi(8 * half + i, par, kT_hi[:, REP * half:REP * half + REP, bass.ds(i * P, P)], cst[:, 11:12])

            def k_step(half, i, par):
                norm_square(8 * half + i, par, k_square, bank[par])
                if isinstance(i, int) and i == 0:
                    if half:
                        k_tail(half - 1, 7, 1)
                else:
                    k_tail(half, i - 1, 1 - par)

            k_units(act, k_step,
                    lambda: cut(2, 0, cut_target(2, 0)[0], 1.0),
                    lambda: cut(3, 1, cut_target(3, 1)[0], W_SCALE))
            k_tail(1, 7, 1)
            cut(4, 0, cut_target(4, 0)[0], W_SCALE)
            cut(5, 1, cut_target(5, 1)[0], W_SCALE)
            act.wait_ge(const_in, 48)
            nc.scalar.activation(gate_hi[:], small[:, 24:56], ACT.Copy, scale=W_SCALE).then_inc(cst_ready, 1)
            for t in range(T):
                layer_norm_std(1, t, t + 1)

            def v_step(half, i, par):
                act.wait_ge(v_proj, 8 * half + i + 1)
                nc.scalar.activation(v_hi[:, REP * half:REP * half + REP, bass.ds(i * P, P)],
                                     bank[par][:].rearrange("p (h n) -> p h n", h=REP), ACT.Copy,
                                     scale=1.0 / W_SCALE).then_inc(v_cut_hi, 1)

            def w13_floats(j, par):
                act.wait_ge(w13_nibbles, j + 1)
                wait(act, w13_cut_lo, j - 1)
                nc.scalar.activation(w13_f[par], nib[:, 0:1024], ACT.Copy).then_inc(w13_float, 1)

            def w2_floats(j, par):
                act.wait_ge(w2_nibbles, j + 1)
                wait(act, w2_cut_lo, j - 1)
                nc.scalar.activation(w2_f[par], nib[:, 1024:1536], ACT.Copy).then_inc(w2_float, 1)

            def w13_hi_part(j, par):
                act.wait_ge(w13_scaled, j + 1)
                wait(act, ab_done, j - 1)
                nc.scalar.activation(w13_hi[par], w13_f[par], ACT.Copy, scale=W_SCALE).then_inc(w13_cut_hi, 1)

            def w2_hi_part(j, par):
                act.wait_ge(w2_scaled, j + 1)
                wait(act, ffn_tile, j - 1)
                nc.scalar.activation(w2_hi[par], w2_f[par], ACT.Copy, scale=W_SCALE).then_inc(w2_cut_hi, 1)

            def weights_in(j, par):
                if not (isinstance(j, int) and not 0 <= j + 2 < HT):
                    w2_floats(j + 2, par)
                if not (isinstance(j, int) and j + 3 >= HT):
                    w13_floats(j + 3, 1 - par)

            def weights_cut(j, par):
                if not (isinstance(j, int) and not 0 <= j + 2 < HT):
                    w13_hi_part(j + 2, par)
                if not (isinstance(j, int) and not 0 <= j + 1 < HT):
                    w2_hi_part(j + 1, 1 - par)

            with act.Fori(0, 2) as m:
                for u in range(4):
                    v_step(0, 4 * m + u, u)
            turned_x(1)
            for i in range(8):
                v_step(1, i, i % 4)
                if i % 2 == 0 and i < 6:
                    weights_in(i // 2 - 3, (i // 2 - 3) % 2)
                elif i % 2 and i < 6:
                    weights_cut(i // 2 - 3, (i // 2 - 3) % 2)

            def q_cut(kv, par, pieces=range(C)):
                if 0 in pieces and not (isinstance(kv, int) and kv < 2):
                    act.wait_ge(n_proj, 16 + 4 * kv - 4)
                cut(CUT_Q + kv, par, chunks(wq_hi[par]), W_SCALE, pieces)

            def ffn_step(j, par):
                weights_in(j, par)
                act.wait_ge(ab_done, j + 1)
                wait(act, h_ready, j - 1)
                nc.scalar.activation(xn[:, par, :], bank[2 * par][:], ACT.Silu, scale=1.0 / W_SCALE).then_inc(silu_a, 1)
                act.wait_ge(h_ready, j + 1)
                wait(act, ffn_tile, j - 1)
                nc.scalar.activation(h_hi[par], xn[:, 2 + par, :], ACT.Copy).then_inc(h_cut_hi, 1)
                weights_cut(j, par)

            ffn_step(0, 0)
            ffn_step(1, 1)
            with act.Fori(1, 4) as m:
                ffn_step(2 * m, 0)
                ffn_step(2 * m + 1, 1)
            for j in range(8, HT):
                ffn_step(j, j % 2)
                if j == 8:
                    q_cut(0, 0)

            def q_target(flat, kv, t):
                base = kv * (B * REP * S) + (t // QT) * (REP * S)
                return flat[:, bass.ds(base, REP * S)].rearrange("p (h n) -> p h n", h=REP)[
                    :, :, (t % QT) * P:(t % QT + 1) * P]

            def q_tail(kv, t):
                norm_hi(16 + 4 * kv + t, t % 2, q_target(q_hi, kv, t), cst[:, 10:11])

            def q_group(kv, par):
                for t in range(T):
                    if not (isinstance(kv, int) and kv + 1 >= KV):
                        q_cut(kv + 1, 1 - par, Q_PIECES[t])
                    norm_square(16 + 4 * kv + t, t % 2, xn[:, 2:4, :], bank[Q_BANKS[t]])
                    if t:
                        q_tail(kv, t - 1)
                    elif not (isinstance(kv, int) and kv == 0):
                        q_tail(kv - 1, T - 1)

            for t in range(T):
                layer_norm_std(2, t, t + 1)
            turned_x(2)
            q_group(0, 0)
            q_group(1, 1)
            with act.Fori(1, 3) as m:
                q_group(2 * m, 0)
                q_group(2 * m + 1, 1)
            q_group(6, 0)
            q_group(7, 1)
            q_tail(7, T - 1)

            def o_cut(kv, par, pieces=range(C)):
                wait(act, o_group, kv - 1)
                cut(CUT_O + kv, par, chunks(wo_hi[par]), W_SCALE, pieces)

            def o_hi_part(m, pair):
                act.wait_ge(pv_done, m + 1)
                nc.scalar.activation(q_hi[:, bass.ds(m * 512, 512)], bank[6 + pair][:], ACT.Copy,
                                     scale=O_SCALE / P_SCALE).then_inc(o_hi, 1)

            def attend(g, u):
                k = 8 * g + u
                first, last = isinstance(g, int) and g == 0, isinstance(g, int) and g == G
                if not (first and u < 3) and not (last and u >= 3):
                    w = (u + 5) % 8
                    act.wait_ge(p_turned, k - 2)
                    if u >= 3:
                        wait(act, pv_done, 2 * g + w // 4 - 1)
                    else:
                        wait(act, pv_done, 2 * g - 2)
                    pair, h, qt = w // 4, w // 2 % 2, w % 2
                    nc.scalar.activation(pT_hi[pair][:, :, h * S + qt * P:h * S + (qt + 1) * P],
                                         bank[4 + w % 2][:].rearrange("p (k n) -> p k n", k=KT),
                                         ACT.Copy, scale=P_SCALE).then_inc(p_hi, 1)
                if not last:
                    act.wait_ge(masked, k + 1)
                    nc.scalar.activation(xn[:, u % 4, :], xn[:, u % 4, :], ACT.Exp, bias=nmax[:, u % 4:u % 4 + 1],
                                         scale=-1.0, accum_out=psum_p[:, u % 4:u % 4 + 1]).then_inc(exped, 1)
                if u == 0 and not (isinstance(g, int) and g < 2):
                    o_hi_part(2 * g - 3, 1)
                if u == 4 and not first:
                    o_hi_part(2 * g - 2, 0)

            for u in range(8):
                attend(0, u)
            for u in range(8):
                attend(1, u)
                if u % 2 == 0:
                    o_cut(0, 0, [u // 2])
            with act.Fori(2, G) as g:
                for u in range(8):
                    attend(g, u)
            for u in range(8):
                attend(G, u)
                if u >= C:
                    o_cut(1, 1, [u - C])
            o_hi_part(2 * G - 1, 1)

            def e_cut(j, par):
                wait(act, e_unit, T * (j - 1))
                cut(CUT_E + j, par, chunks(wq_hi[par]), W_SCALE)

            with act.Fori(1, KV // 2) as m:
                o_cut(2 * m, 0)
                o_cut(2 * m + 1, 1)
            e_cut(0, 0)
            e_cut(1, 1)
            for t in range(T):
                layer_norm_std(3, t, t + 1)
            turned_x(3)
            with act.Fori(1, EXPERTS // 2) as m:
                e_cut(2 * m, 0)
                e_cut(2 * m + 1, 1)

        @block.vector
        def _(dve):
            steps = [0]

            def then(ins):
                steps[0] += 1
                ins.then_inc(dve_step, 1)
                dve.wait_ge(dve_step, steps[0])

            def cut(c, par, hi, lo, scale, pieces=range(C)):
                for p in pieces:
                    dve.wait_ge(cut_hi, C * c + p + 1)
                    nc.vector.scalar_tensor_tensor(lo[:, p, :], chunks(ring[:, par, :])[:, p, :], scale,
                                                   hi[:, p, :], ALU.mult, ALU.subtract).then_inc(cut_lo, 1)

            def cut_k(c):
                hi, lo = cut_target(c, 0)
                cut(c, item_of(c) % 2, hi, lo, 1.0 if c in (0, 2) else W_SCALE)

            def layer_norm_stats(t):
                then(nc.vector.bn_stats(ln_st[:, t, :], x_res[:, t, :]))
                nc.vector.bn_aggr(ln_mv[:, t, :], ln_st[:, t, :]).then_inc(ln_stats, 1)

            def layer_norm_out(stage, t):
                dve.wait_ge(ln_std, 1 + T * (stage - 1) + t + 1)
                then(nc.vector.reciprocal(ln_r[:, t:t + 1], ln_sd[:, t:t + 1]))
                nc.vector.tensor_scalar(xn[:, t, :], x_res[:, t, :], ln_mv[:, t, 0:1], ln_r[:, t:t + 1],
                                        ALU.subtract, ALU.mult).then_inc(xn_ready, 1)

            def turned_x(stage):
                for t in range(T):
                    dve.wait_ge(xT_cut_hi, T * (stage - 1) + t + 1)
                    nc.vector.tensor_tensor(xT_lo[:, :, t * P:(t + 1) * P],
                                            bank[4 + t][:].rearrange("p (c n) -> p c n", c=C),
                                            xT_hi[:, :, t * P:(t + 1) * P], ALU.subtract).then_inc(xT_cut_lo, 1)

            def norm_scale(n, par, square, unit, source):
                dve.wait_ge(n_square, n + 1)
                nc.vector.tensor_reduce(sumsq[:, par, :], square[:, par, :].rearrange("p (h n) -> p h n", h=REP),
                                        AX.X, ALU.add).then_inc(n_sumsq, 1)
                dve.wait_ge(n_rms, n + 1)
                nc.vector.reciprocal(inv_rms[:, par, :], rms[:, par, :]).then_inc(n_inv, 1)
                dve.wait_ge(n_inv, n + 1)
                wait(dve, n_turned, n - 1)
                nc.vector.scalar_tensor_tensor(
                    unit[:, par, :].rearrange("p (h n) -> p h n", h=REP),
                    source[:].rearrange("p (h n) -> p h n", h=REP), 1.0 / W_SCALE,
                    inv_rms[:, par, :].unsqueeze(2).broadcast_to([P, REP, HD]), ALU.mult,
                    ALU.mult).then_inc(n_unit, 1)

            def norm_lo(n, par, hi, lo, weight):
                dve.wait_ge(n_hi, n + 1)
                nc.vector.scalar_tensor_tensor(lo, bank[2 + par][:].rearrange("p (h n) -> p h n", h=REP), weight,
                                               hi, ALU.mult, ALU.subtract).then_inc(n_lo, 1)

            nc.vector.memset(ones_b[:], 1.0)
            nc.vector.memset(eps[:], EPS)
            cut_k(0)
            cut_k(1)
            dve.wait_ge(const_in, 48)
            nc.vector.tensor_copy(ident_b[:], ident[:])
            then(nc.vector.reciprocal(cst[:, 0:1], small[:, 0:1]))
            nc.vector.reciprocal(cst[:, 1:2], small[:, 2:3])
            nc.vector.tensor_tensor(cst[:, 2:3], small[:, 0:1], small[:, 2:3], ALU.mult)
            nc.vector.tensor_scalar(cst[:, 3:4], small[:, 1:2], -1.0, MID, ALU.mult, ALU.add)
            then(nc.vector.tensor_scalar(cst[:, 4:5], small[:, 3:4], -1.0, MID, ALU.mult, ALU.add))
            then(nc.vector.tensor_tensor(cst[:, 5:6], cst[:, 3:4], cst[:, 4:5], ALU.mult))
            then(nc.vector.tensor_scalar(cst[:, 5:6], cst[:, 5:6], float(S2), None, ALU.mult))
            nc.vector.tensor_scalar(cst[:, 10:12], small[:, 4:6], float(HD) ** -0.25, None,
                                    ALU.mult).then_inc(cst_ready, 1)
            dve.wait_ge(x_loaded, 16)
            for t in range(T):
                layer_norm_stats(t)
            dve.wait_ge(ln_std, 1)
            then(nc.vector.reciprocal(ln_r[:], ln_sd[:]))
            then(nc.vector.tensor_tensor(first[:], ln_r[:], ln_r[:], ALU.mult))
            then(nc.vector.scalar_tensor_tensor(first[:], ln_mv[:, :, 1], eps[:], first[:], ALU.add, ALU.mult))
            then(nc.vector.tensor_scalar(first[:], first[:], -0.5, 1.5, ALU.mult, ALU.add))
            nc.vector.tensor_tensor(ln_r[:], ln_r[:], first[:], ALU.mult).then_inc(ln_rstd, 1)

            def k_tail(half, i, par):
                hs = slice(REP * half, REP * half + REP)
                norm_lo(8 * half + i, par, kT_hi[:, hs, bass.ds(i * P, P)], kT_lo[:, hs, bass.ds(i * P, P)],
                        cst[:, 11:12])

            def k_step(half, i, par):
                norm_scale(8 * half + i, par, k_square, k_unit, bank[par])
                if isinstance(i, int) and i == 0:
                    if half:
                        quantise()
                        k_tail(half - 1, 7, 1)
                else:
                    k_tail(half, i - 1, 1 - par)

            def quantise():
                for t in range(T):
                    dve.wait_ge(x_scaled, t + 1)
                    then(nc.vector.tensor_scalar(q1[:, t, :], xn[:, t, :], ROUND, ROUND + MID, ALU.add,
                                                 ALU.subtract))
                    nc.vector.tensor_reduce(row_sum[:, t:t + 1], q1[:, t, :], AX.X, ALU.add).then_inc(q1_ready, 1)
                for b in range(B):
                    dve.wait_ge(nat_scaled, b + 1)
                    nc.vector.tensor_scalar(q2[:, b, :, :], chunks(ring[:, NAT[b] % 2, :]), ROUND, ROUND + MID,
                                            ALU.add, ALU.subtract).then_inc(q2_ready, 1)

            k_units(dve, k_step, lambda: cut_k(2), lambda: cut_k(3))
            k_tail(1, 7, 1)

            for t in range(T):
                dve.wait_ge(q1_turned, t + 1)
                nc.vector.tensor_copy(q1T[:, :, t * P:(t + 1) * P],
                                      bank[4 + t % 2][:].bitcast(BF16)[:, 0:KT * P].rearrange(
                                          "p (k n) -> p k n", k=KT)).then_inc(q1T_ready, 1)
            cut_k(4)
            then(nc.vector.tensor_scalar(row_term[:], row_sum[:], cst[:, 4:5], cst[:, 5:6], ALU.mult, ALU.add))
            for b in range(B):
                dve.wait_ge(col_sum, b + 1)
                then(nc.vector.tensor_scalar(col_term[:, b, :], bank[4 + b][:], cst[:, 3:4], None, ALU.mult))
            for t in range(T + 1):
                if t < T:
                    dve.wait_ge(cross_done, t + 1)
                    ins = nc.vector.scalar_tensor_tensor(cross[:, t % 2, :], bank[6 + t % 2][:],
                                                         row_term[:, t:t + 1], col_term[:, t // QT, :],
                                                         ALU.add, ALU.add)
                    ins.then_inc(cross_used, 1)
                    dve.wait_ge(cross_used, t + 1)
                    then(nc.vector.scalar_tensor_tensor(x_res[:, t, :], cross[:, t % 2, :], cst[:, 2:3],
                                                        x_res[:, t, :], ALU.mult, ALU.add))
                    layer_norm_stats(t)
                if t:
                    layer_norm_out(1, t - 1)
            cut_k(5)

            def v_step(half, i, par):
                hs = slice(REP * half, REP * half + REP)
                dve.wait_ge(v_cut_hi, 8 * half + i + 1)
                nc.vector.scalar_tensor_tensor(v_lo[:, hs, bass.ds(i * P, P)],
                                               bank[par][:].rearrange("p (h n) -> p h n", h=REP), 1.0 / W_SCALE,
                                               v_hi[:, hs, bass.ds(i * P, P)], ALU.mult,
                                               ALU.subtract).then_inc(v_cut_lo, 1)

            def unpack_w13(j, par):
                dve.wait_ge(ffn_in[par], 16 * (j + 2 - par))
                wait(dve, w13_float, j)
                words = raw_int[par][:, 0:512].rearrange("p (m h) -> p m h", m=4)
                out13 = nib[:, 0:1024].rearrange("p (m b h) -> p m b h", m=4, b=2)
                for b in range(2):
                    ins = nc.vector.tensor_scalar(out13[:, :, b, :], words, shift[:, 4 + b:5 + b], 28,
                                                  ALU.logical_shift_left, ALU.arith_shift_right)
                ins.then_inc(w13_nibbles, 1)

            def unpack_w2(j, par):
                wait(dve, w2_float, j)
                out2 = nib[:, 1024:1536].rearrange("p (q r) -> p q r", r=4)
                for r in range(4):
                    ins = nc.vector.tensor_scalar(out2[:, :, r], raw_int[par][:, 512 + 128 * r:640 + 128 * r],
                                                  shift[:, r:r + 1], 28, ALU.logical_shift_left,
                                                  ALU.arith_shift_right)
                ins.then_inc(w2_nibbles, 1)

            def w13_lo_part(j, par):
                dve.wait_ge(w13_cut_hi, j + 1)
                nc.vector.scalar_tensor_tensor(w13_lo[par], w13_f[par], W_SCALE, w13_hi[par], ALU.mult,
                                               ALU.subtract).then_inc(w13_cut_lo, 1)

            def w2_lo_part(j, par):
                dve.wait_ge(w2_cut_hi, j + 1)
                nc.vector.scalar_tensor_tensor(w2_lo[par], w2_f[par], W_SCALE, w2_hi[par], ALU.mult,
                                               ALU.subtract).then_inc(w2_cut_lo, 1)

            def weights_in(j, par):
                if not (isinstance(j, int) and not 0 <= j + 2 < HT):
                    unpack_w2(j + 2, par)
                if not (isinstance(j, int) and j + 3 >= HT):
                    unpack_w13(j + 3, 1 - par)

            def weights_cut(j, par):
                if not (isinstance(j, int) and not 0 <= j + 2 < HT):
                    w13_lo_part(j + 2, par)
                if not (isinstance(j, int) and not 0 <= j + 1 < HT):
                    w2_lo_part(j + 1, 1 - par)

            with dve.Fori(0, 2) as m:
                for u in range(4):
                    v_step(0, 4 * m + u, u)
            turned_x(1)
            for i in range(8):
                v_step(1, i, i % 4)
                if i % 2 == 0 and i < 6:
                    weights_in(i // 2 - 3, (i // 2 - 3) % 2)
                elif i % 2 and i < 6:
                    weights_cut(i // 2 - 3, (i // 2 - 3) % 2)

            def q_cut(kv, par, pieces=range(C)):
                cut(CUT_Q + kv, par, chunks(wq_hi[par]), chunks(wq_lo[par]), W_SCALE, pieces)

            def ffn_step(j, par):
                weights_in(j, par)
                dve.wait_ge(silu_a, j + 1)
                wait(dve, h_cut_lo, j - 1)
                nc.vector.scalar_tensor_tensor(xn[:, 2 + par, :], xn[:, par, :], 1.0 / W_SCALE,
                                               bank[2 * par + 1][:], ALU.mult, ALU.mult).then_inc(h_ready, 1)
                dve.wait_ge(h_cut_hi, j + 1)
                nc.vector.tensor_tensor(h_lo[par], xn[:, 2 + par, :], h_hi[par], ALU.subtract).then_inc(h_cut_lo, 1)
                weights_cut(j, par)

            ffn_step(0, 0)
            ffn_step(1, 1)
            with dve.Fori(1, 4) as m:
                ffn_step(2 * m, 0)
                ffn_step(2 * m + 1, 1)
            for j in range(8, HT):
                ffn_step(j, j % 2)
                if j == 8:
                    q_cut(0, 0)

            def residual(stage, done, per, banks, scale):
                for t in range(T + 1):
                    if t < T:
                        dve.wait_ge(done, per + t)
                        then(nc.vector.scalar_tensor_tensor(x_res[:, t, :], banks[t][:], scale, x_res[:, t, :],
                                                            ALU.mult, ALU.add))
                        layer_norm_stats(t)
                    if t:
                        layer_norm_out(stage, t - 1)

            residual(2, ffn_out, 1, bank[4:8], 1.0 / W_SCALE)

            def q_target(flat, kv, t):
                base = kv * (B * REP * S) + (t // QT) * (REP * S)
                return flat[:, bass.ds(base, REP * S)].rearrange("p (h n) -> p h n", h=REP)[
                    :, :, (t % QT) * P:(t % QT + 1) * P]

            def q_tail(kv, t):
                norm_lo(16 + 4 * kv + t, t % 2, q_target(q_hi, kv, t), q_target(q_lo, kv, t), cst[:, 10:11])

            def q_group(kv, par):
                for t in range(T):
                    if not (isinstance(kv, int) and kv + 1 >= KV):
                        q_cut(kv + 1, 1 - par, Q_PIECES[t])
                    norm_scale(16 + 4 * kv + t, t % 2, xn[:, 2:4, :], xn[:, 0:2, :], bank[Q_BANKS[t]])
                    if t:
                        q_tail(kv, t - 1)
                    elif not (isinstance(kv, int) and kv == 0):
                        q_tail(kv - 1, T - 1)

            turned_x(2)
            q_group(0, 0)
            q_group(1, 1)
            with dve.Fori(1, 3) as m:
                q_group(2 * m, 0)
                q_group(2 * m + 1, 1)
            q_group(6, 0)
            q_group(7, 1)
            q_tail(7, T - 1)

            def o_cut(kv, par, pieces=range(C)):
                cut(CUT_O + kv, par, chunks(wo_hi[par]), chunks(wo_lo[par]), W_SCALE, pieces)

            def o_lo_part(m, pair):
                dve.wait_ge(o_hi, m + 1)
                nc.vector.scalar_tensor_tensor(q_lo[:, bass.ds(m * 512, 512)], bank[6 + pair][:],
                                               O_SCALE / P_SCALE, q_hi[:, bass.ds(m * 512, 512)], ALU.mult,
                                               ALU.subtract).then_inc(o_lo, 1)

            def attend(g, u):
                k = 8 * g + u
                first, last = isinstance(g, int) and g == 0, isinstance(g, int) and g == G
                if not (first and u < 2) and not (last and u > 1):
                    dve.wait_ge(exped, k - 1)
                    v = (u + 2) % 4
                    nc.vector.reciprocal(inv_p[:, v:v + 1], psum_p[:, v:v + 1]).then_inc(inverted, 1)
                if not last:
                    dve.wait_ge(scored, k + 1)
                    wait(dve, p_turned, k - 3)
                    if first and u == 0:
                        dve.wait_ge(mask_loaded, 16)
                if not (first and u < 4) and not (last and u >= 4):
                    w = (u + 4) % 8
                    pair, h, qt = w // 4, w // 2 % 2, w % 2
                    dve.wait_ge(p_hi, k - 3)
                    cols = slice(h * S + qt * P, h * S + (qt + 1) * P)
                    nc.vector.scalar_tensor_tensor(pT_lo[pair][:, :, cols],
                                                   bank[4 + w % 2][:].rearrange("p (k n) -> p k n", k=KT), P_SCALE,
                                                   pT_hi[pair][:, :, cols], ALU.mult,
                                                   ALU.subtract).then_inc(p_lo, 1)
                if not last:
                    nc.vector.tensor_tensor_reduce(xn[:, u % 4, :], bank[u % 4][:], mask[:, u % 2, :], -1.0, BIG,
                                                   ALU.add, ALU.min, nmax[:, u % 4:u % 4 + 1]).then_inc(masked, 1)
                if u == 1 and not (isinstance(g, int) and g < 2):
                    o_lo_part(2 * g - 3, 1)
                if u == 5 and not first:
                    o_lo_part(2 * g - 2, 0)

            for u in range(8):
                attend(0, u)
            for u in range(8):
                attend(1, u)
                if u % 2 == 0:
                    o_cut(0, 0, [u // 2])
            with dve.Fori(2, G) as g:
                for u in range(8):
                    attend(g, u)
            for u in range(8):
                attend(G, u)
                if u >= C:
                    o_cut(1, 1, [u - C])
            o_lo_part(2 * G - 1, 1)

            def e_cut(j, par):
                cut(CUT_E + j, par, chunks(wq_hi[par]), chunks(wq_lo[par]), W_SCALE)

            with dve.Fori(1, KV // 2) as m:
                o_cut(2 * m, 0)
                o_cut(2 * m + 1, 1)
            e_cut(0, 0)
            e_cut(1, 1)
            dve.wait_ge(cst_ready, 2)
            then(nc.vector.scalar_tensor_tensor(gate_lo[:], small[:, 24:56], W_SCALE, gate_hi[:], ALU.mult,
                                                ALU.subtract))
            residual(3, o_out, 1, bank[0:4], 1.0 / (W_SCALE * O_SCALE))
            turned_x(3)

            gate_bias, index = small[:, 8:16], small[:, 16:24]
            for t in range(T):
                dve.wait_ge(logits, T)
                then(nc.vector.scalar_tensor_tensor(lg[:, t, :], bank[0][:, t * EXPERTS:(t + 1) * EXPERTS],
                                                    1.0 / W_SCALE, gate_bias, ALU.mult, ALU.add))
            then(nc.vector.tensor_reduce(top[:], lg[:], AX.X, ALU.max))
            for t in range(T):
                then(nc.vector.tensor_scalar(cand[:, t, :], lg[:, t, :], top[:, t:t + 1], float(EXPERTS),
                                             ALU.is_lt, ALU.mult))
                then(nc.vector.tensor_tensor(cand[:, t, :], cand[:, t, :], index, ALU.add))
            then(nc.vector.tensor_reduce(first[:], cand[:], AX.X, ALU.min))
            for t in range(T):
                then(nc.vector.tensor_scalar(onehot[:, t, :], index, first[:, t:t + 1], None, ALU.is_equal))
                nc.vector.tensor_scalar(onehot_s[:, t, :], onehot[:, t, :], 1.0 / W_SCALE, None,
                                        ALU.mult).then_inc(chosen, 1)
            bias_hl = [wo_hi[0][0:EXPERTS, 0:D], wo_lo[0][0:EXPERTS, 0:D]]
            dve.wait_ge(bias_loaded, 16)
            then(nc.vector.tensor_scalar(bias_hl[0], bias_f[:], W_SCALE, None, ALU.mult))
            then(nc.vector.scalar_tensor_tensor(bias_hl[1], bias_f[:], W_SCALE, bias_hl[0], ALU.mult, ALU.subtract))
            dve.wait_ge(choice_turned, 1)
            nc.vector.tensor_copy(oneT, bank[1][0:EXPERTS, :].rearrange("e (t n) -> e t n", t=T)).then_inc(
                choice_T, 1)
            for t in range(T):
                dve.wait_ge(bias_out, t + 1)
                nc.vector.scalar_tensor_tensor(x_res[:, t, :], bank[2 + t % 2][:], 1.0 / W_SCALE,
                                               x_res[:, t, :], ALU.mult, ALU.add).then_inc(bias_added, 1)
            dve.wait_ge(bias_added, T)

            def expert(j, following=None):
                for t in range(T):
                    if t == 1 and following is not None:
                        e_cut(*following)
                    dve.wait_ge(e_unit, T * j + t + 1)
                    wait(dve, e_added, T * (j - 1) + t + 1)
                    nc.vector.scalar_tensor_tensor(x_res[:, t, :], bank[4 + t][:], onehot_s[:, t, bass.ds(j, 1)],
                                                   x_res[:, t, :], ALU.mult, ALU.add).then_inc(e_added, 1)

            expert(0)
            with dve.Fori(1, EXPERTS // 2) as m:
                expert(2 * m - 1, (2 * m, 0))
                expert(2 * m, (2 * m + 1, 1))
            expert(EXPERTS - 1)

        @block.tensor
        def _(pe):
            def three(out_ap, pairs, start=True, stop=True):
                n = 0
                for (w_hi, w_lo), (m_hi, m_lo) in pairs:
                    for w, m in ((w_hi, m_hi), (w_hi, m_lo), (w_lo, m_hi)):
                        mm = nc.tensor.matmul(out_ap, w, m, start=start and n == 0,
                                              stop=stop and n == 3 * len(pairs) - 1, skip_group_check=True)
                        n += 1
                return mm

            def turn_x(stage):
                for t in range(T):
                    pe.wait_ge(xn_ready, T * (stage - 1) + t + 1)
                    for c in range(C):
                        mm = nc.tensor.transpose(bank[4 + t][:, c * P:(c + 1) * P], xn[:, t, c * P:(c + 1) * P],
                                                 ident[:])
                    mm.then_inc(xT_turned, 1)

            def norm_turn(n, par, unit):
                pe.wait_ge(n_unit, n + 1)
                wait(pe, n_lo, n - 1)
                for h in range(REP):
                    mm = nc.tensor.transpose(bank[2 + par][:, h * HD:(h + 1) * HD],
                                             unit[:, par, h * HD:(h + 1) * HD], ident[:])
                mm.then_inc(n_turned, 1)

            def kv_project(i, par, half, w_hi, w_lo):
                tile = bass.ds(i * P, P)
                return three(bank[par][:], [((cT_hi[:, c, tile], cT_lo[:, c, tile]),
                                             (w_hi[:, half, c * 512:(c + 1) * 512],
                                              w_lo[:, half, c * 512:(c + 1) * 512])) for c in range(C)])

            def k_step(half, i, par):
                n = 8 * half + i
                if isinstance(i, int) and i == 0:
                    pe.wait_ge(cut_lo, C * (2 if half == 0 else 4))
                wait(pe, n_unit, n - 1)
                kv_project(i, par, half, wk_hi, wk_lo).then_inc(n_proj, 1)
                if not (isinstance(n, int) and n == 0):
                    norm_turn(n - 1, 1 - par, k_unit)

            k_units(pe, k_step, None, lambda: pe.wait_ge(cut_lo, C * (3)))
            norm_turn(15, 1, k_unit)

            for t in range(T):
                pe.wait_ge(q1_ready, t + 1)
                wait(pe, q1T_ready, t - 1)
                for c in range(KT):
                    mm = nc.tensor.transpose(bank[4 + t % 2][:].bitcast(BF16)[:, c * P:(c + 1) * P],
                                             q1[:, t, c * P:(c + 1) * P], ident_b[:])
                mm.then_inc(q1_turned, 1)
            pe.wait_ge(q1T_ready, T)
            pe.wait_ge(q2_ready, B)
            for b in range(B):
                for c in range(KT):
                    mm = nc.tensor.matmul(bank[4 + b][:], ones_b[:], q2[:, b, c, :], start=(c == 0),
                                          stop=(c == KT - 1))
                mm.then_inc(col_sum, 1)
            for t in range(T):
                wait(pe, cross_used, t - 1)
                for c in range(KT):
                    mm = nc.tensor.matmul(bank[6 + t % 2][:], q1T[:, c, t * P:(t + 1) * P], q2[:, t // QT, c, :],
                                          start=(c == 0), stop=(c == KT - 1))
                mm.then_inc(cross_done, 1)

            def v_step(half, i, par):
                n = 8 * half + i
                wait(pe, v_cut_lo, n - 3)
                kv_project(i, par, half, wv_hi, wv_lo).then_inc(v_proj, 1)

            pe.wait_ge(n_lo, 16)
            pe.wait_ge(cut_lo, C * (CUT_V + 1))
            for u in range(4):
                v_step(0, u, u)
            for u in range(4):
                v_step(0, 4 + u, u)
            turn_x(1)
            pe.wait_ge(cut_lo, C * (CUT_V + 2))
            with pe.Fori(0, 2) as m:
                for u in range(4):
                    v_step(1, 4 * m + u, u)

            def ffn_ab(j, par):
                pe.wait_ge(w13_cut_lo, j + 1)
                wait(pe, h_ready, j - 1)
                for mat in range(2):
                    mm = three(bank[2 * par + mat][:],
                               [((w13_hi[par][:, (4 * mat + c) * P:(4 * mat + c + 1) * P],
                                  w13_lo[par][:, (4 * mat + c) * P:(4 * mat + c + 1) * P]),
                                 (xT_hi[:, c, :], xT_lo[:, c, :])) for c in range(C)])
                mm.then_inc(ab_done, 1)

            def ffn_down(j, par, start=False, stop=False):
                pe.wait_ge(h_cut_lo, j + 1)
                pe.wait_ge(w2_cut_lo, j + 1)
                for t in range(T):
                    tok = slice(t * P, (t + 1) * P)
                    mm = three(bank[4 + t][:], [((h_hi[par][:, tok], h_lo[par][:, tok]), (w2_hi[par], w2_lo[par]))],
                               start=start, stop=stop)
                    if stop:
                        mm.then_inc(ffn_out, 1)
                if not stop:
                    mm.then_inc(ffn_tile, 1)

            pe.wait_ge(xT_cut_lo, T)
            pe.wait_ge(v_cut_lo, 16)
            ffn_ab(0, 0)
            ffn_ab(1, 1)
            ffn_down(0, 0, start=True)
            with pe.Fori(1, HT // 2) as m:
                ffn_ab(2 * m, 0)
                ffn_down(2 * m - 1, 1)
                ffn_ab(2 * m + 1, 1)
                ffn_down(2 * m, 0)
            ffn_ab(HT - 1, 0)
            ffn_down(HT - 2, 1)
            ffn_down(HT - 1, 0, stop=True)

            turn_x(2)
            pe.wait_ge(xT_cut_lo, 2 * T)

            def q_group(kv, par):
                pe.wait_ge(cut_lo, C * (CUT_Q + kv + 1))
                for t in range(T):
                    n = 16 + 4 * kv + t
                    wait(pe, n_unit, n - 3)
                    tok = slice(t * P, (t + 1) * P)
                    three(bank[Q_BANKS[t]][:], [((xT_hi[:, c, tok], xT_lo[:, c, tok]),
                                            (wq_hi[par][:, c * 512:(c + 1) * 512],
                                             wq_lo[par][:, c * 512:(c + 1) * 512])) for c in range(C)]
                          ).then_inc(n_proj, 1)
                    if not (isinstance(n, int) and n == 16):
                        norm_turn(n - 1, 1 - t % 2, xn[:, 0:2, :])

            q_group(0, 0)
            q_group(1, 1)
            with pe.Fori(1, KV // 2) as m:
                q_group(2 * m, 0)
                q_group(2 * m + 1, 1)
            norm_turn(16 + 4 * KV - 1, 1, xn[:, 0:2, :])
            pe.wait_ge(n_lo, 16 + 4 * KV)

            def attend(g, u):
                k = 8 * g + u
                first, last = isinstance(g, int) and g == 0, isinstance(g, int) and g == G
                if not last:
                    wait(pe, masked, k - 3)
                    h, qt = u // 2, u % 2
                    off = g * (REP * S) + h * S + qt * P
                    three(bank[u % 4][:], [((q_hi[:, bass.ds(off, P)], q_lo[:, bass.ds(off, P)]),
                                            (kT_flat[0][:, bass.ds(g * S2, S2)],
                                             kT_flat[1][:, bass.ds(g * S2, S2)]))]).then_inc(scored, 1)
                if not first:
                    pair, c = u // 4, u % 4
                    if c == 0:
                        pe.wait_ge(p_lo, 8 * g - 4 if pair == 0 else 8 * g)
                        wait(pe, o_lo, 2 * g - 3 + pair)
                    off = (g - 1) * S2 + c * P
                    mm = three(bank[6 + pair][:], [((v_flat[0][:, bass.ds(off, P)], v_flat[1][:, bass.ds(off, P)]),
                                                    (pT_hi[pair][:, c, :], pT_lo[pair][:, c, :]))],
                               start=(c == 0), stop=(c == KT - 1))
                    if c == KT - 1:
                        mm.then_inc(pv_done, 1)
                if not (first and u < 3) and not (last and u >= 3):
                    w = (u + 5) % 8
                    pe.wait_ge(p_ready, k - 2)
                    wait(pe, p_lo, k - 4)
                    for c in range(KT):
                        mm = nc.tensor.transpose(bank[4 + w % 2][:, c * P:(c + 1) * P],
                                                 xn[:, w % 4, c * P:(c + 1) * P], ident[:])
                    mm.then_inc(p_turned, 1)

            for u in range(8):
                attend(0, u)
            for u in range(8):
                attend(1, u)
            with pe.Fori(2, G) as g:
                for u in range(8):
                    attend(g, u)
            for u in range(8):
                attend(G, u)

            def o_step(kv, par, start=False, stop=False):
                pe.wait_ge(o_lo, 4 * kv + 4)
                pe.wait_ge(cut_lo, C * (CUT_O + kv + 1))
                for t in range(T):
                    pairs = []
                    for h in range(REP):
                        off = kv * (B * REP * S) + (t // QT) * (REP * S) + h * S + (t % QT) * P
                        pairs.append(((q_hi[:, bass.ds(off, P)], q_lo[:, bass.ds(off, P)]),
                                      (wo_hi[par][:, h * D:(h + 1) * D], wo_lo[par][:, h * D:(h + 1) * D])))
                    mm = three(bank[t][:], pairs, start=start, stop=stop)
                    if stop:
                        mm.then_inc(o_out, 1)
                if not stop:
                    mm.then_inc(o_group, 1)

            pe.wait_ge(masked, 8 * G)
            o_step(0, 0, start=True)
            o_step(1, 1)
            with pe.Fori(1, KV // 2 - 1) as m:
                o_step(2 * m, 0)
                o_step(2 * m + 1, 1)
            o_step(KV - 2, 0)
            o_step(KV - 1, 1, stop=True)

            turn_x(3)
            for t in range(T):
                pe.wait_ge(xT_cut_lo, 3 * T + t + 1 - T)
                tok = slice(t * P, (t + 1) * P)
                three(bank[0][:, t * EXPERTS:(t + 1) * EXPERTS],
                      [((xT_hi[:, c, tok], xT_lo[:, c, tok]),
                        (gate_hi[:, c * EXPERTS:(c + 1) * EXPERTS], gate_lo[:, c * EXPERTS:(c + 1) * EXPERTS]))
                       for c in range(C)]).then_inc(logits, 1)

            def expert(j, par):
                pe.wait_ge(cut_lo, C * (CUT_E + j + 1))
                for t in range(T):
                    wait(pe, e_added, T * (j - 1) + t + 1)
                    tok = slice(t * P, (t + 1) * P)
                    three(bank[4 + t][:], [((xT_hi[:, c, tok], xT_lo[:, c, tok]),
                                            (wq_hi[par][:, c * 512:(c + 1) * 512],
                                             wq_lo[par][:, c * 512:(c + 1) * 512])) for c in range(C)]
                          ).then_inc(e_unit, 1)

            expert(0, 0)
            pe.wait_ge(chosen, T)
            for t in range(T):
                mm = nc.tensor.transpose(bank[1][0:EXPERTS, t * P:(t + 1) * P], onehot[:, t, :], ident[:])
            mm.then_inc(choice_turned, 1)
            pe.wait_ge(choice_T, 1)
            for t in range(T):
                wait(pe, bias_added, t - 1)
                for hl in range(2):
                    part = (wo_hi if hl == 0 else wo_lo)[0][0:EXPERTS, 0:D]
                    mm = nc.tensor.matmul(bank[2 + t % 2][:], oneT[:, t, :], part, start=(hl == 0), stop=(hl == 1))
                mm.then_inc(bias_out, 1)
            expert(1, 1)
            with pe.Fori(1, EXPERTS // 2) as m:
                expert(2 * m, 0)
                expert(2 * m + 1, 1)


def hidden_tiles(a):
    import numpy as np

    pad = np.zeros((HT * P - a.shape[0],) + a.shape[1:], a.dtype)
    return np.concatenate([a, pad]).reshape((HT, P) + a.shape[1:])


def kernel(**inputs):
    import numpy as np
    import concourse.bacc as bacc
    from concourse import mybir as mb
    from concourse.bass_utils import run_bass_kernel_spmd as run

    a = {k: np.asarray(v) for k, v in inputs.items()}
    x, context = a["x"], a["ctx_4096"]

    order = np.arange(D).reshape(2, 2, 2, GROUP).transpose(0, 2, 1, 3).reshape(-1)

    def item(rows):
        return rows.reshape(C, P, 512).transpose(1, 0, 2).reshape(P, ITEM)

    wk, wv = a["L1_xattn_k_proj_w"].T, a["L1_xattn_v_proj_w"].T
    wq, wo = a["L1_xattn_q_proj_w"].T[order], a["L1_xattn_o_proj_w"].T[:, order]
    stream = [item(context[0].T), item(wk[:, 0:512]), item(context[1].T), item(wk[:, 512:1024]),
              item(context[0][order][:, order]), item(context[1][order][:, order]), item(wv[:, 0:512]), item(wv[:, 512:1024])]
    stream += [item(wq[:, 512 * g:512 * g + 512]) for g in range(KV)]
    stream += [item(wo[512 * g:512 * g + 512]) for g in range(KV)]
    stream += [item(a["L1_ffn_expert_w"][j].T[order][:, order]) for j in range(EXPERTS)]

    def words(w):
        w = w.reshape(HIDDEN, 2, 2, GROUP)
        return hidden_tiles(w).transpose(0, 3, 4, 2, 1).reshape(HT, P, 2 * P)

    def scales(s):
        s = s.reshape(HIDDEN, 2, 2, 2)
        s = np.repeat(hidden_tiles(s).transpose(0, 3, 2, 4, 1), GROUP, axis=1)
        return s.reshape(HT, P, 4 * P)

    w2 = a["L0_ffn_w2"]
    w2 = hidden_tiles(np.concatenate([w2, w2], axis=1).reshape(D, HIDDEN).T[:, order])
    w2 = w2.reshape(HT, P, P, 4).transpose(0, 1, 3, 2).reshape(HT, P, D)
    s2 = hidden_tiles(np.repeat(a["L0_ffn_s2"], GROUP).reshape(D, HIDDEN).T[:, order])
    ffn_int = np.concatenate([words(a["L0_ffn_w1"]), words(a["L0_ffn_w3"]), w2], axis=2)
    ffn_scale = np.concatenate([scales(a["L0_ffn_s1"]), scales(a["L0_ffn_s3"]), s2], axis=2)
    part = np.arange(P)
    shift = np.stack([np.where((96 * r + part) % P < GROUP, 24, 28) for r in range(4)]
                     + [np.full(P, 24), np.full(P, 28)], axis=1).astype(np.int32)

    small = np.zeros((P, 56), np.float32)
    for i, name in enumerate(["x1_scale", "x1_zp", "x2_scale", "x2_zp"]):
        small[:, i] = a["L0_xattn_" + name][0]
    small[:, 4] = a["L1_xattn_q_norm_w"]
    small[:, 5] = a["L1_xattn_k_norm_w"]
    small[:, 8:16] = a["L1_ffn_gate_b"]
    small[:, 16:24] = np.arange(EXPERTS)
    small[:, 24:56] = a["L1_ffn_gate_w"].T[order].reshape(C, P, EXPERTS).transpose(1, 0, 2).reshape(P, -1)

    arrays = {"x": x.reshape(B * S, D)[:, order], "stream": np.stack(stream), "ffn_int": ffn_int, "ffn_scale": ffn_scale,
              "mask": a["mask_1x1xSxS2_ff0"].reshape(S, S2), "small": small, "shift": shift,
              "ident": np.eye(P, dtype=np.float32), "bias": a["L1_ffn_expert_b"][:, order]}
    arrays = {k: np.ascontiguousarray(v) for k, v in arrays.items()}
    nc = bacc.Bacc("TRN2", target_bir_lowering=False, num_devices=1)
    args = [nc.dram_tensor(f"in_{k}", v.shape, mb.dt.from_np(v.dtype), kind="ExternalInput").ap()
            for k, v in arrays.items()]
    out = nc.dram_tensor("out", (B * S, D), mb.dt.float32, kind="ExternalOutput").ap()
    kernel_program(nc, *args, out)
    r = run(nc, [{f"in_{k}": v for k, v in arrays.items()}], core_ids=[0])
    return np.ascontiguousarray(r.results[0]["out"][:, np.argsort(order)]).reshape(B, S, D)
```

```python
from contextlib import ExitStack

import concourse.bass as bass
from concourse import mybir

ALU = mybir.AluOpType
ACT = mybir.ActivationFunctionType
AX = mybir.AxisListType
F32 = mybir.dt.float32
F16 = mybir.dt.float16
BF16 = mybir.dt.bfloat16
I32 = mybir.dt.int32

P = 128
B, S, S2, D = 2, 256, 512, 512
T = B * S // P
C = D // P
KT = S2 // P
HEADS, KV, HD = 32, 8, 128
REP = HEADS // KV
G = KV * B
QT = S // P
GROUP = 64
HIDDEN = 1376
HT = -(-HIDDEN // P)
EXPERTS = 8
EPS = 1e-5

Q_BANKS = [0, 1, 4, 5]
CROSS_BANKS = [6, 7, 2, 3]
V_BANKS = [[0, 1, 4, 5], [0, 1, 2, 3]]
TURN_BANKS = {1: [6, 7, 4, 5], 2: [4, 5, 6, 7], 3: [4, 5, 6, 7]}
START_PIECES = [[], [], [(2, [0, 1, 2, 3])], [], [(3, [0, 1])], [(3, [2])], [(3, [3])], []]
Q_PIECES = [[0, 1], [2], [3], []]
W_SCALE = 64.0
P_SCALE = 1024.0
O_SCALE = 16.0
ROUND = 12582912.0
MID = 128.0
BIG = 3.0e38

WV, WQ, WO = 4, 6, 14
ITEMS = 30
ITEM = 2048
FFN_INT, FFN_SC = 1024, 1536

STEPS = EXPERTS + T - 1
SC_IOTA, SC_BEFORE, SC_PLACE = 0, B * S, B * S + P
SC_TILE8, SC_N = SC_PLACE + T, SC_PLACE + 2 * T
SC_N8 = SC_N + STEPS
SC_COLS = SC_N8 + STEPS


def kernel_program(nc, x_in, stream, nat_in, ffn_int, ffn_scale, mask_in, small_in, shift_in, ident_in,
                   bias_in, sort_in, out):
    with ExitStack() as ctx:
        def sem(name):
            return ctx.enter_context(nc.semaphore(name))

        arena = ctx.enter_context(nc.sbuf_tensor("arena", [P, 204 * 256], F32))

        def at(kib, n, dtype):
            words = n if dtype in (F32, I32) else n // 2
            a = arena[:, kib * 256:kib * 256 + words]
            return a if dtype == F32 else a.bitcast(dtype)

        x_res = at(0, T * D, F32).rearrange("p (t d) -> p t d", t=T)
        xn = at(8, T * D, F32).rearrange("p (t d) -> p t d", t=T)
        xT_hi = at(16, C * 512, F16).rearrange("p (c n) -> p c n", c=C)
        xT_lo = at(20, C * 512, F16).rearrange("p (c n) -> p c n", c=C)
        kT_hi = at(24, KV * B * S2, F16).rearrange("p (h n) -> p h n", h=KV)
        kT_lo = at(40, KV * B * S2, F16).rearrange("p (h n) -> p h n", h=KV)
        kT_flat = [at(24, KV * B * S2, F16), at(40, KV * B * S2, F16)]
        v_hi = at(56, KV * B * S2, F16).rearrange("p (h n) -> p h n", h=KV)
        v_lo = at(72, KV * B * S2, F16).rearrange("p (h n) -> p h n", h=KV)
        v_flat = [at(56, KV * B * S2, F16), at(72, KV * B * S2, F16)]
        nat = at(56, B * ITEM, F32).rearrange("p (b n) -> p b n", b=B)
        ring_flat = at(88, 2 * ITEM, F32)
        ring = at(88, 2 * ITEM, F32).rearrange("p (s n) -> p s n", s=2)
        raw_int = [at(104 + 10 * s, FFN_INT, I32) for s in range(2)]
        raw_sc = [at(108 + 10 * s, FFN_SC, F32) for s in range(2)]
        wo_hi = [at(104 + 8 * s, ITEM, F16) for s in range(2)]
        wo_lo = [at(108 + 8 * s, ITEM, F16) for s in range(2)]
        mask = at(120, QT * S2, F32).rearrange("p (q n) -> p q n", q=QT)
        cT_hi = at(124, C * B * S2, F16).rearrange("p (c n) -> p c n", c=C)
        cT_lo = at(132, C * B * S2, F16).rearrange("p (c n) -> p c n", c=C)
        wv_hi = at(140, 2 * ITEM, F16).rearrange("p (h n) -> p h n", h=2)
        wv_lo = at(148, 2 * ITEM, F16).rearrange("p (h n) -> p h n", h=2)
        wv_flat = [at(140, 2 * ITEM, F16), at(148, 2 * ITEM, F16)]
        wk_hi = at(156, 2 * ITEM, F16).rearrange("p (h n) -> p h n", h=2)
        wk_lo = at(164, 2 * ITEM, F16).rearrange("p (h n) -> p h n", h=2)
        q2 = at(172, B * KT * D, BF16).rearrange("p (b k n) -> p b k n", b=B, k=KT)
        q1T = at(180, KT * 512, BF16).rearrange("p (k n) -> p k n", k=KT)
        k_unit = at(184, 2 * 512, F32).rearrange("p (s n) -> p s n", s=2)
        k_square = at(188, 2 * 512, F32).rearrange("p (s n) -> p s n", s=2)
        q1 = at(192, T * D, BF16).rearrange("p (t n) -> p t n", t=T)
        col_term = at(196, B * D, F32).rearrange("p (b n) -> p b n", b=B)
        cross = at(200, 2 * D, F32).rearrange("p (s n) -> p s n", s=2)
        nib = at(156, FFN_SC, I32)
        w13_f = [at(162, 1024, F32), at(200, 1024, F32)]
        w2_f = [at(166 + 2 * s, 512, F32) for s in range(2)]
        w13_hi = [at(170 + 4 * s, 1024, F16) for s in range(2)]
        w13_lo = [at(172 + 4 * s, 1024, F16) for s in range(2)]
        w2_hi = [at(178 + 2 * s, 512, F16) for s in range(2)]
        w2_lo = [at(179 + 2 * s, 512, F16) for s in range(2)]
        h_hi = [at(182 + 2 * s, 512, F16) for s in range(2)]
        h_lo = [at(183 + 2 * s, 512, F16) for s in range(2)]
        q_square = at(112, 2 * 512, F32).rearrange("p (s n) -> p s n", s=2)
        q_hi = at(124, G * REP * S, F16)
        q_lo = at(156, G * REP * S, F16)
        wq_hi = [at(188 + 8 * s, ITEM, F16) for s in range(2)]
        wq_lo = [at(192 + 8 * s, ITEM, F16) for s in range(2)]
        pT_hi = [at(188 + 8 * s, KT * 512, F16).rearrange("p (k n) -> p k n", k=KT) for s in range(2)]
        pT_lo = [at(192 + 8 * s, KT * 512, F16).rearrange("p (k n) -> p k n", k=KT) for s in range(2)]

        we_hi = at(24, EXPERTS * ITEM, F16)
        we_lo = at(56, EXPERTS * ITEM, F16)
        xn_hi = at(104, T * D, F16).rearrange("p (t d) -> p t d", t=T)
        xn_lo = at(108, T * D, F16).rearrange("p (t d) -> p t d", t=T)
        sort_c = at(120, SC_COLS, F32)
        xs_hi = at(124, C * 512, F16).rearrange("p (c n) -> p c n", c=C)
        xs_lo = at(128, C * 512, F16).rearrange("p (c n) -> p c n", c=C)
        ys = at(132, T * D, F32)
        ys_hi = at(140, T * D, F16).rearrange("p (t d) -> p t d", t=T)
        ys_lo = at(144, T * D, F16).rearrange("p (t d) -> p t d", t=T)
        perm = at(188, T * 512, F16).rearrange("p (t n) -> p t n", t=T)
        permT = at(192, T * 512, F16).rearrange("p (t n) -> p t n", t=T)
        ident_h = at(196, P, F16)
        before = at(197, P, BF16)
        oneT = at(198, T * P, F16)[0:EXPERTS, :].rearrange("e (t n) -> e t n", t=T)
        bias_f = at(200, D, F32)[0:EXPERTS, :]
        bias_hl = [at(202, D, F16)[0:EXPERTS, :], at(203, D, F16)[0:EXPERTS, :]]

        def sb(name, shape, dtype):
            return ctx.enter_context(nc.sbuf_tensor(name, shape, dtype))

        ident = sb("ident", [P, P], F32)
        ident_b = sb("ident_b", [P, P], BF16)
        ones_b = sb("ones_b", [P, P], BF16)
        small = sb("small", [P, 56], F32)
        shift = sb("shift", [P, 6], I32)
        eps = sb("eps", [P, 1], F32)
        cst = sb("cst", [P, 12], F32)
        gate_hi = sb("gate_hi", [P, C * EXPERTS], F16)
        gate_lo = sb("gate_lo", [P, C * EXPERTS], F16)
        ln_st = sb("ln_st", [P, T, 6], F32)
        ln_mv = sb("ln_mv", [P, T, 2], F32)
        ln_sd = sb("ln_sd", [P, T], F32)
        ln_r = sb("ln_r", [P, T], F32)
        row_sum = sb("row_sum", [P, T], F32)
        row_term = sb("row_term", [P, T], F32)
        table = sb("table", [P, 2], F32)
        sumsq = sb("sumsq", [P, 2, REP], F32)
        rms = sb("rms", [P, 2, REP], F32)
        inv_rms = sb("inv_rms", [P, 2, REP], F32)
        nmax = sb("nmax", [P, 4], F32)
        psum_p = sb("psum_p", [P, 4], F32)
        inv_p = sb("inv_p", [P, 4], F32)
        lg = sb("lg", [P, T, EXPERTS], F32)
        top = sb("top", [P, T], F32)
        cand = sb("cand", [P, T, EXPERTS], F32)
        first = sb("first", [P, T], F32)
        onehot = sb("onehot", [P, T, EXPERTS], F32)
        choice_b = at(148, T * EXPERTS, BF16).rearrange("p (t e) -> p t e", t=T)
        below = at(149, T * (EXPERTS + 1), BF16).rearrange("p (t e) -> p t e", t=T)
        place = at(150, T, F32)
        starts = at(151, EXPERTS + 1, F32)
        passed = at(152, EXPERTS - 1, F32)
        step_e = at(153, STEPS, F32)
        step_key = at(154, STEPS, F32)
        tile_key = at(155, T, F32)
        step_mask = at(156, STEPS, F32)
        step_e_int = at(157, STEPS, I32)
        compare = at(158, STEPS * EXPERTS, F32)

        bank = [ctx.enter_context(nc.psum_tensor(f"bank{i}", [P, 512], F32)) for i in range(8)]

        const_in = sem("const_in")
        eps_set = sem("eps_set")
        x_loaded = sem("x_loaded")
        start_in = [sem(f"start_in{c}") for c in range(C)]
        nat_loaded = [sem(f"nat_loaded{b}") for b in range(B)]
        mask_loaded = sem("mask_loaded")
        bias_loaded = sem("bias_loaded")
        ring_in = [sem("ring_in0"), sem("ring_in1")]
        ffn_in = [sem("ffn_in0"), sem("ffn_in1")]
        out_stored = sem("out_stored")
        cst_ready = sem("cst_ready")
        dve_step = sem("dve_step")
        pool_step = sem("pool_step")
        cut_hi = sem("cut_hi")
        cut_lo = sem("cut_lo")
        ln_stats = sem("ln_stats")
        ln_std = sem("ln_std")
        ln_rstd = sem("ln_rstd")
        xn_ready = sem("xn_ready")
        xT_turned = sem("xT_turned")
        xT_cut_hi = sem("xT_cut_hi")
        xT_cut_lo = sem("xT_cut_lo")
        x_scaled = sem("x_scaled")
        nat_scaled = sem("nat_scaled")
        q1_ready = sem("q1_ready")
        q2_ready = sem("q2_ready")
        q1_turned = sem("q1_turned")
        q1T_ready = sem("q1T_ready")
        col_sum = sem("col_sum")
        cross_done = sem("cross_done")
        cross_used = sem("cross_used")
        n_proj = sem("n_proj")
        n_square = sem("n_square")
        n_rms = sem("n_rms")
        n_inv = sem("n_inv")
        n_unit = sem("n_unit")
        n_turned = sem("n_turned")
        n_hi = sem("n_hi")
        n_lo = sem("n_lo")
        v_proj = sem("v_proj")
        v_cut_hi = sem("v_cut_hi")
        v_cut_lo = sem("v_cut_lo")
        w13_nibbles = sem("w13_nibbles")
        w2_nibbles = sem("w2_nibbles")
        w13_float = sem("w13_float")
        w2_float = sem("w2_float")
        w13_scaled = sem("w13_scaled")
        w2_scaled = sem("w2_scaled")
        w13_cut_hi = sem("w13_cut_hi")
        w13_cut_lo = sem("w13_cut_lo")
        w2_cut_hi = sem("w2_cut_hi")
        w2_cut_lo = sem("w2_cut_lo")
        ab_done = sem("ab_done")
        silu_a = sem("silu_a")
        h_ready = sem("h_ready")
        h_cut_hi = sem("h_cut_hi")
        h_cut_lo = sem("h_cut_lo")
        ffn_tile = sem("ffn_tile")
        ffn_out = sem("ffn_out")
        scored = sem("scored")
        masked = sem("masked")
        exped = sem("exped")
        inverted = sem("inverted")
        p_ready = sem("p_ready")
        p_turned = sem("p_turned")
        p_hi = sem("p_hi")
        p_lo = sem("p_lo")
        pv_done = sem("pv_done")
        o_hi = sem("o_hi")
        o_lo = sem("o_lo")
        o_group = sem("o_group")
        o_out = sem("o_out")
        logits = sem("logits")
        chosen = sem("chosen")
        choice_turned = sem("choice_turned")
        choice_T = sem("choice_T")
        sort_loaded = sem("sort_loaded")
        xn_hi_cut = sem("xn_hi_cut")
        xn_lo_cut = sem("xn_lo_cut")
        counted = sem("counted")
        perm_ready = sem("perm_ready")
        perm_turned = sem("perm_turned")
        permT_ready = sem("permT_ready")
        sort_hi = sem("sort_hi")
        sort_lo = sem("sort_lo")
        xs_hi_ready = sem("xs_hi_ready")
        xs_lo_ready = sem("xs_lo_ready")
        steps_ready = sem("steps_ready")
        ys_zero = sem("ys_zero")
        ys_hi_cut = sem("ys_hi_cut")
        ys_lo_cut = sem("ys_lo_cut")
        moe_out = sem("moe_out")
        result = sem("result")
        e_unit = sem("e_unit")
        e_added = sem("e_added")

        def wait(eng, s, count):
            if not (isinstance(count, int) and count <= 0):
                eng.wait_ge(s, count)

        def chunks(a):
            return a.rearrange("p (c n) -> p c n", c=C)

        def cut_target(item):
            if item in (0, 2):
                b = item // 2
                return cT_hi[:, :, b * S2:(b + 1) * S2], cT_lo[:, :, b * S2:(b + 1) * S2]
            return chunks(wk_hi[:, item // 2, :]), chunks(wk_lo[:, item // 2, :])

        block = ctx.enter_context(nc.Block())

        @block.sync
        def _(sp):

            def load_item(r, slot):
                sp.wait_ge(cut_lo, 2 * C if isinstance(r, int) and r < 4 else C * (r - 1))
                sp.dma_start(ring[:, slot, :], stream[r]).then_inc(ring_in[slot], 16)

            def load_ffn(j, par):
                wait(sp, w2_scaled, j - 1)
                sp.dma_start(raw_int[par], ffn_int[j]).then_inc(ffn_in[par], 16)
                sp.dma_start(raw_sc[par], ffn_scale[j]).then_inc(ffn_in[par], 16)

            for c in range(C):
                for r in range(2):
                    sp.dma_start(ring[:, r, c * 512:(c + 1) * 512],
                                 stream[r][:, c * 512:(c + 1) * 512]).then_inc(start_in[c], 16)
            sp.dma_start(small[:], small_in).then_inc(const_in, 16)
            sp.dma_start(shift[:], shift_in).then_inc(const_in, 16)
            sp.dma_start(ident[:], ident_in).then_inc(const_in, 16)
            sp.dma_start(x_res, x_in.rearrange("(t p) d -> p t d", p=P)).then_inc(x_loaded, 16)
            load_item(2, 0)
            load_item(3, 1)
            for b in range(B):
                sp.dma_start(nat[:, b, :], nat_in[b]).then_inc(nat_loaded[b], 16)
            load_ffn(0, 0)
            load_ffn(1, 1)
            for r in range(4, 8):
                load_item(r, r % 2)
            with sp.Fori(1, HT // 2) as m:
                load_ffn(2 * m, 0)
                load_ffn(2 * m + 1, 1)
            load_ffn(HT - 1, 0)
            sp.wait_ge(w2_scaled, HT - 1)
            sp.dma_start(mask, mask_in.rearrange("(q p) n -> p q n", p=P)).then_inc(mask_loaded, 16)
            with sp.Fori(4, 9) as m:
                load_item(2 * m, 0)
                load_item(2 * m + 1, 1)
            sp.wait_ge(masked, 8 * G)
            sp.wait_ge(pv_done, 2 * G)
            sp.dma_start(bias_f, bias_in).then_inc(bias_loaded, 16)
            sp.dma_start(sort_c, sort_in).then_inc(sort_loaded, 16)
            with sp.Fori(9, ITEMS // 2) as m:
                load_item(2 * m, 0)
                load_item(2 * m + 1, 1)
            for t in range(T):
                sp.wait_ge(result, t + 1)
                sp.dma_start(out[t * P:(t + 1) * P, :], x_res[:, t, :]).then_inc(out_stored, 16)
            sp.wait_ge(out_stored, 16 * T)

        @block.gpsimd
        def _(pool):
            steps = [0]

            def then(ins):
                steps[0] += 1
                ins.then_inc(pool_step, 1)
                pool.wait_ge(pool_step, steps[0])

            pool.wait_ge(cst_ready, 1)
            pool.wait_ge(ln_rstd, 1)
            for t in range(T):
                then(nc.gpsimd.tensor_scalar(xn[:, t, :], x_res[:, t, :], ln_mv[:, t, 0:1], ln_r[:, t:t + 1],
                                             ALU.subtract, ALU.mult))
                nc.gpsimd.tensor_scalar(xn[:, t, :], xn[:, t, :], cst[:, 0:1], small[:, 1:2],
                                        ALU.mult, ALU.add).then_inc(x_scaled, 1)
            for b in range(B):
                pool.wait_ge(nat_loaded[b], 16)
                raw = nat[:, b, :]
                then(nc.gpsimd.tensor_scalar(raw, raw, cst[:, 1:2], small[:, 3:4], ALU.mult, ALU.add))
                nc.gpsimd.tensor_scalar(raw, raw, 255.0, 0.0, ALU.min, ALU.max).then_inc(nat_scaled, 1)

            def scale_w2(j, par):
                pool.wait_ge(w2_float, j + 1)
                nc.gpsimd.tensor_tensor(w2_f[par], w2_f[par], raw_sc[par][:, 1024:1536], ALU.mult).then_inc(
                    w2_scaled, 1)

            def scale_w13(j, par):
                pool.wait_ge(ffn_in[par], 16 * (j + 2 - par))
                pool.wait_ge(w13_float, j + 1)
                nc.gpsimd.tensor_tensor(w13_f[par], w13_f[par], raw_sc[par][:, 0:1024], ALU.mult).then_inc(
                    w13_scaled, 1)

            scale_w13(0, 0)
            scale_w2(0, 0)
            scale_w13(1, 1)
            with pool.Fori(1, HT // 2) as m:
                scale_w2(2 * m - 1, 1)
                scale_w13(2 * m, 0)
                scale_w2(2 * m, 0)
                scale_w13(2 * m + 1, 1)
            scale_w2(HT - 2, 1)
            scale_w13(HT - 1, 0)
            scale_w2(HT - 1, 0)

            def normalise(k, u):
                pool.wait_ge(inverted, k + 1)
                nc.gpsimd.tensor_tensor(xn[:, u % 4, :], xn[:, u % 4, :],
                                        inv_p[:, u % 4:u % 4 + 1].broadcast_to([P, S2]),
                                        ALU.mult).then_inc(p_ready, 1)

            with pool.Fori(0, G) as g:
                for u in range(8):
                    normalise(8 * g + u, u)

            pool.wait_ge(o_out, T)
            nc.gpsimd.memset(ys, 0.0).then_inc(ys_zero, 1)
            for t in range(T):
                pool.wait_ge(xn_hi_cut, t + 1)
                nc.gpsimd.tensor_tensor(xn_lo[:, t, :], xn[:, t, :], xn_hi[:, t, :], ALU.subtract).then_inc(
                    xn_lo_cut, 1)

        @block.scalar
        def _(act):
            def cut(r, par, target, scale, pieces=range(C)):
                for p in pieces:
                    if p == 0:
                        act.wait_ge(ring_in[par], 8 * (r - par))
                    nc.scalar.activation(target[:, p, :], chunks(ring[:, par, :])[:, p, :], ACT.Copy,
                                         scale=scale).then_inc(cut_hi, 1)

            def layer_norm_std(stage, t0, t1):
                act.wait_ge(ln_stats, T * stage + t1)
                nc.scalar.activation(ln_sd[:, t0:t1], ln_mv[:, t0:t1, 1], ACT.Sqrt, bias=eps[:]).then_inc(ln_std, 1)

            def turned_x(stage, tiles=range(T)):
                for t in tiles:
                    act.wait_ge(xT_turned, T * (stage - 1) + t + 1)
                    nc.scalar.activation(xT_hi[:, :, t * P:(t + 1) * P],
                                         bank[TURN_BANKS[stage][t]][:].rearrange("p (c n) -> p c n", c=C),
                                         ACT.Copy).then_inc(xT_cut_hi, 1)

            def norm_square(n, par, square, source):
                act.wait_ge(n_proj, n + 1)
                wait(act, n_inv, n - 1)
                for h in range(REP):
                    nc.scalar.activation(square[:, par, h * HD:(h + 1) * HD], source[:, h * HD:(h + 1) * HD],
                                         ACT.Square, scale=1.0 / W_SCALE,
                                         accum_out=sumsq[:, par, h:h + 1]).then_inc(n_square, 1)
                act.wait_ge(n_square, REP * (n + 1))
                nc.scalar.activation(rms[:, par, :], sumsq[:, par, :], ACT.Sqrt, bias=eps[:],
                                     scale=1.0 / HD).then_inc(n_rms, 1)

            def norm_hi(n, par, target, weight):
                act.wait_ge(n_turned, n + 1)
                nc.scalar.activation(target, bank[2 + par][:].rearrange("p (h n) -> p h n", h=REP), ACT.Copy,
                                     scale=weight).then_inc(n_hi, 1)

            def first_cut(p):
                act.wait_ge(start_in[p], 32)
                for r in range(2):
                    nc.scalar.activation(cut_target(r)[0][:, p, :], chunks(ring[:, r, :])[:, p, :], ACT.Copy,
                                         scale=[1.0, W_SCALE][r]).then_inc(cut_hi, 1)

            act.wait_ge(eps_set, 1)
            nc.scalar.activation(table[:, 0:1], eps[:], ACT.Sqrt)
            for p in range(C):
                first_cut(p)

            def k_tail(half, i, par):
                norm_hi(8 * half + i, par, kT_hi[:, REP * half:REP * half + REP, bass.ds(i * P, P)], cst[:, 11:12])

            def k_step(half, i, par):
                norm_square(8 * half + i, par, k_square, bank[par])
                if not (isinstance(i, int) and i < 2):
                    k_tail(half, i - 2, par)
                elif half:
                    k_tail(0, 6 + i, par)

            def v_cut_piece(i):
                piece = bass.ds(i * 512, 512)
                nc.scalar.activation(wv_flat[0][:, piece], ring_flat[:, piece], ACT.Copy,
                                     scale=W_SCALE).then_inc(cut_hi, 1)

            for i in range(8):
                if i == 2:
                    act.wait_ge(cst_ready, 1)
                if i == 3:
                    layer_norm_std(0, 0, T)
                for r, pieces in START_PIECES[i]:
                    cut(r, r % 2, cut_target(r)[0], [1.0, W_SCALE][r % 2], pieces)
                k_step(0, i, i % 2)
            for slot in range(2):
                act.wait_ge(ring_in[slot], 32)
            for u in range(2):
                k_step(1, u, u)
                v_cut_piece(u)
            with act.Fori(1, 4) as m:
                for u in range(2):
                    k_step(1, 2 * m + u, u)
                    v_cut_piece(2 * m + u)
            k_tail(1, 6, 0)
            k_tail(1, 7, 1)
            act.wait_ge(const_in, 48)
            nc.scalar.activation(gate_hi[:], small[:, 24:56], ACT.Copy, scale=W_SCALE).then_inc(cst_ready, 1)
            def v_step(half, i, par):
                act.wait_ge(v_proj, 8 * half + i + 1)
                if half == 0 and i == 0:
                    act.wait_ge(q2_ready, B)
                nc.scalar.activation(v_hi[:, REP * half:REP * half + REP, bass.ds(i * P, P)],
                                     bank[V_BANKS[half][par]][:].rearrange("p (h n) -> p h n", h=REP), ACT.Copy,
                                     scale=1.0 / W_SCALE).then_inc(v_cut_hi, 1)

            v_step(0, 0, 0)
            for t in range(T):
                if t + 1 < T:
                    v_step(0, t + 1, t + 1)
                layer_norm_std(1, t, t + 1)

            def w13_floats(j, par):
                act.wait_ge(w13_nibbles, j + 1)
                wait(act, w13_cut_lo, j - 1)
                nc.scalar.activation(w13_f[par], nib[:, 0:1024], ACT.Copy).then_inc(w13_float, 1)

            def w2_floats(j, par):
                act.wait_ge(w2_nibbles, j + 1)
                wait(act, w2_cut_lo, j - 1)
                nc.scalar.activation(w2_f[par], nib[:, 1024:1536], ACT.Copy).then_inc(w2_float, 1)

            def w13_hi_part(j, par):
                act.wait_ge(w13_scaled, j + 1)
                wait(act, ab_done, j - 1)
                nc.scalar.activation(w13_hi[par], w13_f[par], ACT.Copy, scale=W_SCALE).then_inc(w13_cut_hi, 1)

            def w2_hi_part(j, par):
                act.wait_ge(w2_scaled, j + 1)
                wait(act, ffn_tile, j - 1)
                nc.scalar.activation(w2_hi[par], w2_f[par], ACT.Copy, scale=W_SCALE).then_inc(w2_cut_hi, 1)

            def weights_in(j, par):
                if not (isinstance(j, int) and not 0 <= j + 2 < HT):
                    w2_floats(j + 2, par)
                if not (isinstance(j, int) and j + 3 >= HT):
                    w13_floats(j + 3, 1 - par)

            def weights_cut(j, par):
                if not (isinstance(j, int) and not 0 <= j + 2 < HT):
                    w13_hi_part(j + 2, par)
                if not (isinstance(j, int) and not 0 <= j + 1 < HT):
                    w2_hi_part(j + 1, 1 - par)

            weights_in(-3, 1)
            for i in range(4, 8):
                v_step(0, i, i % 4)
            turned_x(1)
            for i in range(8):
                v_step(1, i, i % 4)
                if i in (0, 3):
                    weights_in(i // 3 - 2, i // 3)
                if i in (2, 5):
                    weights_cut(i // 3 - 2, i // 3)

            def q_cut(kv, par, pieces=range(C)):
                if 0 in pieces and not (isinstance(kv, int) and kv < 2):
                    act.wait_ge(n_proj, 16 + 4 * kv - 4)
                cut(WQ + kv, par, chunks(wq_hi[par]), W_SCALE, pieces)

            def ffn_step(j, par):
                weights_in(j, par)
                act.wait_ge(ab_done, j + 1)
                wait(act, h_ready, j - 1)
                nc.scalar.activation(xn[:, par, :], bank[2 * par][:], ACT.Silu, scale=1.0 / W_SCALE).then_inc(silu_a, 1)
                act.wait_ge(h_ready, j + 1)
                wait(act, ffn_tile, j - 1)
                nc.scalar.activation(h_hi[par], xn[:, 2 + par, :], ACT.Copy).then_inc(h_cut_hi, 1)
                weights_cut(j, par)

            ffn_step(0, 0)
            ffn_step(1, 1)
            with act.Fori(1, 4) as m:
                ffn_step(2 * m, 0)
                ffn_step(2 * m + 1, 1)
            for j in range(8, HT):
                ffn_step(j, j % 2)
                if j >= 8 and j < 10:
                    q_cut(j - 8, j - 8)

            def q_target(flat, kv, t):
                base = kv * (B * REP * S) + (t // QT) * (REP * S)
                return flat[:, bass.ds(base, REP * S)].rearrange("p (h n) -> p h n", h=REP)[
                    :, :, (t % QT) * P:(t % QT + 1) * P]

            def q_tail(kv, t):
                norm_hi(16 + 4 * kv + t, t % 2, q_target(q_hi, kv, t), cst[:, 10:11])

            def o_cut(kv, par, pieces=range(C)):
                wait(act, o_group, kv - 1)
                first = isinstance(kv, int) and kv < 2
                cut(WO + kv if first else 2 * kv + 13, par if first else 1, chunks(wo_hi[par]), W_SCALE, pieces)

            def q_group(kv, par):
                for t in range(T):
                    if isinstance(kv, int) and kv + 1 >= KV:
                        o_cut(0, 0, Q_PIECES[t])
                    elif not (isinstance(kv, int) and kv == 0):
                        q_cut(kv + 1, 1 - par, Q_PIECES[t])
                    if not (isinstance(kv, int) and kv == 0 and t < 2):
                        norm_square(16 + 4 * kv + t, t % 2, q_square, bank[Q_BANKS[t]])
                    if t >= 2:
                        q_tail(kv, t - 2)
                    elif not (isinstance(kv, int) and kv == 0):
                        q_tail(kv - 1, T + t - 2)

            for t in range(T):
                layer_norm_std(2, t, t + 1)
                if t == T - 1:
                    for n in range(2):
                        norm_square(16 + n, n, q_square, bank[Q_BANKS[n]])
                turned_x(2, [t])
            q_group(0, 0)
            q_group(1, 1)
            with act.Fori(1, 3) as m:
                q_group(2 * m, 0)
                q_group(2 * m + 1, 1)
            q_group(6, 0)
            q_group(7, 1)
            q_tail(7, T - 2)
            nc.scalar.activation(table[:, 1:2], eps[:], ACT.Exp)
            q_tail(7, T - 1)

            def o_hi_part(m, pair):
                act.wait_ge(pv_done, m + 1)
                nc.scalar.activation(q_hi[:, bass.ds(m * 512, 512)], bank[6 + pair][:], ACT.Copy,
                                     scale=O_SCALE / P_SCALE).then_inc(o_hi, 1)

            def attend(g, u):
                k = 8 * g + u
                first, last = isinstance(g, int) and g == 0, isinstance(g, int) and g == G
                if not (first and u < 3) and not (last and u >= 3):
                    w = (u + 5) % 8
                    act.wait_ge(p_turned, k - 2)
                    if u >= 3:
                        wait(act, pv_done, 2 * g + w // 4 - 1)
                    else:
                        wait(act, pv_done, 2 * g - 2)
                    pair, h, qt = w // 4, w // 2 % 2, w % 2
                    nc.scalar.activation(pT_hi[pair][:, :, h * S + qt * P:h * S + (qt + 1) * P],
                                         bank[4 + w % 2][:].rearrange("p (k n) -> p k n", k=KT),
                                         ACT.Copy, scale=P_SCALE).then_inc(p_hi, 1)
                if not last:
                    act.wait_ge(masked, k + 1)
                    nc.scalar.activation(xn[:, u % 4, :], xn[:, u % 4, :], ACT.Exp, bias=nmax[:, u % 4:u % 4 + 1],
                                         scale=-1.0, accum_out=psum_p[:, u % 4:u % 4 + 1]).then_inc(exped, 1)
                if u == 0 and not (isinstance(g, int) and g < 2):
                    o_hi_part(2 * g - 3, 1)
                if u == 4 and not first:
                    o_hi_part(2 * g - 2, 0)

            for u in range(8):
                attend(0, u)
            for u in range(8):
                attend(1, u)
            with act.Fori(2, G) as g:
                for u in range(8):
                    attend(g, u)
            for u in range(8):
                attend(G, u)
                if u >= C:
                    o_cut(1, 1, [u - C])
            o_hi_part(2 * G - 1, 1)

            def e_cut(j, r, slot):
                cut(r, slot, chunks(we_hi[:, bass.ds(j * ITEM, ITEM)]), W_SCALE)

            act.wait_ge(scored, 8 * G)
            with act.Fori(1, KV // 2) as m:
                e_cut(2 * m - 2, 4 * m + 12, 0)
                o_cut(2 * m, 0)
                e_cut(2 * m - 1, 4 * m + 14, 0)
                o_cut(2 * m + 1, 1)
            e_cut(EXPERTS - 2, ITEMS - 2, 0)
            e_cut(EXPERTS - 1, ITEMS - 1, 1)
            def xn_hi_part(t):
                act.wait_ge(xn_ready, 2 * T + t + 1)
                nc.scalar.activation(xn_hi[:, t, :], xn[:, t, :], ACT.Copy).then_inc(xn_hi_cut, 1)

            layer_norm_std(3, 0, 1)
            layer_norm_std(3, 1, 2)
            for t in range(T):
                if t == 2:
                    layer_norm_std(3, 2, 3)
                    layer_norm_std(3, 3, 4)
                turned_x(3, [t])
                if t < 2:
                    xn_hi_part(t)
            xn_hi_part(2)
            xn_hi_part(3)

            for c in range(C):
                act.wait_ge(sort_hi, c + 1)
                nc.scalar.activation(xs_hi[:, c, :], bank[4 + c][:], ACT.Copy).then_inc(xs_hi_ready, 1)
            for t in range(T):
                act.wait_ge(perm_turned, t + 1)
                nc.scalar.activation(permT[:, t, :], bank[4 + t][:].bitcast(F16)[:, 0:512], ACT.Copy).then_inc(
                    permT_ready, 1)
            for t in range(T):
                act.wait_ge(e_added, EXPERTS + t)
                nc.scalar.activation(ys_hi[:, t, :], ys[:, t * D:(t + 1) * D], ACT.Copy).then_inc(ys_hi_cut, 1)

        @block.vector
        def _(dve):
            steps = [0]

            def then(ins):
                steps[0] += 1
                ins.then_inc(dve_step, 1)
                dve.wait_ge(dve_step, steps[0])

            def cut(c, par, hi, lo, scale, pieces=range(C)):
                for p in pieces:
                    dve.wait_ge(cut_hi, C * c + p + 1)
                    nc.vector.scalar_tensor_tensor(lo[:, p, :], chunks(ring[:, par, :])[:, p, :], scale,
                                                   hi[:, p, :], ALU.mult, ALU.subtract).then_inc(cut_lo, 1)

            def layer_norm_stats(t):
                then(nc.vector.bn_stats(ln_st[:, t, :], x_res[:, t, :]))
                nc.vector.bn_aggr(ln_mv[:, t, :], ln_st[:, t, :]).then_inc(ln_stats, 1)

            def layer_norm_out(stage, t):
                dve.wait_ge(ln_std, 1 + T * (stage - 1) + t + 1)
                then(nc.vector.reciprocal(ln_r[:, t:t + 1], ln_sd[:, t:t + 1]))
                nc.vector.tensor_scalar(xn[:, t, :], x_res[:, t, :], ln_mv[:, t, 0:1], ln_r[:, t:t + 1],
                                        ALU.subtract, ALU.mult).then_inc(xn_ready, 1)

            def turned_x(stage, tiles=range(T)):
                for t in tiles:
                    dve.wait_ge(xT_cut_hi, T * (stage - 1) + t + 1)
                    nc.vector.tensor_tensor(xT_lo[:, :, t * P:(t + 1) * P],
                                            bank[TURN_BANKS[stage][t]][:].rearrange("p (c n) -> p c n", c=C),
                                            xT_hi[:, :, t * P:(t + 1) * P], ALU.subtract).then_inc(xT_cut_lo, 1)

            def norm_scale(n, par, unit, source):
                dve.wait_ge(n_rms, n + 1)
                nc.vector.reciprocal(inv_rms[:, par, :], rms[:, par, :]).then_inc(n_inv, 1)
                dve.wait_ge(n_inv, n + 1)
                wait(dve, n_turned, n - 1)
                nc.vector.scalar_tensor_tensor(
                    unit[:, par, :].rearrange("p (h n) -> p h n", h=REP),
                    source[:].rearrange("p (h n) -> p h n", h=REP), 1.0 / W_SCALE,
                    inv_rms[:, par, :].unsqueeze(2).broadcast_to([P, REP, HD]), ALU.mult,
                    ALU.mult).then_inc(n_unit, 1)

            def norm_lo(n, par, hi, lo, weight):
                dve.wait_ge(n_hi, n + 1)
                nc.vector.scalar_tensor_tensor(lo, bank[2 + par][:].rearrange("p (h n) -> p h n", h=REP), weight,
                                               hi, ALU.mult, ALU.subtract).then_inc(n_lo, 1)

            nc.vector.memset(eps[:], EPS).then_inc(eps_set, 1)
            nc.vector.memset(ones_b[:], 1.0)
            for p in range(C):
                for r in range(2):
                    hi, lo = cut_target(r)
                    dve.wait_ge(cut_hi, 2 * p + r + 1)
                    nc.vector.scalar_tensor_tensor(lo[:, p, :], chunks(ring[:, r, :])[:, p, :], [1.0, W_SCALE][r],
                                                   hi[:, p, :], ALU.mult, ALU.subtract).then_inc(cut_lo, 1)
            def k_tail(half, i, par):
                hs = slice(REP * half, REP * half + REP)
                norm_lo(8 * half + i, par, kT_hi[:, hs, bass.ds(i * P, P)], kT_lo[:, hs, bass.ds(i * P, P)],
                        cst[:, 11:12])

            def k_step(half, i, par):
                norm_scale(8 * half + i, par, k_unit, bank[par])
                if not (isinstance(i, int) and i < 2):
                    k_tail(half, i - 2, par)
                elif half:
                    k_tail(0, 6 + i, par)

            def v_cut_piece(i):
                piece = bass.ds(i * 512, 512)
                dve.wait_ge(cut_hi, C * WV + i + 1)
                nc.vector.scalar_tensor_tensor(wv_flat[1][:, piece], ring_flat[:, piece], W_SCALE,
                                               wv_flat[0][:, piece], ALU.mult, ALU.subtract).then_inc(cut_lo, 1)

            def quantise_tokens(t):
                dve.wait_ge(x_scaled, t + 1)
                then(nc.vector.tensor_scalar(xn[:, t, :], xn[:, t, :], 255.0, 0.0, ALU.min, ALU.max))
                then(nc.vector.tensor_scalar(q1[:, t, :], xn[:, t, :], ROUND, ROUND + MID, ALU.add,
                                             ALU.subtract))
                nc.vector.tensor_reduce(row_sum[:, t:t + 1], q1[:, t, :], AX.X, ALU.add).then_inc(q1_ready, 1)

            def quantise_context(b):
                dve.wait_ge(nat_scaled, b + 1)
                nc.vector.tensor_scalar(q2[:, b, :, :], chunks(nat[:, b, :]), ROUND, ROUND + MID,
                                        ALU.add, ALU.subtract).then_inc(q2_ready, 1)

            def turned_q1(t):
                dve.wait_ge(q1_turned, t + 1)
                nc.vector.tensor_copy(q1T[:, :, t * P:(t + 1) * P],
                                      bank[6 + t % 2][:].bitcast(BF16)[:, 0:KT * P].rearrange(
                                          "p (k n) -> p k n", k=KT)).then_inc(q1T_ready, 1)

            def constants_and_stats():
                dve.wait_ge(const_in, 48)
                nc.vector.tensor_copy(ident_b[:], ident[:])
                then(nc.vector.reciprocal(cst[:, 0:1], small[:, 0:1]))
                nc.vector.reciprocal(cst[:, 1:2], small[:, 2:3])
                nc.vector.tensor_tensor(cst[:, 2:3], small[:, 0:1], small[:, 2:3], ALU.mult)
                nc.vector.tensor_scalar(cst[:, 3:4], small[:, 1:2], -1.0, MID, ALU.mult, ALU.add)
                then(nc.vector.tensor_scalar(cst[:, 4:5], small[:, 3:4], -1.0, MID, ALU.mult, ALU.add))
                then(nc.vector.tensor_tensor(cst[:, 5:6], cst[:, 3:4], cst[:, 4:5], ALU.mult))
                then(nc.vector.tensor_scalar(cst[:, 5:6], cst[:, 5:6], float(S2), None, ALU.mult))
                nc.vector.tensor_scalar(cst[:, 10:12], small[:, 4:6], float(HD) ** -0.25, None,
                                        ALU.mult).then_inc(cst_ready, 1)
                dve.wait_ge(x_loaded, 16)
                layer_norm_stats(0)

            def first_rstd():
                dve.wait_ge(ln_std, 1)
                then(nc.vector.reciprocal(ln_r[:], ln_sd[:]))
                then(nc.vector.tensor_tensor(first[:], ln_r[:], ln_r[:], ALU.mult))
                then(nc.vector.scalar_tensor_tensor(first[:], ln_mv[:, :, 1], eps[:], first[:], ALU.add, ALU.mult))
                then(nc.vector.tensor_scalar(first[:], first[:], -0.5, 1.5, ALU.mult, ALU.add))
                nc.vector.tensor_tensor(ln_r[:], ln_r[:], first[:], ALU.mult).then_inc(ln_rstd, 1)

            for i in range(8):
                if i == 0:
                    constants_and_stats()
                if i == 1:
                    layer_norm_stats(1)
                    layer_norm_stats(2)
                if i == 3:
                    layer_norm_stats(3)
                    first_rstd()
                for r, pieces in START_PIECES[i]:
                    hi, lo = cut_target(r)
                    cut(r, r % 2, hi, lo, [1.0, W_SCALE][r % 2], pieces)
                if i >= 5:
                    quantise_tokens(i - 5)
                k_step(0, i, i % 2)
            quantise_tokens(3)
            for u in range(2):
                k_step(1, u, u)
                v_cut_piece(u)
            with dve.Fori(1, 3) as m:
                for u in range(2):
                    k_step(1, 2 * m + u, u)
                    v_cut_piece(2 * m + u)
            for i in range(6, 8):
                k_step(1, i, i % 2)
                v_cut_piece(i)
                quantise_context(i - 6)
            k_tail(1, 6, 0)
            turned_q1(0)
            turned_q1(1)
            k_tail(1, 7, 1)
            turned_q1(2)
            turned_q1(3)

            def v_step(half, i, par):
                hs = slice(REP * half, REP * half + REP)
                dve.wait_ge(v_cut_hi, 8 * half + i + 1)
                nc.vector.scalar_tensor_tensor(v_lo[:, hs, bass.ds(i * P, P)],
                                               bank[V_BANKS[half][par]][:].rearrange("p (h n) -> p h n", h=REP),
                                               1.0 / W_SCALE,
                                               v_hi[:, hs, bass.ds(i * P, P)], ALU.mult,
                                               ALU.subtract).then_inc(v_cut_lo, 1)

            then(nc.vector.tensor_scalar(row_term[:], row_sum[:], cst[:, 4:5], cst[:, 5:6], ALU.mult, ALU.add))
            for b in range(B):
                dve.wait_ge(col_sum, b + 1)
                then(nc.vector.tensor_scalar(col_term[:, b, :], bank[4 + b][:], cst[:, 3:4], None, ALU.mult))
            for t in range(T + 1):
                if t < T:
                    dve.wait_ge(cross_done, t + 1)
                    ins = nc.vector.scalar_tensor_tensor(cross[:, t % 2, :], bank[CROSS_BANKS[t]][:],
                                                         row_term[:, t:t + 1], col_term[:, t // QT, :],
                                                         ALU.add, ALU.add)
                    ins.then_inc(cross_used, 1)
                    dve.wait_ge(cross_used, t + 1)
                    then(nc.vector.scalar_tensor_tensor(x_res[:, t, :], cross[:, t % 2, :], cst[:, 2:3],
                                                        x_res[:, t, :], ALU.mult, ALU.add))
                    layer_norm_stats(t)
                if t:
                    v_step(0, t - 1, t - 1)
                    layer_norm_out(1, t - 1)

            def unpack_w13(j, par):
                dve.wait_ge(ffn_in[par], 16 * (j + 2 - par))
                wait(dve, w13_float, j)
                words = raw_int[par][:, 0:512].rearrange("p (m h) -> p m h", m=4)
                out13 = nib[:, 0:1024].rearrange("p (m b h) -> p m b h", m=4, b=2)
                for b in range(2):
                    ins = nc.vector.tensor_scalar(out13[:, :, b, :], words, shift[:, 4 + b:5 + b], 28,
                                                  ALU.logical_shift_left, ALU.arith_shift_right)
                ins.then_inc(w13_nibbles, 1)

            def unpack_w2(j, par):
                wait(dve, w2_float, j)
                out2 = nib[:, 1024:1536].rearrange("p (q r) -> p q r", r=4)
                for r in range(4):
                    ins = nc.vector.tensor_scalar(out2[:, :, r], raw_int[par][:, 512 + 128 * r:640 + 128 * r],
                                                  shift[:, r:r + 1], 28, ALU.logical_shift_left,
                                                  ALU.arith_shift_right)
                ins.then_inc(w2_nibbles, 1)

            def w13_lo_part(j, par):
                dve.wait_ge(w13_cut_hi, j + 1)
                nc.vector.scalar_tensor_tensor(w13_lo[par], w13_f[par], W_SCALE, w13_hi[par], ALU.mult,
                                               ALU.subtract).then_inc(w13_cut_lo, 1)

            def w2_lo_part(j, par):
                dve.wait_ge(w2_cut_hi, j + 1)
                nc.vector.scalar_tensor_tensor(w2_lo[par], w2_f[par], W_SCALE, w2_hi[par], ALU.mult,
                                               ALU.subtract).then_inc(w2_cut_lo, 1)

            def weights_in(j, par):
                if not (isinstance(j, int) and not 0 <= j + 2 < HT):
                    unpack_w2(j + 2, par)
                if not (isinstance(j, int) and j + 3 >= HT):
                    unpack_w13(j + 3, 1 - par)

            def weights_cut(j, par):
                if not (isinstance(j, int) and not 0 <= j + 2 < HT):
                    w13_lo_part(j + 2, par)
                if not (isinstance(j, int) and not 0 <= j + 1 < HT):
                    w2_lo_part(j + 1, 1 - par)

            weights_in(-3, 1)
            for i in range(4, 8):
                v_step(0, i, i % 4)
            turned_x(1)
            for i in range(8):
                v_step(1, i, i % 4)
                if i in (0, 3):
                    weights_in(i // 3 - 2, i // 3)
                if i in (2, 5):
                    weights_cut(i // 3 - 2, i // 3)

            def q_cut(kv, par, pieces=range(C)):
                cut(WQ + kv, par, chunks(wq_hi[par]), chunks(wq_lo[par]), W_SCALE, pieces)

            def ffn_step(j, par):
                weights_in(j, par)
                dve.wait_ge(silu_a, j + 1)
                wait(dve, h_cut_lo, j - 1)
                nc.vector.scalar_tensor_tensor(xn[:, 2 + par, :], xn[:, par, :], 1.0 / W_SCALE,
                                               bank[2 * par + 1][:], ALU.mult, ALU.mult).then_inc(h_ready, 1)
                dve.wait_ge(h_cut_hi, j + 1)
                nc.vector.tensor_tensor(h_lo[par], xn[:, 2 + par, :], h_hi[par], ALU.subtract).then_inc(h_cut_lo, 1)
                weights_cut(j, par)

            ffn_step(0, 0)
            ffn_step(1, 1)
            with dve.Fori(1, 4) as m:
                ffn_step(2 * m, 0)
                ffn_step(2 * m + 1, 1)
            for j in range(8, HT):
                ffn_step(j, j % 2)
                if j >= 8 and j < 10:
                    q_cut(j - 8, j - 8)

            def residual(stage, done, banks, scale):
                lag = 1 if stage == 2 else 2
                for t in range(T + lag):
                    if t < T:
                        dve.wait_ge(done, t + 1)
                        then(nc.vector.scalar_tensor_tensor(x_res[:, t, :], banks[t][:], scale, x_res[:, t, :],
                                                            ALU.mult, ALU.add))
                        layer_norm_stats(t)
                    if stage == 2 and t == T:
                        for n in range(2):
                            norm_scale(16 + n, n, xn[:, 0:2, :], bank[Q_BANKS[n]])
                    if t >= lag:
                        turned_x(stage, [t - lag])
                    if t < T:
                        layer_norm_out(stage, t)

            residual(2, ffn_out, bank[4:8], 1.0 / W_SCALE)

            def q_target(flat, kv, t):
                base = kv * (B * REP * S) + (t // QT) * (REP * S)
                return flat[:, bass.ds(base, REP * S)].rearrange("p (h n) -> p h n", h=REP)[
                    :, :, (t % QT) * P:(t % QT + 1) * P]

            def q_tail(kv, t):
                norm_lo(16 + 4 * kv + t, t % 2, q_target(q_hi, kv, t), q_target(q_lo, kv, t), cst[:, 10:11])

            def o_cut(kv, par, pieces=range(C)):
                first = isinstance(kv, int) and kv < 2
                cut(WO + kv if first else 2 * kv + 13, par if first else 1, chunks(wo_hi[par]),
                    chunks(wo_lo[par]), W_SCALE, pieces)

            def q_group(kv, par):
                for t in range(T):
                    if isinstance(kv, int) and kv + 1 >= KV:
                        o_cut(0, 0, Q_PIECES[t])
                    elif not (isinstance(kv, int) and kv == 0):
                        q_cut(kv + 1, 1 - par, Q_PIECES[t])
                    if not (isinstance(kv, int) and kv == 0 and t < 2):
                        norm_scale(16 + 4 * kv + t, t % 2, xn[:, 0:2, :], bank[Q_BANKS[t]])
                    if t >= 2:
                        q_tail(kv, t - 2)
                    elif not (isinstance(kv, int) and kv == 0):
                        q_tail(kv - 1, T + t - 2)

            q_group(0, 0)
            q_group(1, 1)
            with dve.Fori(1, 3) as m:
                q_group(2 * m, 0)
                q_group(2 * m + 1, 1)
            q_group(6, 0)
            q_group(7, 1)
            q_tail(7, T - 2)

            def o_lo_part(m, pair):
                dve.wait_ge(o_hi, m + 1)
                nc.vector.scalar_tensor_tensor(q_lo[:, bass.ds(m * 512, 512)], bank[6 + pair][:],
                                               O_SCALE / P_SCALE, q_hi[:, bass.ds(m * 512, 512)], ALU.mult,
                                               ALU.subtract).then_inc(o_lo, 1)

            def attend(g, u):
                k = 8 * g + u
                first, last = isinstance(g, int) and g == 0, isinstance(g, int) and g == G
                if not (first and u < 2) and not (last and u > 1):
                    dve.wait_ge(exped, k - 1)
                    v = (u + 2) % 4
                    nc.vector.reciprocal(inv_p[:, v:v + 1], psum_p[:, v:v + 1]).then_inc(inverted, 1)
                if not last:
                    dve.wait_ge(scored, k + 1)
                    wait(dve, p_turned, k - 3)
                    if first and u == 0:
                        dve.wait_ge(mask_loaded, 16)
                    if first and u < 2:
                        dve.wait_ge(n_turned, 16 + T * KV - 1 + u)
                if not (first and u < 4) and not (last and u >= 4):
                    w = (u + 4) % 8
                    pair, h, qt = w // 4, w // 2 % 2, w % 2
                    dve.wait_ge(p_hi, k - 3)
                    cols = slice(h * S + qt * P, h * S + (qt + 1) * P)
                    nc.vector.scalar_tensor_tensor(pT_lo[pair][:, :, cols],
                                                   bank[4 + w % 2][:].rearrange("p (k n) -> p k n", k=KT), P_SCALE,
                                                   pT_hi[pair][:, :, cols], ALU.mult,
                                                   ALU.subtract).then_inc(p_lo, 1)
                if not last:
                    nc.vector.tensor_tensor_reduce(xn[:, u % 4, :], bank[u % 4][:], mask[:, u % 2, :], -1.0, BIG,
                                                   ALU.add, ALU.min, nmax[:, u % 4:u % 4 + 1]).then_inc(masked, 1)
                if u == 1 and not (isinstance(g, int) and g < 2):
                    o_lo_part(2 * g - 3, 1)
                if u == 5 and not first:
                    o_lo_part(2 * g - 2, 0)

            for u in range(8):
                attend(0, u)
                if u == 0:
                    q_tail(7, T - 1)
            for u in range(8):
                attend(1, u)
            with dve.Fori(2, G) as g:
                for u in range(8):
                    attend(g, u)
            for u in range(8):
                attend(G, u)
                if u >= C:
                    o_cut(1, 1, [u - C])
            o_lo_part(2 * G - 1, 1)

            def e_cut(j, r, slot):
                cut(r, slot, chunks(we_hi[:, bass.ds(j * ITEM, ITEM)]), chunks(we_lo[:, bass.ds(j * ITEM, ITEM)]),
                    W_SCALE)

            dve.wait_ge(pv_done, 2 * G)
            with dve.Fori(1, KV // 2) as m:
                e_cut(2 * m - 2, 4 * m + 12, 0)
                o_cut(2 * m, 0)
                e_cut(2 * m - 1, 4 * m + 14, 0)
                o_cut(2 * m + 1, 1)
            e_cut(EXPERTS - 2, ITEMS - 2, 0)
            e_cut(EXPERTS - 1, ITEMS - 1, 1)
            dve.wait_ge(cst_ready, 2)
            then(nc.vector.scalar_tensor_tensor(gate_lo[:], small[:, 24:56], W_SCALE, gate_hi[:], ALU.mult,
                                                ALU.subtract))
            dve.wait_ge(bias_loaded, 16)
            then(nc.vector.tensor_scalar(bias_hl[0], bias_f[:], 1.0, None, ALU.mult))
            nc.vector.tensor_tensor(bias_hl[1], bias_f[:], bias_hl[0], ALU.subtract)
            dve.wait_ge(sort_loaded, 16)
            nc.vector.tensor_copy(before, sort_c[:, SC_BEFORE:SC_BEFORE + P])
            nc.vector.tensor_copy(ident_h, ident[:])
            residual(3, o_out, bank[0:4], 1.0 / (W_SCALE * O_SCALE))

            def over(a, shape):
                return a.broadcast_to(shape)

            gate_bias, index = small[:, 8:16], small[:, 16:24]
            iota = sort_c[:, SC_IOTA:SC_IOTA + 512]
            te = [P, T, EXPERTS]
            dve.wait_ge(logits, T)
            then(nc.vector.scalar_tensor_tensor(lg[:], bank[0][:, 0:T * EXPERTS].rearrange("p (t e) -> p t e", t=T),
                                                1.0 / W_SCALE, over(gate_bias.unsqueeze(1), te), ALU.mult, ALU.add))
            then(nc.vector.tensor_reduce(top[:], lg[:], AX.X, ALU.max))
            then(nc.vector.tensor_tensor(cand[:], lg[:], over(top[:].unsqueeze(2), te), ALU.is_lt))
            then(nc.vector.scalar_tensor_tensor(cand[:], cand[:], float(EXPERTS), over(index.unsqueeze(1), te),
                                                ALU.mult, ALU.add))
            then(nc.vector.tensor_reduce(first[:], cand[:], AX.X, ALU.min))
            chosen_of = over(first[:].unsqueeze(2), te)
            then(nc.vector.tensor_tensor(onehot[:], over(index.unsqueeze(1), te), chosen_of, ALU.is_equal))
            nc.vector.tensor_copy(choice_b, onehot[:])
            nc.vector.tensor_tensor(below, over(iota[:, 0:EXPERTS + 1].unsqueeze(1), [P, T, EXPERTS + 1]),
                                    over(first[:].unsqueeze(2), [P, T, EXPERTS + 1]), ALU.is_gt).then_inc(chosen, 1)

            dve.wait_ge(counted, 1)
            counts = bank[1][:, 0:T * EXPERTS].rearrange("p (t e) -> p t e", t=T)
            then(nc.vector.tensor_tensor(cand[:], onehot[:], counts, ALU.mult))
            nc.vector.tensor_copy(starts, bank[1][:, T * EXPERTS:T * EXPERTS + EXPERTS + 1])
            then(nc.vector.tensor_reduce(place, cand[:], AX.X, ALU.add))
            for t in range(T):
                nc.vector.tensor_scalar(perm[:, t, :], iota, place[:, t:t + 1], None, ALU.is_equal).then_inc(
                    perm_ready, 1)
            dve.wait_ge(choice_turned, 1)
            nc.vector.tensor_copy(oneT, bank[2][0:EXPERTS, :].rearrange("e (t n) -> e t n", t=T)).then_inc(
                choice_T, 1)

            ends = starts[:, 1:EXPERTS]
            ends_past = compare[:, 0:(EXPERTS - 1) * (T - 1)].rearrange("p (e i) -> p e i", i=T - 1)
            then(nc.vector.tensor_tensor(ends_past, over(ends.unsqueeze(2), [P, EXPERTS - 1, T - 1]),
                                         over(iota.rearrange("p (i n) -> p i n", n=P)[:, 1:T, 0].unsqueeze(1),
                                              [P, EXPERTS - 1, T - 1]), ALU.is_gt))
            then(nc.vector.tensor_reduce(passed, ends_past, AX.X, ALU.add))
            then(nc.vector.tensor_tensor(passed, passed, index[:, 0:EXPERTS - 1], ALU.add))
            ce = compare[:, 0:STEPS * (EXPERTS - 1)].rearrange("p (n e) -> p n e", n=STEPS)
            shape = [P, STEPS, EXPERTS - 1]
            then(nc.vector.tensor_tensor(ce, over(passed.unsqueeze(1), shape),
                                         over(sort_c[:, SC_N:SC_N + STEPS].unsqueeze(2), shape), ALU.is_lt))
            then(nc.vector.tensor_reduce(step_e, ce, AX.X, ALU.add))
            nc.vector.tensor_copy(step_e_int, step_e).then_inc(steps_ready, 1)
            then(nc.vector.scalar_tensor_tensor(step_key, step_e, 1.0 - EXPERTS, sort_c[:, SC_N8:SC_N8 + STEPS],
                                                ALU.mult, ALU.add))
            ct = compare[:, 0:T * (EXPERTS - 1)].rearrange("p (i e) -> p i e", i=T)
            shape = [P, T, EXPERTS - 1]
            then(nc.vector.tensor_tensor(ct, over(sort_c[:, SC_PLACE:SC_PLACE + T].unsqueeze(2), shape),
                                         over(ends.unsqueeze(1), shape), ALU.is_ge))
            then(nc.vector.tensor_reduce(tile_key, ct, AX.X, ALU.add))
            then(nc.vector.tensor_tensor(tile_key, tile_key, sort_c[:, SC_TILE8:SC_TILE8 + T], ALU.add))
            cm = compare[:, 0:STEPS * T].rearrange("p (n i) -> p n i", n=STEPS)
            shape = [P, STEPS, T]
            then(nc.vector.tensor_tensor(cm, over(step_key.unsqueeze(2), shape), over(tile_key.unsqueeze(1), shape),
                                         ALU.is_equal))
            then(nc.vector.tensor_reduce(step_mask, cm, AX.X, ALU.add))
            then(nc.vector.tensor_scalar(step_mask, step_mask, 1.0 / W_SCALE, None, ALU.mult))

            for c in range(C):
                dve.wait_ge(sort_lo, c + 1)
                nc.vector.tensor_copy(xs_lo[:, c, :], bank[c][:]).then_inc(xs_lo_ready, 1)

            def ys_lo_part(t):
                dve.wait_ge(ys_hi_cut, t + 1)
                nc.vector.tensor_tensor(ys_lo[:, t, :], ys[:, t * D:(t + 1) * D], ys_hi[:, t, :],
                                        ALU.subtract).then_inc(ys_lo_cut, 1)

            dve.wait_ge(ys_zero, 1)
            dve.wait_ge(steps_ready, 1)
            for n in range(STEPS):
                e = nc.values_load(step_e_int[0:1, n:n + 1], engines=(mybir.EngineType.DVE,),
                                   min_val=max(0, n - T + 1), max_val=min(EXPERTS - 1, n))
                rows = ys[:, bass.ds((n - e) * D, D)]
                dve.wait_ge(e_unit, n + 1)
                wait(dve, e_added, n)
                nc.vector.scalar_tensor_tensor(rows, bank[n % 4][:], step_mask[:, n:n + 1], rows, ALU.mult,
                                               ALU.add).then_inc(e_added, 1)
                if n >= EXPERTS:
                    ys_lo_part(n - EXPERTS)
            ys_lo_part(T - 1)
            for t in range(T):
                dve.wait_ge(moe_out, t + 1)
                nc.vector.tensor_tensor(x_res[:, t, :], bank[4 + t][:], x_res[:, t, :], ALU.add).then_inc(result, 1)

        @block.tensor
        def _(pe):
            def three(out_ap, pairs, start=True, stop=True):
                n = 0
                for (w_hi, w_lo), (m_hi, m_lo) in pairs:
                    for w, m in ((w_hi, m_hi), (w_hi, m_lo), (w_lo, m_hi)):
                        mm = nc.tensor.matmul(out_ap, w, m, start=start and n == 0,
                                              stop=stop and n == 3 * len(pairs) - 1, skip_group_check=True)
                        n += 1
                return mm

            def turn_x(stage, tiles=range(T)):
                for t in tiles:
                    pe.wait_ge(xn_ready, T * (stage - 1) + t + 1)
                    for c in range(C):
                        mm = nc.tensor.transpose(bank[TURN_BANKS[stage][t]][:, c * P:(c + 1) * P],
                                                 xn[:, t, c * P:(c + 1) * P],
                                                 ident[:])
                    mm.then_inc(xT_turned, 1)

            def norm_turn(n, par, unit):
                pe.wait_ge(n_unit, n + 1)
                wait(pe, n_lo, n - 1)
                for h in range(REP):
                    mm = nc.tensor.transpose(bank[2 + par][:, h * HD:(h + 1) * HD],
                                             unit[:, par, h * HD:(h + 1) * HD], ident[:])
                mm.then_inc(n_turned, 1)

            def kv_project(i, where, half, w_hi, w_lo):
                tile = bass.ds(i * P, P)
                return three(bank[where][:], [((cT_hi[:, c, tile], cT_lo[:, c, tile]),
                                             (w_hi[:, half, c * 512:(c + 1) * 512],
                                              w_lo[:, half, c * 512:(c + 1) * 512])) for c in range(C)])

            def k_step(half, i, par):
                n = 8 * half + i
                wait(pe, n_unit, n - 1)
                if isinstance(n, int) and n == 0:
                    for c in range(C):
                        pe.wait_ge(cut_lo, 2 * (c + 1))
                        mm = three(bank[0][:], [((cT_hi[:, c, 0:P], cT_lo[:, c, 0:P]),
                                                 (wk_hi[:, 0, c * 512:(c + 1) * 512],
                                                  wk_lo[:, 0, c * 512:(c + 1) * 512]))],
                                   start=(c == 0), stop=(c == C - 1))
                    mm.then_inc(n_proj, 1)
                else:
                    kv_project(i, par, half, wk_hi, wk_lo).then_inc(n_proj, 1)
                if not (isinstance(n, int) and n < 2):
                    norm_turn(n - 2, par, k_unit)

            for i in range(4):
                if i == 2:
                    pe.wait_ge(const_in, 48)
                k_step(0, i, i % 2)
            pe.wait_ge(cut_lo, C * 3)
            with pe.Fori(2, 4) as m:
                for u in range(2):
                    k_step(0, 2 * m + u, u)
            pe.wait_ge(cut_lo, C * 4)
            with pe.Fori(0, 4) as m:
                for u in range(2):
                    k_step(1, 2 * m + u, u)
            norm_turn(14, 0, k_unit)

            def v_step(half, i, par):
                n = 8 * half + i
                wait(pe, v_cut_lo, n - 3)
                kv_project(i, V_BANKS[half][par], half, wv_hi, wv_lo).then_inc(v_proj, 1)

            def turn_q1(t):
                pe.wait_ge(q1_ready, t + 1)
                wait(pe, q1T_ready, t - 1)
                for c in range(KT):
                    mm = nc.tensor.transpose(bank[6 + t % 2][:].bitcast(BF16)[:, c * P:(c + 1) * P],
                                             q1[:, t, c * P:(c + 1) * P], ident_b[:])
                mm.then_inc(q1_turned, 1)

            def sum_columns(b):
                pe.wait_ge(q2_ready, b + 1)
                for c in range(KT):
                    mm = nc.tensor.matmul(bank[4 + b][:], ones_b[:], q2[:, b, c, :], start=(c == 0),
                                          stop=(c == KT - 1))
                mm.then_inc(col_sum, 1)

            turn_q1(0)
            turn_q1(1)
            pe.wait_ge(cut_lo, C * (WV + 1))
            v_step(0, 0, 0)
            norm_turn(15, 1, k_unit)
            sum_columns(0)
            sum_columns(1)

            turn_q1(2)
            turn_q1(3)
            v_step(0, 1, 1)
            pe.wait_ge(q1T_ready, T)
            pe.wait_ge(n_lo, 16)
            for t in range(T):
                for c in range(KT):
                    mm = nc.tensor.matmul(bank[CROSS_BANKS[t]][:], q1T[:, c, t * P:(t + 1) * P], q2[:, t // QT, c, :],
                                          start=(c == 0), stop=(c == KT - 1))
                mm.then_inc(cross_done, 1)

            pe.wait_ge(cross_used, 1)
            v_step(0, 2, 2)
            v_step(0, 3, 3)
            for u in range(4):
                v_step(0, 4 + u, u)
            turn_x(1, [0, 1])
            pe.wait_ge(v_cut_lo, 8)
            turn_x(1, [2, 3])
            pe.wait_ge(cross_used, T)
            pe.wait_ge(cut_lo, C * (WV + 2))
            with pe.Fori(0, 2) as m:
                for u in range(4):
                    v_step(1, 4 * m + u, u)

            def ffn_ab(j, par):
                pe.wait_ge(w13_cut_lo, j + 1)
                wait(pe, h_ready, j - 1)
                for mat in range(2):
                    mm = three(bank[2 * par + mat][:],
                               [((w13_hi[par][:, (4 * mat + c) * P:(4 * mat + c + 1) * P],
                                  w13_lo[par][:, (4 * mat + c) * P:(4 * mat + c + 1) * P]),
                                 (xT_hi[:, c, :], xT_lo[:, c, :])) for c in range(C)])
                mm.then_inc(ab_done, 1)

            def ffn_down(j, par, start=False, stop=False):
                pe.wait_ge(h_cut_lo, j + 1)
                pe.wait_ge(w2_cut_lo, j + 1)
                for t in range(T):
                    tok = slice(t * P, (t + 1) * P)
                    mm = three(bank[4 + t][:], [((h_hi[par][:, tok], h_lo[par][:, tok]), (w2_hi[par], w2_lo[par]))],
                               start=start, stop=stop)
                    if stop:
                        mm.then_inc(ffn_out, 1)
                if not stop:
                    mm.then_inc(ffn_tile, 1)

            pe.wait_ge(xT_cut_lo, T)
            pe.wait_ge(v_cut_lo, 14)
            ffn_ab(0, 0)
            pe.wait_ge(v_cut_lo, 16)
            ffn_ab(1, 1)
            ffn_down(0, 0, start=True)
            with pe.Fori(1, HT // 2) as m:
                ffn_ab(2 * m, 0)
                ffn_down(2 * m - 1, 1)
                ffn_ab(2 * m + 1, 1)
                ffn_down(2 * m, 0)
            ffn_ab(HT - 1, 0)
            ffn_down(HT - 2, 1)
            ffn_down(HT - 1, 0, stop=True)

            def token_unit(where, t, w_hi, w_lo, stage=None):
                tok = slice(t * P, (t + 1) * P)
                for c in range(C):
                    if c == C // 2 and stage and t + 1 < T:
                        turn_x(stage, [t + 1])
                    mm = three(where[:], [((xT_hi[:, c, tok], xT_lo[:, c, tok]),
                                           (w_hi[:, c * 512:(c + 1) * 512], w_lo[:, c * 512:(c + 1) * 512]))],
                               start=(c == 0), stop=(c == C - 1))
                return mm

            def q_group(kv, par):
                pe.wait_ge(cut_lo, C * (WQ + kv + 1))
                for t in range(T):
                    n = 16 + 4 * kv + t
                    start = isinstance(kv, int) and kv == 0
                    if start:
                        pe.wait_ge(xT_cut_lo, T + t + 1)
                    wait(pe, n_unit, n - 3)
                    token_unit(bank[Q_BANKS[t]], t, wq_hi[par], wq_lo[par], 2 if start else None).then_inc(n_proj, 1)
                    if not (isinstance(n, int) and n < 18):
                        norm_turn(n - 2, t % 2, xn[:, 0:2, :])

            turn_x(2, [0])
            q_group(0, 0)
            q_group(1, 1)
            with pe.Fori(1, KV // 2) as m:
                q_group(2 * m, 0)
                q_group(2 * m + 1, 1)
            norm_turn(16 + 4 * KV - 2, 0, xn[:, 0:2, :])

            def attend(g, u):
                k = 8 * g + u
                first, last = isinstance(g, int) and g == 0, isinstance(g, int) and g == G
                if not last:
                    wait(pe, masked, k - 3)
                    h, qt = u // 2, u % 2
                    off = g * (REP * S) + h * S + qt * P
                    three(bank[u % 4][:], [((q_hi[:, bass.ds(off, P)], q_lo[:, bass.ds(off, P)]),
                                            (kT_flat[0][:, bass.ds(g * S2, S2)],
                                             kT_flat[1][:, bass.ds(g * S2, S2)]))]).then_inc(scored, 1)
                if not first:
                    pair, c = u // 4, u % 4
                    if c == 0:
                        pe.wait_ge(p_lo, 8 * g - 4 if pair == 0 else 8 * g)
                        wait(pe, o_lo, 2 * g - 3 + pair)
                    off = (g - 1) * S2 + c * P
                    mm = three(bank[6 + pair][:], [((v_flat[0][:, bass.ds(off, P)], v_flat[1][:, bass.ds(off, P)]),
                                                    (pT_hi[pair][:, c, :], pT_lo[pair][:, c, :]))],
                               start=(c == 0), stop=(c == KT - 1))
                    if c == KT - 1:
                        mm.then_inc(pv_done, 1)
                if not (first and u < 3) and not (last and u >= 3):
                    w = (u + 5) % 8
                    pe.wait_ge(p_ready, k - 2)
                    wait(pe, p_lo, k - 4)
                    for c in range(KT):
                        mm = nc.tensor.transpose(bank[4 + w % 2][:, c * P:(c + 1) * P],
                                                 xn[:, w % 4, c * P:(c + 1) * P], ident[:])
                    mm.then_inc(p_turned, 1)

            for u in range(8):
                if u == 2:
                    norm_turn(16 + 4 * KV - 1, 1, xn[:, 0:2, :])
                if u in (2, 3):
                    pe.wait_ge(n_lo, 16 + 4 * KV - 3 + u)
                attend(0, u)
            for u in range(8):
                attend(1, u)
            with pe.Fori(2, G) as g:
                for u in range(8):
                    attend(g, u)
            for u in range(8):
                attend(G, u)

            def o_step(kv, par, start=False, stop=False):
                pe.wait_ge(o_lo, 4 * kv + 4)
                pe.wait_ge(cut_lo, C * (WO + 1 if isinstance(kv, int) and kv == 0 else 2 * kv + 14))
                for t in range(T):
                    pairs = []
                    for h in range(REP):
                        off = kv * (B * REP * S) + (t // QT) * (REP * S) + h * S + (t % QT) * P
                        pairs.append(((q_hi[:, bass.ds(off, P)], q_lo[:, bass.ds(off, P)]),
                                      (wo_hi[par][:, h * D:(h + 1) * D], wo_lo[par][:, h * D:(h + 1) * D])))
                    if stop and t == T - 1:
                        turn_x(3, [0])
                        three(bank[t][:], pairs[:2], start=start, stop=False)
                        turn_x(3, [1])
                        mm = three(bank[t][:], pairs[2:], start=False, stop=True)
                    else:
                        mm = three(bank[t][:], pairs, start=start, stop=stop)
                    if stop:
                        mm.then_inc(o_out, 1)
                if not stop:
                    mm.then_inc(o_group, 1)

            pe.wait_ge(masked, 8 * G)
            o_step(0, 0, start=True)
            o_step(1, 1)
            with pe.Fori(1, KV // 2 - 1) as m:
                o_step(2 * m, 0)
                o_step(2 * m + 1, 1)
            o_step(KV - 2, 0)
            o_step(KV - 1, 1, stop=True)

            for t in range(T):
                if t in (0, 1):
                    turn_x(3, [t + 2])
                pe.wait_ge(xT_cut_lo, 2 * T + t + 1)
                tok = slice(t * P, (t + 1) * P)
                three(bank[0][:, t * EXPERTS:(t + 1) * EXPERTS],
                      [((xT_hi[:, c, tok], xT_lo[:, c, tok]),
                        (gate_hi[:, c * EXPERTS:(c + 1) * EXPERTS], gate_lo[:, c * EXPERTS:(c + 1) * EXPERTS]))
                       for c in range(C)]).then_inc(logits, 1)

            pe.wait_ge(chosen, 1)
            for t in range(T):
                terms = [(ones_b[:], choice_b[:, i, :]) for i in range(t)] + [(before, choice_b[:, t, :])]
                terms += [(ones_b[:], below[:, i, 0:EXPERTS]) for i in range(T)]
                for i, (w, m) in enumerate(terms):
                    nc.tensor.matmul(bank[1][:, t * EXPERTS:(t + 1) * EXPERTS], w, m, start=(i == 0),
                                     stop=(i == len(terms) - 1), skip_group_check=True)
            for t in range(T):
                mm = nc.tensor.matmul(bank[1][:, T * EXPERTS:T * EXPERTS + EXPERTS + 1], ones_b[:], below[:, t, :],
                                      start=(t == 0), stop=(t == T - 1), skip_group_check=True)
            mm.then_inc(counted, 1)
            for t in range(T):
                mm = nc.tensor.transpose(bank[2][0:EXPERTS, t * P:(t + 1) * P], onehot[:, t, :], ident[:])
            mm.then_inc(choice_turned, 1)

            for part, done, where in ((xn_hi, sort_hi, 4), (xn_lo, sort_lo, 0)):
                for c in range(C):
                    if part is xn_lo and c == 0:
                        pe.wait_ge(xn_lo_cut, T)
                        pe.wait_ge(choice_T, 1)
                    for t in range(T):
                        if part is xn_hi and c == 0:
                            pe.wait_ge(xn_hi_cut, t + 1)
                            pe.wait_ge(perm_ready, t + 1)
                        mm = nc.tensor.matmul(bank[where + c][:], part[:, t, c * P:(c + 1) * P], perm[:, t, :],
                                              start=(t == 0), stop=(t == T - 1))
                    mm.then_inc(done, 1)
            for t in range(T):
                pe.wait_ge(xs_hi_ready, t + 1)
                for i in range(T):
                    mm = nc.tensor.transpose(bank[4 + t][:].bitcast(F16)[:, i * P:(i + 1) * P],
                                             perm[:, t, i * P:(i + 1) * P], ident_h)
                mm.then_inc(perm_turned, 1)

            pe.wait_ge(steps_ready, 1)
            pe.wait_ge(cut_lo, C * ITEMS)
            pe.wait_ge(xs_lo_ready, C)
            for n in range(STEPS):
                e = nc.values_load(step_e_int[0:1, n:n + 1], engines=(mybir.EngineType.PE,),
                                   min_val=max(0, n - T + 1), max_val=min(EXPERTS - 1, n))
                wait(pe, e_added, n - 3)
                three(bank[n % 4][:], [((xs_hi[:, c, bass.ds((n - e) * P, P)], xs_lo[:, c, bass.ds((n - e) * P, P)]),
                                        (we_hi[:, bass.ds(e * ITEM + c * 512, 512)],
                                         we_lo[:, bass.ds(e * ITEM + c * 512, 512)])) for c in range(C)]
                      ).then_inc(e_unit, 1)

            pe.wait_ge(permT_ready, T)
            for t in range(T):
                for hl in range(2):
                    nc.tensor.matmul(bank[4 + t][:], oneT[:, t, :], bias_hl[hl], start=(hl == 0), stop=False,
                                     skip_group_check=True)
            for i in range(T):
                pe.wait_ge(ys_lo_cut, i + 1)
                for t in range(T):
                    for part in (ys_hi, ys_lo):
                        last = i == T - 1 and part is ys_lo
                        mm = nc.tensor.matmul(bank[4 + t][:], permT[:, t, i * P:(i + 1) * P], part[:, i, :],
                                              start=False, stop=last, skip_group_check=True)
                    if last:
                        mm.then_inc(moe_out, 1)


def hidden_tiles(a):
    import numpy as np

    pad = np.zeros((HT * P - a.shape[0],) + a.shape[1:], a.dtype)
    return np.concatenate([a, pad]).reshape((HT, P) + a.shape[1:])


def kernel(**inputs):
    import numpy as np
    import concourse.bacc as bacc
    from concourse import mybir as mb
    from concourse.bass_utils import run_bass_kernel_spmd as run

    a = {k: np.asarray(v) for k, v in inputs.items()}
    x, context = a["x"], a["ctx_4096"]

    order = np.arange(D).reshape(2, 2, 2, GROUP).transpose(0, 2, 1, 3).reshape(-1)

    def item(rows):
        return rows.reshape(C, P, 512).transpose(1, 0, 2).reshape(P, ITEM)

    wk, wv = a["L1_xattn_k_proj_w"].T, a["L1_xattn_v_proj_w"].T
    wq, wo = a["L1_xattn_q_proj_w"].T[order], a["L1_xattn_o_proj_w"].T[:, order]
    stream = [item(context[0].T), item(wk[:, 0:512]), item(context[1].T), item(wk[:, 512:1024]),
              item(wv[:, 0:512]), item(wv[:, 512:1024])]
    stream += [item(wq[:, 512 * g:512 * g + 512]) for g in range(KV)]
    w_o = [item(wo[512 * g:512 * g + 512]) for g in range(KV)]
    w_e = [item(a["L1_ffn_expert_w"][j].T[order][:, order]) for j in range(EXPERTS)]
    stream += w_o[0:2]
    for g in range(2, KV):
        stream += [w_e[g - 2], w_o[g]]
    stream += w_e[KV - 2:]

    def words(w):
        w = w.reshape(HIDDEN, 2, 2, GROUP)
        return hidden_tiles(w).transpose(0, 3, 4, 2, 1).reshape(HT, P, 2 * P)

    def scales(s):
        s = s.reshape(HIDDEN, 2, 2, 2)
        s = np.repeat(hidden_tiles(s).transpose(0, 3, 2, 4, 1), GROUP, axis=1)
        return s.reshape(HT, P, 4 * P)

    w2 = a["L0_ffn_w2"]
    w2 = hidden_tiles(np.concatenate([w2, w2], axis=1).reshape(D, HIDDEN).T[:, order])
    w2 = w2.reshape(HT, P, P, 4).transpose(0, 1, 3, 2).reshape(HT, P, D)
    s2 = hidden_tiles(np.repeat(a["L0_ffn_s2"], GROUP).reshape(D, HIDDEN).T[:, order])
    ffn_int = np.concatenate([words(a["L0_ffn_w1"]), words(a["L0_ffn_w3"]), w2], axis=2)
    ffn_scale = np.concatenate([scales(a["L0_ffn_s1"]), scales(a["L0_ffn_s3"]), s2], axis=2)
    part = np.arange(P)
    shift = np.stack([np.where((96 * r + part) % P < GROUP, 24, 28) for r in range(4)]
                     + [np.full(P, 24), np.full(P, 28)], axis=1).astype(np.int32)

    small = np.zeros((P, 56), np.float32)
    for i, name in enumerate(["x1_scale", "x1_zp", "x2_scale", "x2_zp"]):
        small[:, i] = a["L0_xattn_" + name][0]
    small[:, 4] = a["L1_xattn_q_norm_w"]
    small[:, 5] = a["L1_xattn_k_norm_w"]
    small[:, 8:16] = a["L1_ffn_gate_b"]
    small[:, 16:24] = np.arange(EXPERTS)
    small[:, 24:56] = a["L1_ffn_gate_w"].T[order].reshape(C, P, EXPERTS).transpose(1, 0, 2).reshape(P, -1)

    sort = np.zeros((P, SC_COLS), np.float32)
    sort[:, SC_IOTA:SC_IOTA + 512] = np.arange(512)
    sort[:, SC_BEFORE:SC_BEFORE + P] = part[:, None] < part[None, :]
    sort[:, SC_PLACE:SC_PLACE + T] = part[:, None] + P * np.arange(T)
    sort[:, SC_TILE8:SC_TILE8 + T] = EXPERTS * np.arange(T)
    sort[:, SC_N:SC_N + STEPS] = np.arange(STEPS)
    sort[:, SC_N8:SC_N8 + STEPS] = EXPERTS * np.arange(STEPS)

    arrays = {"x": x.reshape(B * S, D)[:, order], "stream": np.stack(stream),
              "nat": np.stack([item(c[order][:, order]) for c in context]), "ffn_int": ffn_int, "ffn_scale": ffn_scale,
              "mask": a["mask_1x1xSxS2_ff0"].reshape(S, S2), "small": small, "shift": shift,
              "ident": np.eye(P, dtype=np.float32), "bias": a["L1_ffn_expert_b"][:, order],
              "sort": sort}
    arrays = {k: np.ascontiguousarray(v) for k, v in arrays.items()}
    nc = bacc.Bacc("TRN2", target_bir_lowering=False, num_devices=1)
    args = [nc.dram_tensor(f"in_{k}", v.shape, mb.dt.from_np(v.dtype), kind="ExternalInput").ap()
            for k, v in arrays.items()]
    out = nc.dram_tensor("out", (B * S, D), mb.dt.float32, kind="ExternalOutput").ap()
    kernel_program(nc, *args, out)
    r = run(nc, [{f"in_{k}": v for k, v in arrays.items()}], core_ids=[0])
    return np.ascontiguousarray(r.results[0]["out"][:, np.argsort(order)]).reshape(B, S, D)
```
